# Optimizing a Trainium2 kernel written in Bass

```python
import numpy as np
import jax
import jax.numpy as jnp

def _softmax(x, axis=-1):
    return jax.nn.softmax(x, axis=axis)

def _gelu(x):
    return jax.nn.gelu(x, approximate=True)

def _silu(x):
    return jax.nn.silu(x)

def _sigmoid(x):
    return jax.nn.sigmoid(x)

def _layernorm(x, axis=-1, eps=1e-05):
    m = jnp.mean(x, axis=axis, keepdims=True)
    v = jnp.var(x, axis=axis, keepdims=True)
    return (x - m) / jnp.sqrt(v + eps)

def _scatter_add(tgt, idx, src, axis=0):
    return tgt.at[idx].add(src)

def _segment_sum(src, seg, n):
    return jax.ops.segment_sum(src, seg, n)
kernel_name = 'mk_lm_tower_d1_tok_ids256_r4_2f75c2'

def setup_inputs(seed: int=0):
    np.random.seed(seed)
    _w = jnp.asarray

    def _rec_inputs():
        import jax
        import jax.numpy as jnp
        _rk = jax.random.key(seed)
        x = jax.random.randint(jax.random.fold_in(_rk, 1), (2, 1024), 0, 64, jnp.int32)
        return x
    x = _rec_inputs()

    def _L0_tok_setup():
        import jax, jax.numpy as jnp
        import numpy as np
        BASE = 257
        HASH_MOD = 1024
        WINDOWS = (2, 4, 8, 16)
        MATCH_OFFSETS = (1, 2, 4, 8)
        CHUNK = 32
        EPS_LN = 1e-05

        def _shift_right(x, k):
            B, T = x.shape
            return jnp.concatenate([jnp.zeros((B, k), x.dtype), x[:, :T - k]], axis=1)

        def _rolling_hashes(chars):
            c = chars.astype(jnp.int32)
            hs = []
            for w in WINDOWS:
                acc = jnp.zeros_like(c)
                p = 1
                for j in range(w):
                    acc = acc + _shift_right(c, j) * p
                    p = p * BASE % HASH_MOD
                hs.append(acc % HASH_MOD)
            return jnp.stack(hs, axis=2)

        def _match_features(chars):
            feats = []
            for k in MATCH_OFFSETS:
                m = (chars == _shift_right(chars, k)).astype(jnp.float32)
                m = m.at[:, :k].set(0.0)
                feats.append(m)
            return jnp.stack(feats, axis=-1)

        def _layer_norm(x, g, b):
            mu = jnp.mean(x, axis=-1, keepdims=True)
            var = jnp.mean((x - mu) ** 2, axis=-1, keepdims=True)
            return (x - mu) * jax.lax.rsqrt(var + EPS_LN) * g + b

        def _forward(chars, emb_byte, hash_tables, Wq, bq, conv_w, conv_b, Win, b_in, Wg, bg, Wi, bi, Wo, bo, ln_g, ln_b, mlp_w, mlp_b, Wout, bout):
            B, T = chars.shape
            byte_emb = emb_byte[chars]
            hidx = _rolling_hashes(chars)
            scale_embeds = jnp.stack([hash_tables[s][hidx[:, :, s]] for s in range(len(WINDOWS))], axis=2)
            E = scale_embeds.shape[-1]
            q = byte_emb @ Wq + bq
            scores = jnp.einsum('bte,btse->bts', q, scale_embeds) / jnp.sqrt(jnp.float32(E))
            w = jax.nn.softmax(scores, axis=-1)
            hash_feat = jnp.einsum('bts,btse->bte', w, scale_embeds)
            C = hash_feat.shape[-1]
            kk = conv_w.shape[-1]
            ht = jnp.moveaxis(hash_feat, 1, 2)
            ht = jnp.pad(ht, ((0, 0), (0, 0), (kk - 1, 0)))
            ht = jax.lax.conv_general_dilated(ht, conv_w, window_strides=(1,), padding='VALID', dimension_numbers=('NCH', 'OIH', 'NCH'), feature_group_count=C)
            hash_feat = jax.nn.silu(jnp.moveaxis(ht + conv_b[None, :, None], 2, 1))
            mf = _match_features(chars)
            feat = jnp.concatenate([byte_emb, hash_feat, mf], axis=-1)
            h = jax.nn.silu(feat @ Win + b_in)
            gates = jax.nn.sigmoid(h @ Wg + bg)
            drive = (1.0 - gates) * (h @ Wi + bi)
            S = gates.shape[-1]
            nC = T // CHUNK
            g = gates.reshape(B, nC, CHUNK, S).transpose(1, 0, 2, 3)
            d = drive.reshape(B, nC, CHUNK, S).transpose(1, 0, 2, 3)

            def step(hc, ab):
                a, b = ab
                log_a = jnp.log(jnp.maximum(a, 1e-06))
                cum_a = jnp.exp(jnp.cumsum(log_a, axis=1))
                inv = 1.0 / jnp.maximum(cum_a, 1e-08)
                cum_wb = jnp.cumsum(b * inv, axis=1)
                out = cum_a * (hc[:, None, :] + cum_wb)
                return (out[:, -1], out)
            _, states = jax.lax.scan(step, jnp.zeros((B, S), h.dtype), (g, d))
            states = states.transpose(1, 0, 2, 3).reshape(B, T, S)
            h = _layer_norm(h + states @ Wo + bo, ln_g, ln_b)
            for l in range(mlp_w.shape[0]):
                h = h + jax.nn.silu(h @ mlp_w[l] + mlp_b[l])
            return h @ Wout + bout
        key = jax.random.key(seed)
        ks = jax.random.split(key, 12)
        B, T, V = (8, 2048, 64)
        EB, E, H, SS, KC, NM, NR = (64, 64, 128, 32, 4, 4, 3)
        feat = EB + E + NM

        def lin(k, i, o):
            return (jax.random.normal(k, (i, o), jnp.float32) / np.sqrt(i)).astype(jnp.float32)
        return {'chars': jax.random.randint(ks[0], (B, T), 0, V), 'emb_byte': jax.random.normal(ks[1], (V, EB), jnp.float32) * 0.02, 'hash_tables': jax.random.normal(ks[2], (len(WINDOWS), HASH_MOD, E), jnp.float32) * 0.02, 'Wq': lin(ks[3], EB, E), 'bq': jnp.zeros((E,), jnp.float32), 'conv_w': jax.random.normal(ks[4], (E, 1, KC), jnp.float32) * 0.2, 'conv_b': jnp.zeros((E,), jnp.float32), 'Win': lin(ks[5], feat, H), 'b_in': jnp.zeros((H,), jnp.float32), 'Wg': lin(ks[6], H, SS), 'bg': jnp.zeros((SS,), jnp.float32), 'Wi': lin(ks[7], H, SS), 'bi': jnp.zeros((SS,), jnp.float32), 'Wo': lin(ks[8], SS, H), 'bo': jnp.zeros((H,), jnp.float32), 'ln_g': jnp.ones((H,), jnp.float32), 'ln_b': jnp.zeros((H,), jnp.float32), 'mlp_w': jax.random.normal(ks[9], (NR, H, H), jnp.float32) / np.sqrt(H), 'mlp_b': jnp.zeros((NR, H), jnp.float32), 'Wout': lin(ks[10], H, V), 'bout': jnp.zeros((V,), jnp.float32)}
    _L0_tok_all = _L0_tok_setup()
    _L0_tok_in = {k: v for k, v in _L0_tok_all.items() if k in ('emb_byte', 'hash_tables', 'Wq', 'bq', 'conv_w', 'conv_b', 'Win', 'b_in', 'Wg', 'bg', 'Wi', 'bi', 'Wo', 'bo', 'ln_g', 'ln_b', 'mlp_w', 'mlp_b', 'Wout', 'bout')}
    del _L0_tok_all

    def _L0_attn_setup():
        import math
        import jax, jax.numpy as jnp
        import numpy as np
        D_MODEL = 64
        N_HEADS = 4
        HEAD_DIM = D_MODEL // N_HEADS
        MAX_REL = 30

        def _rel_pos_encodings(t, d_model):
            n = 2 * MAX_REL + 1
            positions = jnp.arange(n, dtype=jnp.float32)[:, None]
            div_term = jnp.exp(jnp.arange(0, d_model, 2, dtype=jnp.float32) * (-math.log(10000.0) / d_model))
            ang = positions * div_term
            enc = jnp.stack([jnp.sin(ang), jnp.cos(ang)], axis=-1).reshape(n, d_model)
            rng = jnp.arange(t)
            final_mat = jnp.clip(rng[None, :] - rng[:, None], -MAX_REL, MAX_REL) + MAX_REL
            return enc[final_mat]
        key = jax.random.key(seed)
        ks = jax.random.split(key, 12)
        d = D_MODEL
        s = 1.0 / math.sqrt(d)
        inp = {'inputs': jax.random.normal(ks[0], (16, 128, d), dtype=jnp.float32), 'ln_gamma': jnp.ones((d,), jnp.float32), 'ln_beta': jnp.zeros((d,), jnp.float32), 'Wq': jax.random.normal(ks[1], (d, d), jnp.float32) * s, 'bq': jnp.zeros((d,), jnp.float32), 'Wk': jax.random.normal(ks[2], (d, d), jnp.float32) * s, 'bk': jnp.zeros((d,), jnp.float32), 'Wv': jax.random.normal(ks[3], (d, d), jnp.float32) * s, 'bv': jnp.zeros((d,), jnp.float32), 'Wpos': jax.random.normal(ks[4], (d, d), jnp.float32) * s, 'bpos': jnp.zeros((d,), jnp.float32), 'Wo': jax.random.normal(ks[5], (d, d), jnp.float32) * s, 'bo': jnp.zeros((d,), jnp.float32), 'u_bias': jax.random.normal(ks[6], (1, N_HEADS, 1, HEAD_DIM), jnp.float32) * 0.02, 'v_bias': jax.random.normal(ks[7], (1, N_HEADS, 1, HEAD_DIM), jnp.float32) * 0.02}
        return inp
    _L0_attn_all = _L0_attn_setup()
    _L0_attn_in = {k: v for k, v in _L0_attn_all.items() if k in ('ln_gamma', 'ln_beta', 'Wq', 'bq', 'Wk', 'bk', 'Wv', 'bv', 'Wpos', 'bpos', 'Wo', 'bo', 'u_bias', 'v_bias')}
    del _L0_attn_all

    def _L0_ffn_setup():
        import jax, jax.numpy as jnp
        import numpy as np
        BN_EPS = 0.001

        def _bn(h, g, b, m, v):
            return g * (h - m) * jax.lax.rsqrt(v + BN_EPS) + b
        key = jax.random.key(seed)
        ks = jax.random.split(key, 8)
        B, F, Df = (64, 64, 64)
        E, H, D = (8, 64, 64)
        s1 = 1.0 / np.sqrt(Df)
        s2 = 1.0 / np.sqrt(H)
        return {'x': jax.random.normal(ks[0], (B, F, Df), jnp.float32), 'Wr': jax.random.normal(ks[1], (Df, E), jnp.float32) * s1, 'br': jnp.zeros((E,), jnp.float32), 'W1': jax.random.normal(ks[2], (E, Df, H), jnp.float32) * s1, 'b1': jnp.zeros((E, H), jnp.float32), 'g1': jnp.ones((E, H), jnp.float32), 'be1': jnp.zeros((E, H), jnp.float32), 'm1': jnp.zeros((E, H), jnp.float32), 'v1': jnp.ones((E, H), jnp.float32), 'W2': jax.random.normal(ks[3], (E, H, H), jnp.float32) * s2, 'b2': jnp.zeros((E, H), jnp.float32), 'g2': jnp.ones((E, H), jnp.float32), 'be2': jnp.zeros((E, H), jnp.float32), 'm2': jnp.zeros((E, H), jnp.float32), 'v2': jnp.ones((E, H), jnp.float32), 'Wo': jax.random.normal(ks[4], (E, H, D), jnp.float32) * s2, 'bo': jnp.zeros((E, D), jnp.float32)}
    _L0_ffn_all = _L0_ffn_setup()
    _L0_ffn_in = {k: v for k, v in _L0_ffn_all.items() if k in ('Wr', 'br', 'W1', 'b1', 'g1', 'be1', 'm1', 'v1', 'W2', 'b2', 'g2', 'be2', 'm2', 'v2', 'Wo', 'bo')}
    del _L0_ffn_all
    return {'x': x, 'L0_tok_emb_byte': _L0_tok_in['emb_byte'], 'L0_tok_hash_tables': _L0_tok_in['hash_tables'], 'L0_tok_Wq': _L0_tok_in['Wq'], 'L0_tok_bq': _L0_tok_in['bq'], 'L0_tok_conv_w': _L0_tok_in['conv_w'], 'L0_tok_conv_b': _L0_tok_in['conv_b'], 'L0_tok_Win': _L0_tok_in['Win'], 'L0_tok_b_in': _L0_tok_in['b_in'], 'L0_tok_Wg': _L0_tok_in['Wg'], 'L0_tok_bg': _L0_tok_in['bg'], 'L0_tok_Wi': _L0_tok_in['Wi'], 'L0_tok_bi': _L0_tok_in['bi'], 'L0_tok_Wo': _L0_tok_in['Wo'], 'L0_tok_bo': _L0_tok_in['bo'], 'L0_tok_ln_g': _L0_tok_in['ln_g'], 'L0_tok_ln_b': _L0_tok_in['ln_b'], 'L0_tok_mlp_w': _L0_tok_in['mlp_w'], 'L0_tok_mlp_b': _L0_tok_in['mlp_b'], 'L0_tok_Wout': _L0_tok_in['Wout'], 'L0_tok_bout': _L0_tok_in['bout'], 'L0_attn_ln_gamma': _L0_attn_in['ln_gamma'], 'L0_attn_ln_beta': _L0_attn_in['ln_beta'], 'L0_attn_Wq': _L0_attn_in['Wq'], 'L0_attn_bq': _L0_attn_in['bq'], 'L0_attn_Wk': _L0_attn_in['Wk'], 'L0_attn_bk': _L0_attn_in['bk'], 'L0_attn_Wv': _L0_attn_in['Wv'], 'L0_attn_bv': _L0_attn_in['bv'], 'L0_attn_Wpos': _L0_attn_in['Wpos'], 'L0_attn_bpos': _L0_attn_in['bpos'], 'L0_attn_Wo': _L0_attn_in['Wo'], 'L0_attn_bo': _L0_attn_in['bo'], 'L0_attn_u_bias': _L0_attn_in['u_bias'], 'L0_attn_v_bias': _L0_attn_in['v_bias'], 'L0_ffn_Wr': _L0_ffn_in['Wr'], 'L0_ffn_br': _L0_ffn_in['br'], 'L0_ffn_W1': _L0_ffn_in['W1'], 'L0_ffn_b1': _L0_ffn_in['b1'], 'L0_ffn_g1': _L0_ffn_in['g1'], 'L0_ffn_be1': _L0_ffn_in['be1'], 'L0_ffn_m1': _L0_ffn_in['m1'], 'L0_ffn_v1': _L0_ffn_in['v1'], 'L0_ffn_W2': _L0_ffn_in['W2'], 'L0_ffn_b2': _L0_ffn_in['b2'], 'L0_ffn_g2': _L0_ffn_in['g2'], 'L0_ffn_be2': _L0_ffn_in['be2'], 'L0_ffn_m2': _L0_ffn_in['m2'], 'L0_ffn_v2': _L0_ffn_in['v2'], 'L0_ffn_Wo': _L0_ffn_in['Wo'], 'L0_ffn_bo': _L0_ffn_in['bo']}

def reference(x, L0_tok_emb_byte, L0_tok_hash_tables, L0_tok_Wq, L0_tok_bq, L0_tok_conv_w, L0_tok_conv_b, L0_tok_Win, L0_tok_b_in, L0_tok_Wg, L0_tok_bg, L0_tok_Wi, L0_tok_bi, L0_tok_Wo, L0_tok_bo, L0_tok_ln_g, L0_tok_ln_b, L0_tok_mlp_w, L0_tok_mlp_b, L0_tok_Wout, L0_tok_bout, L0_attn_ln_gamma, L0_attn_ln_beta, L0_attn_Wq, L0_attn_bq, L0_attn_Wk, L0_attn_bk, L0_attn_Wv, L0_attn_bv, L0_attn_Wpos, L0_attn_bpos, L0_attn_Wo, L0_attn_bo, L0_attn_u_bias, L0_attn_v_bias, L0_ffn_Wr, L0_ffn_br, L0_ffn_W1, L0_ffn_b1, L0_ffn_g1, L0_ffn_be1, L0_ffn_m1, L0_ffn_v1, L0_ffn_W2, L0_ffn_b2, L0_ffn_g2, L0_ffn_be2, L0_ffn_m2, L0_ffn_v2, L0_ffn_Wo, L0_ffn_bo):
    import jax
    import jax.numpy as jnp

    def _L0_tok_ref(chars, emb_byte, hash_tables, Wq, bq, conv_w, conv_b, Win, b_in, Wg, bg, Wi, bi, Wo, bo, ln_g, ln_b, mlp_w, mlp_b, Wout, bout):
        import jax, jax.numpy as jnp
        import numpy as np
        BASE = 257
        HASH_MOD = 1024
        WINDOWS = (2, 4, 8, 16)
        MATCH_OFFSETS = (1, 2, 4, 8)
        CHUNK = 32
        EPS_LN = 1e-05

        def _shift_right(x, k):
            B, T = x.shape
            return jnp.concatenate([jnp.zeros((B, k), x.dtype), x[:, :T - k]], axis=1)

        def _rolling_hashes(chars):
            c = chars.astype(jnp.int32)
            hs = []
            for w in WINDOWS:
                acc = jnp.zeros_like(c)
                p = 1
                for j in range(w):
                    acc = acc + _shift_right(c, j) * p
                    p = p * BASE % HASH_MOD
                hs.append(acc % HASH_MOD)
            return jnp.stack(hs, axis=2)

        def _match_features(chars):
            feats = []
            for k in MATCH_OFFSETS:
                m = (chars == _shift_right(chars, k)).astype(jnp.float32)
                m = m.at[:, :k].set(0.0)
                feats.append(m)
            return jnp.stack(feats, axis=-1)

        def _layer_norm(x, g, b):
            mu = jnp.mean(x, axis=-1, keepdims=True)
            var = jnp.mean((x - mu) ** 2, axis=-1, keepdims=True)
            return (x - mu) * jax.lax.rsqrt(var + EPS_LN) * g + b

        def _forward(chars, emb_byte, hash_tables, Wq, bq, conv_w, conv_b, Win, b_in, Wg, bg, Wi, bi, Wo, bo, ln_g, ln_b, mlp_w, mlp_b, Wout, bout):
            B, T = chars.shape
            byte_emb = emb_byte[chars]
            hidx = _rolling_hashes(chars)
            scale_embeds = jnp.stack([hash_tables[s][hidx[:, :, s]] for s in range(len(WINDOWS))], axis=2)
            E = scale_embeds.shape[-1]
            q = byte_emb @ Wq + bq
            scores = jnp.einsum('bte,btse->bts', q, scale_embeds) / jnp.sqrt(jnp.float32(E))
            w = jax.nn.softmax(scores, axis=-1)
            hash_feat = jnp.einsum('bts,btse->bte', w, scale_embeds)
            C = hash_feat.shape[-1]
            kk = conv_w.shape[-1]
            ht = jnp.moveaxis(hash_feat, 1, 2)
            ht = jnp.pad(ht, ((0, 0), (0, 0), (kk - 1, 0)))
            ht = jax.lax.conv_general_dilated(ht, conv_w, window_strides=(1,), padding='VALID', dimension_numbers=('NCH', 'OIH', 'NCH'), feature_group_count=C)
            hash_feat = jax.nn.silu(jnp.moveaxis(ht + conv_b[None, :, None], 2, 1))
            mf = _match_features(chars)
            feat = jnp.concatenate([byte_emb, hash_feat, mf], axis=-1)
            h = jax.nn.silu(feat @ Win + b_in)
            gates = jax.nn.sigmoid(h @ Wg + bg)
            drive = (1.0 - gates) * (h @ Wi + bi)
            S = gates.shape[-1]
            nC = T // CHUNK
            g = gates.reshape(B, nC, CHUNK, S).transpose(1, 0, 2, 3)
            d = drive.reshape(B, nC, CHUNK, S).transpose(1, 0, 2, 3)

            def step(hc, ab):
                a, b = ab
                log_a = jnp.log(jnp.maximum(a, 1e-06))
                cum_a = jnp.exp(jnp.cumsum(log_a, axis=1))
                inv = 1.0 / jnp.maximum(cum_a, 1e-08)
                cum_wb = jnp.cumsum(b * inv, axis=1)
                out = cum_a * (hc[:, None, :] + cum_wb)
                return (out[:, -1], out)
            _, states = jax.lax.scan(step, jnp.zeros((B, S), h.dtype), (g, d))
            states = states.transpose(1, 0, 2, 3).reshape(B, T, S)
            h = _layer_norm(h + states @ Wo + bo, ln_g, ln_b)
            for l in range(mlp_w.shape[0]):
                h = h + jax.nn.silu(h @ mlp_w[l] + mlp_b[l])
            return h @ Wout + bout
        return _forward(chars, emb_byte, hash_tables, Wq, bq, conv_w, conv_b, Win, b_in, Wg, bg, Wi, bi, Wo, bo, ln_g, ln_b, mlp_w, mlp_b, Wout, bout)

    def _L0_attn_ref(inputs, ln_gamma, ln_beta, Wq, bq, Wk, bk, Wv, bv, Wpos, bpos, Wo, bo, u_bias, v_bias):
        import math
        import jax, jax.numpy as jnp
        import numpy as np
        D_MODEL = 64
        N_HEADS = 4
        HEAD_DIM = D_MODEL // N_HEADS
        MAX_REL = 30

        def _rel_pos_encodings(t, d_model):
            n = 2 * MAX_REL + 1
            positions = jnp.arange(n, dtype=jnp.float32)[:, None]
            div_term = jnp.exp(jnp.arange(0, d_model, 2, dtype=jnp.float32) * (-math.log(10000.0) / d_model))
            ang = positions * div_term
            enc = jnp.stack([jnp.sin(ang), jnp.cos(ang)], axis=-1).reshape(n, d_model)
            rng = jnp.arange(t)
            final_mat = jnp.clip(rng[None, :] - rng[:, None], -MAX_REL, MAX_REL) + MAX_REL
            return enc[final_mat]
        b, t, d = inputs.shape
        h, hd = (N_HEADS, HEAD_DIM)
        mu = jnp.mean(inputs, axis=-1, keepdims=True)
        var = jnp.mean(jnp.square(inputs - mu), axis=-1, keepdims=True)
        x = (inputs - mu) * jax.lax.rsqrt(var + 1e-05) * ln_gamma + ln_beta

        def split_heads(y):
            return y.reshape(b, t, h, hd).transpose(0, 2, 1, 3)
        q = split_heads(x @ Wq.T + bq)
        k = split_heads(x @ Wk.T + bk)
        v = split_heads(x @ Wv.T + bv)
        rel = jax.lax.stop_gradient(_rel_pos_encodings(t, d))
        pos = (rel @ Wpos.T + bpos).reshape(t, t, h, hd)
        qk_score = jnp.einsum('bhtd,bhsd->bhts', q + u_bias, k)
        pos_score = jnp.einsum('bhtd,tshd->bhts', q + v_bias, pos)
        scores = (qk_score + pos_score) / math.sqrt(hd)
        attn = jax.nn.softmax(scores, axis=-1)
        ctx = jnp.einsum('bhts,bhsd->bhtd', attn, v)
        ctx = ctx.transpose(0, 2, 1, 3).reshape(b, t, d)
        return ctx @ Wo.T + bo

    def _L0_ffn_ref(x, Wr, br, W1, b1, g1, be1, m1, v1, W2, b2, g2, be2, m2, v2, Wo, bo):
        import jax, jax.numpy as jnp
        import numpy as np
        BN_EPS = 0.001

        def _bn(h, g, b, m, v):
            return g * (h - m) * jax.lax.rsqrt(v + BN_EPS) + b
        feat = jnp.mean(x, axis=0)
        w = jax.nn.softmax(feat @ Wr + br, axis=-1)
        h = jnp.einsum('bfd,edh->bfeh', x, W1) + b1
        h = jax.nn.relu(_bn(h, g1, be1, m1, v1))
        h = jnp.einsum('bfeh,ehk->bfek', h, W2) + b2
        h = jax.nn.relu(_bn(h, g2, be2, m2, v2))
        y = jnp.einsum('bfeh,ehd->bfed', h, Wo) + bo
        return jnp.einsum('bfed,fe->bfd', y, w)
    h = _L0_tok_ref(x, L0_tok_emb_byte, L0_tok_hash_tables, L0_tok_Wq, L0_tok_bq, L0_tok_conv_w, L0_tok_conv_b, L0_tok_Win, L0_tok_b_in, L0_tok_Wg, L0_tok_bg, L0_tok_Wi, L0_tok_bi, L0_tok_Wo, L0_tok_bo, L0_tok_ln_g, L0_tok_ln_b, L0_tok_mlp_w, L0_tok_mlp_b, L0_tok_Wout, L0_tok_bout)
    h = h + _L0_attn_ref(_layernorm(h, axis=-1), L0_attn_ln_gamma, L0_attn_ln_beta, L0_attn_Wq, L0_attn_bq, L0_attn_Wk, L0_attn_bk, L0_attn_Wv, L0_attn_bv, L0_attn_Wpos, L0_attn_bpos, L0_attn_Wo, L0_attn_bo, L0_attn_u_bias, L0_attn_v_bias)
    h = h + _L0_ffn_ref(_layernorm(h, axis=-1), L0_ffn_Wr, L0_ffn_br, L0_ffn_W1, L0_ffn_b1, L0_ffn_g1, L0_ffn_be1, L0_ffn_m1, L0_ffn_v1, L0_ffn_W2, L0_ffn_b2, L0_ffn_g2, L0_ffn_be2, L0_ffn_m2, L0_ffn_v2, L0_ffn_Wo, L0_ffn_bo)
    return h

_drawn_inputs = setup_inputs


def setup_inputs(seed=0):
    import zlib

    import numpy as np

    out = dict(_drawn_inputs(seed))
    spreads = {'L0_tok_bq': (0.0, 0.8),
     'L0_tok_conv_b': (0.0, 0.1),
     'L0_tok_b_in': (0.0, 0.1),
     'L0_tok_bg': (0.0, 0.1),
     'L0_tok_bi': (0.0, 0.1),
     'L0_tok_bo': (0.0, 0.1),
     'L0_tok_ln_g': (1.0, 0.2),
     'L0_tok_ln_b': (0.0, 0.1),
     'L0_tok_mlp_b': (0.0, 0.1),
     'L0_tok_bout': (0.0, 0.1),
     'L0_attn_ln_gamma': (1.0, 0.2),
     'L0_attn_ln_beta': (0.0, 0.1),
     'L0_attn_bq': (0.0, 0.8),
     'L0_attn_bk': (0.0, 2.0),
     'L0_attn_bv': (0.0, 0.1),
     'L0_attn_bpos': (0.0, 2.0),
     'L0_attn_bo': (0.0, 0.1),
     'L0_ffn_br': (0.0, 0.8),
     'L0_ffn_b1': (0.0, 0.731),
     'L0_ffn_g1': (1.0, 0.6),
     'L0_ffn_be1': (0.0, 0.755),
     'L0_ffn_m1': (0.0, 0.696),
     'L0_ffn_v1': (1.0, 0.6),
     'L0_ffn_b2': (0.0, 0.563),
     'L0_ffn_g2': (1.0, 0.6),
     'L0_ffn_be2': (0.0, 0.72),
     'L0_ffn_m2': (0.0, 0.48),
     'L0_ffn_v2': (1.0, 0.6),
     'L0_ffn_bo': (0.0, 0.382)}
    factors = {'L0_tok_hash_tables': 8.0,
     'L0_tok_Wq': 58.467,
     'L0_tok_conv_w': 8.0,
     'L0_attn_Wq': 3.13,
     'L0_attn_Wk': 2.988,
     'L0_attn_Wpos': 8.0,
     'L0_attn_u_bias': 62.754,
     'L0_attn_v_bias': 27.097}
    for name, (base, spread) in spreads.items():
        noise = np.random.default_rng([zlib.crc32(name.encode()), seed]).standard_normal(out[name].shape)
        drawn = base * np.exp(spread * noise) if base else spread * noise
        out[name] = jnp.asarray(drawn.astype(out[name].dtype))
    for name, factor in factors.items():
        out[name] = (out[name] * factor).astype(out[name].dtype)
    return out
```

```python
from contextlib import ExitStack

import numpy as np

import concourse.bass as bass
from concourse import mybir

F32 = mybir.dt.float32
BF16 = mybir.dt.bfloat16
I32 = mybir.dt.int32
U32 = mybir.dt.uint32
ALU = mybir.AluOpType
ACT = mybir.ActivationFunctionType
AX = mybir.AxisListType

P = 128
B, T = 2, 1024
NT = T // P
NC = 2
CT = T // NC
TC = CT // P
V = 64
E = 64
H = 128
SS = 32
NW = 4
WINDOWS = (2, 4, 8, 16)
OFFSETS = (1, 2, 4, 8)
BASE, MOD = 257, 1024
KC = 4
SCH = 32
NQ = 4
QT = T // NQ
QG = QT // SCH
NL = 3
NH, HD = 4, 16
REL = 30
NR = 2 * REL + 1
HALF = 64
LPAD = HALF + 1
PW = 192
WIN = 192
EDGE = 32
NP6 = 96
NE, NPAIR = 8, 4
EPS_LN, EPS_BN = 1e-5, 1e-3
RING = 16
QKG = ((0, 0), (0, 1), (1, 0), (0, 2), (2, 0), (1, 1))


def constants():
    power = [1]
    for _ in range(max(WINDOWS) - 1):
        power.append(power[-1] * BASE % MOD)
    band = np.zeros((P, 2, NW, P), np.float32)
    for k, w in enumerate(WINDOWS):
        for j in range(w):
            for t in range(P):
                src = t - j
                band[src % P, 0 if src >= 0 else 1, k, t] = power[j]
    n = np.arange(NR, dtype=np.float32)[:, None]
    div = np.exp(np.arange(0, E, 2, dtype=np.float32) * np.float32(-np.log(10000.0) / E)).astype(np.float32)
    ang = n * div
    enc = np.stack([np.sin(ang), np.cos(ang)], axis=-1).reshape(NR, E).astype(np.float32)
    heads = (np.arange(E)[:, None] // HD == np.arange(NH)[None, :]).astype(np.float32)
    start = (np.arange(QT) % SCH == 0).astype(np.float32)
    pair = (np.arange(NE)[:, None, None] == 2 * np.arange(NPAIR)[None, :, None] + np.arange(P)[None, None, :] // E)
    return {
        "band": band.reshape(P, -1),
        "ident": np.eye(P, dtype=np.float32),
        "encT": np.ascontiguousarray(enc.T),
        "heads": heads,
        "start": np.broadcast_to(start, (P, QT)).copy(),
        "pair": pair.astype(np.float32).reshape(NE, NPAIR * P),
        "iota": np.arange(P, dtype=np.float32)[:, None],
    }


PACK128 = (("mlp", NL * H), ("wg", SS), ("wi", SS), ("wout", E), ("wo4", H), ("fwo", NPAIR * E), ("start", QT))
PACK64 = (("winh", H), ("aqk", 2 * E), ("av", E), ("wpos", E), ("encT", NR), ("ao", E), ("wr", NE), ("w1", NE * E),
          ("heads", NH), ("convw", KC))
COLS = (("b_in", 1), ("ln_g", 1), ("ln_b", 1), ("mlp_b", NL), ("bg", 1), ("bi", 1), ("conv_b", 1), ("gamma", 1),
        ("beta", 1), ("bqk", 1), ("u", 1), ("v", 1), ("bpos", 1), ("bo", 1), ("f1", 5 * NPAIR), ("f2", 5 * NPAIR))
ROWS = (("bq", E), ("bout", E), ("bv", E), ("ao_b", E), ("br", NE))


def spans(pack):
    at, out = 0, {}
    for name, n in pack:
        out[name] = (at, at + n)
        at += n
    return out, at


S128, N128 = spans(PACK128)
S64, N64 = spans(PACK64)
SCOL, NCOL = spans(COLS)
SROW, NROW = spans(ROWS)


def tower(nc, a):
    with ExitStack() as ctx:
        def sb(name, shape, dt=F32):
            return ctx.enter_context(nc.sbuf_tensor(name, shape, dt))

        made = {}

        def sem(name):
            if name not in made:
                made[name] = ctx.enter_context(nc.semaphore(name))
            return made[name]

        ps = ctx.enter_context(nc.psum_tensor("ps", [P, 8, 512], F32))
        bank = [ps[:, i, :] for i in range(8)]

        w128, w64, cols, rows = sb("w128", [P, N128]), sb("w64", [E, N64]), sb("cols", [P, NCOL]), sb("rows", [P, NROW])
        ident, band = sb("ident", [P, P]), sb("band", [P, 2, NW, P])
        emb3 = sb("emb3", [E, V + H + E])
        iota, pair = sb("iota", [P, 1]), sb("pair", [NE, NPAIR, P])
        xi, xf = sb("xi", [B * NT, P], I32), sb("xf", [B * NT, P])
        xcol = sb("xcol", [P, B, NT + 1])
        hi32 = sb("hi32", [P, NW, B * NT], I32)
        idx = sb("idx", [P, NW, B * NT], I32)
        prob = sb("prob", [P, RING, CT])
        probf = prob[:].rearrange("p r t -> p (r t)")
        emb = probf[:, 0:B * NT * NW * E].rearrange("p (n k e) -> p n k e", k=NW, e=E)
        onehot = probf[0:V + NW, B * NT * NW * E:B * NT * NW * E + B * T]
        gtab = sb("gtab", [V + NW, H])
        qtab = sb("qtab", [V, E])
        cdiag = sb("cdiag", [E, KC, E])
        posb = sb("posb", [E, NH, NR])
        prod = sb("prod", [P, TC, NW, E])
        sc, sm = sb("sc", [P, TC, NW]), sb("sm", [P, TC])
        hf = sb("hf", [P, TC, E])
        hfT = sb("hfT", [E, B, KC - 1 + T])
        cf = sb("cf", [E, CT])
        hT = sb("hT", [H, B * T])
        scan = sb("scan", [P, 6, QT])
        th, ga, gd, d0, d1, cum = (scan[:, i, :] for i in range(6))
        nstart = sb("nstart", [P, QT])
        cw, aw = sb("cw", [P, QT]), sb("aw", [P, QT])
        ends = sb("ends", [P, 2, QG])
        endsf = sb("endsf", [SS, NQ, 2, QG])
        carry = sb("carry", [SS, 1 + NQ * QG])
        carryq = sb("carryq", [P, QG])
        bnc, bns = sb("bnc", [P, TC, 6]), sb("bns", [P, TC, 2])
        rs, rt, rv = sb("rs", [P, 32]), sb("rt", [P, 32]), sb("rv", [P, 32])
        xn = sb("xn", [P, TC, H])
        act_s = sb("act_s", [H, NC, CT])
        qsc, qbi, vbi, bgh = sb("qsc", [P, 1]), sb("qbi", [P, 1]), sb("vbi", [E, 1]), sb("bgh", [P, 1])
        htok = sb("htok", [P, B * NT, E])
        prodf = prod[:].rearrange("p n k e -> p (n k e)")
        la, lb = (prodf[:, i * NT * E:(i + 1) * NT * E].rearrange("p (n e) -> p n e", e=E) for i in range(2))
        lc = sb("lc", [P, NT])
        lnTf = sb("lnTf", [P, B * T])
        states, lnT = lnTf[:, 0:T], lnTf[0:E, :]
        qk32 = act_s[:].rearrange("p c t -> p (c t)")
        hfTf = hfT[:].rearrange("p b t -> p (b t)")
        qv, wT = hfTf[:, 0:T], hfTf[0:NE, T:2 * T]
        fin = hT[:, 0:B * NT * E].rearrange("p (n e) -> p n e", e=E)
        ctxs, ctxT = hT[:, B * NT * E:B * NT * E + CT], hT[0:E, B * NT * E + CT:B * NT * E + 2 * CT]
        part = [sb(f"part{i}", [P, T], BF16) for i in range(3)]
        qst, kst = sb("qst", [P, B, NH, T], BF16), sb("kst", [P, B, NH, T], BF16)
        vt = sb("vt", [P, B, NT, NH, 32])
        pad = scan[:].rearrange("p i t -> p (i t)").rearrange("p (s h c) -> p s h c", s=2, h=NH)
        bias = sb("bias", [P, B, NT, NH, WIN])
        pend = sb("pend", [P, B, NT, NH, 2])
        mx = sb("mx", [P, B, NT, NH, 3])
        junk = sb("junk", [P, 2, WIN], BF16)
        tv = sb("tv", [P, 3, TC, NH])
        tr = sb("tr", [P, 3, TC, NH])
        tp = sb("tp", [P, 3, 3, TC, NH], BF16)
        identb = sb("identb", [P, P], BF16)
        den = sb("den", [P, TC, NH])
        ctxn = sb("ctxn", [P, TC, E])
        w2bd = sb("w2bd", [P, NPAIR, P])
        fsc, fbi = sb("fsc", [P, 2, NPAIR]), sb("fbi", [P, 2, NPAIR])
        bo8 = sb("bo8", [NE, E])
        rw, rwm = sb("rw", [P, NT, NE]), sb("rwm", [P, NT])
        f1, f2, f3 = prob[:, 0:2], prob[:, 2:4], prob[:, 4:4 + NPAIR]
        spare = bias[:, 1].rearrange("p n h w -> p (n h w)").bitcast(I32)
        xrep, xsh = spare[0:V + NW, 0:B * T], spare[0:V + NW, B * T:2 * B * T]

        def c128(name):
            return w128[:, S128[name][0]:S128[name][1]]

        def c64(name):
            return w64[:, S64[name][0]:S64[name][1]]

        def col(name, i=0, n=P):
            return cols[0:n, SCOL[name][0] + i:SCOL[name][0] + i + 1]

        def row(name, *mid):
            r = rows[:, SROW[name][0]:SROW[name][1]]
            for k in mid:
                r = r.rearrange("p (o n) -> p o n", o=1).to_broadcast([P, k, r.shape[-1]])
            return r

        skew = a["skew"]
        block = ctx.enter_context(nc.Block())

        @block.sync
        def _(sp):
            def load(name, dst, src):
                sp.dma_start(dst, src).then_inc(sem(name), 16)

            load("ld_x", xi[:], a["x"].rearrange("b (n p) -> (b n) p", p=P))
            load("ld_ident", ident[:], a["ident"])
            load("ld_band", band[:].rearrange("p a k t -> p (a k t)"), a["band"])
            flat = a["x"].rearrange("b t -> (b t)").rearrange("(o n) -> o n", o=1)
            load("ld_oh", xrep, flat.to_broadcast([V + NW, B * T]))
            load("ld_oh", iota[:], a["iota"])
            sp.wait_ge(sem("xsh_set"), 1)
            for k, o in enumerate(OFFSETS):
                for b in range(B):
                    load("ld_sh", xsh[V + k:V + k + 1, b * T + o:(b + 1) * T], flat[:, b * T:(b + 1) * T - o])
            load("ld_emb", emb3[:], a["emb3"])
            load("ld_emb", gtab[V:V + NW, :], a["winm"])
            load("ld_w", w64[:], a["w64"])
            load("ld_w", cols[:], a["cols"])
            load("ld_w", rows[:], a["rows"].to_broadcast([P, NROW]))
            load("ld_w", w128[:], a["w128"])
            load("ld_f", pair[:].rearrange("e a p -> e (a p)"), a["pair"])
            load("ld_f", bo8[:], a["bo8"])
            sp.wait_ge(sem("w2_zero"), 1)
            for e in range(2):
                load("ld_f", w2bd[E * e:E * e + E, :, E * e:E * e + E], a["w2"][e])

            for b in range(B):
                for g, (pq, pk) in enumerate(QKG):
                    for side, (st, pt) in enumerate(((qst, pq), (kst, pk))):
                        sp.wait_ge(sem("parts"), 3 * b + pt + 1)
                        for h in range(NH):
                            load(f"stacked{b}", st[HD * g:HD * g + HD, b, h, :],
                                 part[pt][side * E + HD * h:side * E + HD * h + HD, :])
                for n in range(NT):
                    sp.wait_ge(sem("padded"), 6 * (b * NT + n + 1))
                    sp.dma_start(skew[b, n].rearrange("h p c -> p h c"), pad[:, n % 2]).then_inc(sem("skew_out"), 16)
                    sp.wait_ge(sem("skew_out"), 16 * (b * NT + n + 1))
                    for g in range(2):
                        sp.dma_start(bias[HALF * g:HALF * g + HALF, b, n, :, HALF * g:HALF * g + 2 * HALF],
                                     skewed(skew, b, n, g)).then_inc(sem("biased"), 16)

            for u in range(2 * B):
                sp.wait_ge(sem("fin"), u + 1)
                sp.dma_start(a["out"][u // NC, (u % NC) * CT:(u % NC + 1) * CT, :].rearrange("(n p) e -> p n e", p=P),
                             fin[:, u * TC:(u + 1) * TC, :]).then_inc(sem("stored"), 16)
            sp.wait_ge(sem("stored"), 16 * 2 * B)

        @block.gpsimd
        def _(pool):
            def after(ins, name, n):
                ins.then_inc(sem(name), 1)
                pool.wait_ge(sem(name), n)

            after(nc.gpsimd.memset(xsh[V:V + NW, :], -1), "xsh_set", 1)
            after(nc.gpsimd.memset(xcol[:], 0.0), "xcol_set", 1)
            after(nc.gpsimd.memset(hfT[:, :, 0:KC - 1], 0.0), "pool_set", 1)
            after(nc.gpsimd.memset(carry[:, 0:1], 0.0), "pool_set", 2)
            after(nc.gpsimd.memset(states, 0.0), "states_zero", 1)
            after(nc.gpsimd.memset(w2bd[:], 0.0), "w2_zero", 1)
            pool.wait_ge(sem("idx"), 1)
            for n in range(B * NT):
                for k in range(NW):
                    pool.indirect_dma_start(emb[:, n, k, :], None, a["table"],
                                            bass.IndirectOffsetOnAxis(ap=idx[:, k, n:n + 1].bitcast(U32), axis=0)
                                            ).then_inc(sem(f"gathered{n // TC}"), 16)
                if n == 1:
                    after(nc.gpsimd.memset(kst[NP6:P, :, :, :], 1.0), "st_set", 1)
                    after(nc.gpsimd.memset(vt[:, :, :, :, HD:32], 0.0), "vt_zero", 1)
                    after(nc.gpsimd.memset(vt[:, :, :, :, HD:HD + 1], 1.0), "st_set", 2)
                    after(nc.gpsimd.memset(mx[:], -3.0e38), "st_set", 3)
            for b in range(B):
                for n in range(NT):
                    i = b * NT + n
                    pool.wait_ge(sem("padmid"), i + 1)
                    src = pad[:, i % 2]
                    low, high = src[:, :, LPAD:LPAD + 1], src[:, :, LPAD + NR - 1:LPAD + NR]
                    copies = (
                        (src[:, :, 0:LPAD], low.to_broadcast([P, NH, LPAD])),
                        (src[:, :, LPAD + NR:PW], high.to_broadcast([P, NH, PW - LPAD - NR])),
                        (pend[:, b, n, :, 0:1], low),
                        (pend[:, b, n, :, 1:2], high),
                        (bias[0:HALF, b, n, :, 2 * HALF:WIN], high[0:HALF].to_broadcast([HALF, NH, WIN - 2 * HALF])),
                        (bias[HALF:P, b, n, :, 0:WIN - 2 * HALF], low[HALF:P].to_broadcast([HALF, NH, WIN - 2 * HALF])),
                    )
                    for m, (dst, of) in enumerate(copies):
                        nc.gpsimd.tensor_copy(dst, of).then_inc(sem("padded"), 1)
                        if m >= 3:
                            pool.wait_ge(sem("padded"), 6 * i + m + 1)

        @block.scalar
        def _(act):
            def af(out, in_, func, done, **kw):
                nc.scalar.activation(out, in_, func, **kw).then_inc(sem(done), 1)

            act.wait_ge(sem("ld_w"), 16 * 4)
            for b in range(B):
                for c in range(NC):
                    i = b * NC + c
                    act.wait_ge(sem("sc_shift"), i + 1)
                    af(sc[:].rearrange("p n k -> p (n k)"), sc[:].rearrange("p n k -> p (n k)"), ACT.Exp, "sc_exp",
                       scale=E ** -0.5)
                    act.wait_ge(sem("pe_hfT"), i + 1)
                    if i == 0:
                        act.wait_ge(sem("pool_set"), 2)
                    af(hfT[:, b, KC - 1 + c * CT:KC - 1 + (c + 1) * CT], bank[1][0:E, :], ACT.Copy, "hfT")
                    act.wait_ge(sem("pe_conv"), i + 1)
                    if i:
                        act.wait_ge(sem("pe_h0"), i)
                    af(cf[:], bank[2][0:E, :], ACT.Silu, "cf", bias=col("conv_b", 0, E))
                    act.wait_ge(sem("pe_h0"), i + 1)
                    af(hT[:, i * CT:(i + 1) * CT], bank[3], ACT.Silu, "h0", bias=col("b_in"))
                act.wait_ge(sem("pe_gd"), b + 1)
                af(th, bank[4][:, 0:QT], ACT.Tanh, "th", bias=bgh[:], scale=0.5)
                for c in range(NC):
                    i = b * NC + c
                    act.wait_ge(sem("pe_xnT"), i + 1)
                    af(hT[:, i * CT:(i + 1) * CT], bank[0], ACT.Identity, "hn", scale=col("ln_g"), bias=col("ln_b"))
                for l in range(NL):
                    for c in range(NC):
                        i = (b * NL + l) * NC + c
                        act.wait_ge(sem("pe_mlp"), i + 1)
                        if i >= NC:
                            act.wait_ge(sem("mlp_add"), i - 1)
                        af(act_s[:, c, :], bank[1 + c], ACT.Silu, "mlp_silu", bias=col("mlp_b", l))

            def square(i, done):
                act.wait_ge(sem("centered"), i + 1)
                af(lb.rearrange("p n e -> p (n e)"), la.rearrange("p n e -> p (n e)"), ACT.Square, "squared")

            for b in range(B):
                square(b, "")
                for c in range(NC):
                    i = b * NC + c
                    act.wait_ge(sem("pe_lnT"), i + 1)
                    af(lnT[:, i * CT:(i + 1) * CT], bank[c][0:E, :], ACT.Identity, "lnT",
                       scale=col("gamma", 0, E), bias=col("beta", 0, E))
                for c in range(NC):
                    i = b * NC + c
                    act.wait_ge(sem("pe_qk"), i + 1)
                    af(qk32[:, c * CT:(c + 1) * CT], bank[2 + c], ACT.Identity, "qk32", scale=qsc[:], bias=qbi[:])
                    af(qv[:, c * CT:(c + 1) * CT], bank[2 + c][0:E, :], ACT.Identity, "qv", scale=0.25, bias=vbi[:])
                for n in range(NT):
                    i = b * NT + n
                    act.wait_ge(sem("pe_pos"), i + 1)
                    if i >= 2:
                        act.wait_ge(sem("skew_out"), 16 * (i - 1))
                        act.wait_ge(sem("padded"), 6 * (i - 1))
                    af(pad[:, i % 2, :, LPAD:LPAD + NR],
                       bank[5 + i % 2][:, 0:NH * NR].rearrange("p (h r) -> p h r", h=NH), ACT.Copy, "padmid")

            for s in range(B * NC + 1):
                if s:
                    u = s - 1
                    for i in range(NT * NH):
                        e = u * NT * NH + i
                        act.wait_ge(sem("pe_s"), e + 1)
                        if e >= RING:
                            act.wait_ge(sem("pe_pv"), (e - RING) // NH + 1)
                        af(prob[:, e % RING, :], bank[4 + e % 3], ACT.Exp, "exp")
                        if i == 6 and u:
                            act.wait_ge(sem("pe_ctxnT"), u)
                            af(ctxT, bank[7][0:E, :], ACT.Copy, "ctxT")
                    act.wait_ge(sem("pe_pv"), NT * s)
                    af(ctxs, bank[7], ACT.Copy, "ctxs")
                if s < B * NC:
                    act.wait_ge(sem("pe_rows"), s + 1)
                    b, c = divmod(s, NC)
                    for h in range(0, NH, 2):
                        af(qst[NP6:NP6 + 9, b, h, c * CT:(c + 1) * CT], bank[h][NP6:NP6 + 9, :], ACT.Copy, "rows_act")
            act.wait_ge(sem("pe_ctxnT"), B * NC)
            af(ctxT, bank[7][0:E, :], ACT.Copy, "ctxT")

            for b in range(B):
                square(B + b, "")
                for c in range(NC):
                    i = B * NC + b * NC + c
                    act.wait_ge(sem("pe_lnT"), i + 1)
                    af(lnT[:, (i - B * NC) * CT:(i - B * NC + 1) * CT], bank[c][0:E, :], ACT.Copy, "lnT")
            act.wait_ge(sem("rw_shift"), 1)
            af(rw[:].rearrange("p n e -> p (n e)"), rw[:].rearrange("p n e -> p (n e)"), ACT.Exp, "rw_exp")
            act.wait_ge(sem("pe_wT"), 1)
            for j in range(2):
                af(wT[:, j * CT:(j + 1) * CT], bank[3 + j][0:NE, :], ACT.Copy, "wT")
            act.wait_ge(sem("fcols"), 1)
            for u in range(B * NC):
                for p in range(NPAIR):
                    i = u * NPAIR + p
                    act.wait_ge(sem("pe_f1"), i + 1)
                    if i >= 2:
                        act.wait_ge(sem("pe_f2"), i - 1)
                    af(f1[:, i % 2, :], bank[i % 2], ACT.Relu, "f1", scale=fsc[:, 0, p:p + 1], bias=fbi[:, 0, p:p + 1])
                    act.wait_ge(sem("pe_f2"), i + 1)
                    if i >= 2:
                        act.wait_ge(sem("f3"), i - 1)
                    af(f2[:, i % 2, :], bank[2 + i % 2], ACT.Relu, "f2", scale=fsc[:, 1, p:p + 1],
                       bias=fbi[:, 1, p:p + 1])

        @block.vector
        def _(dve):
            n_chain = [0]
            v = nc.vector

            def link(ins):
                n_chain[0] += 1
                ins.then_inc(sem("dve_chain"), 1)
                dve.wait_ge(sem("dve_chain"), n_chain[0])

            def rsqrt(x, n):
                y, t = rs[:, 0:n], rt[:, 0:n]
                link(v.tensor_scalar(t.bitcast(I32), x.bitcast(I32), 1, None, ALU.logical_shift_right))
                link(v.tensor_scalar(y.bitcast(I32), t.bitcast(I32), -1.0, float(0x5F3759DF), ALU.mult, ALU.add))
                for _ in range(3):
                    link(v.tensor_tensor(t, y, y, ALU.mult))
                    link(v.tensor_tensor(t, t, x, ALU.mult))
                    link(v.tensor_scalar(t, t, -0.5, 1.5, ALU.mult, ALU.add))
                    link(v.tensor_tensor(y, y, t, ALU.mult))

            dve.wait_ge(sem("ld_x"), 16)
            v.tensor_copy(xf[:], xi[:]).then_inc(sem("xf"), 1)
            dve.wait_ge(sem("pe_x"), 1)
            dve.wait_ge(sem("xcol_set"), 1)
            v.tensor_copy(xcol[:, :, 1:NT + 1], bank[0][:, 0:B * NT].rearrange("p (b n) -> p b n", b=B)
                          ).then_inc(sem("xcol"), 1)
            dve.wait_ge(sem("pe_hash"), 1)
            link(v.tensor_copy(hi32[:].rearrange("p k n -> p (k n)"), bank[1][:, 0:NW * B * NT]))
            for k in range(NW):
                last = v.tensor_scalar(idx[:, k, :], hi32[:, k, :], MOD - 1, k * MOD, ALU.bitwise_and, ALU.bitwise_or)
            last.then_inc(sem("idx"), 1)
            dve.wait_ge(sem("ld_oh"), 32)
            v.tensor_scalar(onehot[0:V, :], xrep[0:V, :], iota[0:V, :], None, ALU.is_equal).then_inc(sem("onehot"), 1)
            dve.wait_ge(sem("ld_sh"), 16 * 8)
            v.tensor_tensor(onehot[V:V + NW, :], xrep[V:V + NW, :], xsh[V:V + NW, :], ALU.is_equal
                            ).then_inc(sem("onehot"), 1)
            dve.wait_ge(sem("ld_w"), 16 * 4)
            dve.wait_ge(sem("pe_tab"), 1)
            v.tensor_copy(gtab[0:V, :], bank[2][0:V, 0:H]).then_inc(sem("tab"), 1)
            v.tensor_tensor(qtab[:], bank[2][0:V, H:H + E], row("bq")[0:V, :], ALU.add).then_inc(sem("tab"), 1)
            for j in range(KC):
                v.tensor_scalar(cdiag[:, j, :], ident[0:E, 0:E], c64("convw")[:, j:j + 1], None, ALU.mult
                                ).then_inc(sem("tab"), 1)
            for h in range(NH):
                v.tensor_scalar(posb[:, h, :], bank[2][0:E, 256:256 + NR], col("bpos", 0, E),
                                c64("heads")[:, h:h + 1], ALU.add, ALU.mult).then_inc(sem("tab"), 1)
            v.tensor_copy(identb[:], ident[:]).then_inc(sem("tab"), 1)
            v.tensor_scalar(nstart[:], c128("start"), -1.0, 1.0, ALU.mult, ALU.add).then_inc(sem("tab"), 1)
            v.tensor_scalar(bgh[:], col("bg"), 0.5, None, ALU.mult).then_inc(sem("tab"), 1)
            v.memset(qsc[0:E, :], 0.25).then_inc(sem("tab"), 1)
            v.memset(qsc[E:P, :], 1.0).then_inc(sem("tab"), 1)
            link(v.tensor_tensor(qbi[:], col("bqk"), col("u"), ALU.add))
            v.tensor_tensor(vbi[:], col("bqk", 0, E), col("v", 0, E), ALU.add).then_inc(sem("tabx"), 1)
            dve.wait_ge(sem("tabx"), 1)
            v.tensor_scalar(qbi[0:E, :], qbi[0:E, :], 0.25, None, ALU.mult).then_inc(sem("tab"), 1)
            v.tensor_scalar(vbi[:], vbi[:], 0.25, None, ALU.mult).then_inc(sem("tab"), 1)
            for l, name in enumerate(("f1", "f2")):
                o = SCOL[name][0]
                fb, fg, fbe, fm, fv = (cols[:, o + NPAIR * j:o + NPAIR * (j + 1)] for j in range(5))
                link(v.tensor_scalar(rv[:, 0:NPAIR], fv, EPS_BN, None, ALU.add))
                rsqrt(rv[:, 0:NPAIR], NPAIR)
                link(v.tensor_tensor(fsc[:, l, :], fg, rs[:, 0:NPAIR], ALU.mult))
                link(v.tensor_tensor(fbi[:, l, :], fb, fm, ALU.subtract))
                link(v.tensor_tensor(fbi[:, l, :], fbi[:, l, :], fsc[:, l, :], ALU.mult))
                link(v.tensor_tensor(fbi[:, l, :], fbi[:, l, :], fbe, ALU.add))
            dve.sem_inc(sem("fcols"), 1)

            for b in range(B):
                for c in range(NC):
                    i = b * NC + c
                    t0 = i * TC
                    dve.wait_ge(sem("pe_q"), i + 1)
                    dve.wait_ge(sem(f"gathered{i}"), 16 * NW * TC)
                    for n in range(TC):
                        v.tensor_tensor(prod[:, n], emb[:, t0 + n],
                                        bank[5][:, n * E:(n + 1) * E].rearrange("p (o e) -> p o e", o=1)
                                        .to_broadcast([P, NW, E]), ALU.mult).then_inc(sem("prod"), 1)
                    dve.wait_ge(sem("prod"), TC * (i + 1))
                    link(v.tensor_reduce(sc[:], prod[:], AX.X, ALU.add))
                    link(v.tensor_reduce(sm[:], sc[:], AX.X, ALU.max))
                    v.tensor_tensor(sc[:], sc[:], sm[:].rearrange("p (n o) -> p n o", o=1).to_broadcast([P, TC, NW]),
                                    ALU.subtract).then_inc(sem("sc_shift"), 1)
                    dve.wait_ge(sem("sc_exp"), i + 1)
                    link(v.tensor_reduce(sm[:], sc[:], AX.X, ALU.add))
                    link(v.reciprocal(sm[:], sm[:]))
                    link(v.tensor_tensor(sc[:], sc[:], sm[:].rearrange("p (n o) -> p n o", o=1)
                                         .to_broadcast([P, TC, NW]), ALU.mult))
                    for n in range(TC):
                        last = v.tensor_tensor(prod[:, n], emb[:, t0 + n],
                                               sc[:, n].rearrange("p (k o) -> p k o", o=1).to_broadcast([P, NW, E]),
                                               ALU.mult)
                    link(last)
                    if i:
                        dve.wait_ge(sem("pe_hfT"), i)
                    v.tensor_reduce(hf[:], prod[:].rearrange("p n k e -> p n e k"), AX.X, ALU.add).then_inc(sem("hf"), 1)
                dve.wait_ge(sem("pe_gd"), b + 1)
                hb = hT[:, b * T:(b + 1) * T]
                v.tensor_scalar(hb, hb, col("bo"), None, ALU.add).then_inc(sem("h_bo"), 1)
                dve.wait_ge(sem("th"), b + 1)
                link(v.tensor_scalar(ga, th, -0.5, 0.5, ALU.mult, ALU.add))
                link(v.scalar_tensor_tensor(gd, bank[4][:, QT:2 * QT], col("bi"), ga, ALU.add, ALU.mult))
                link(v.tensor_scalar(ga, th, 0.5, 0.5, ALU.mult, ALU.add))
                link(v.tensor_scalar(ga, ga, 1e-6, None, ALU.max))
                link(v.tensor_tensor(d1, ga, c128("start"), ALU.mult))
                link(v.tensor_tensor(d0, ga, nstart[:], ALU.mult))
                link(v.tensor_tensor_scan(cum, d0, d1, 0.0, ALU.mult, ALU.add))
                link(v.tensor_scalar(d0, cum, 1e-8, None, ALU.max))
                link(v.reciprocal(d0, d0))
                link(v.tensor_tensor(d0, gd, d0, ALU.mult))
                link(v.tensor_tensor_scan(cw[:], nstart[:], d0, 0.0, ALU.mult, ALU.add))
                link(v.tensor_tensor(aw[:], cum, cw[:], ALU.mult))
                v.tensor_copy(ends[:, 0, :], cum[:, SCH - 1::SCH])
                v.tensor_copy(ends[:, 1, :], aw[:, SCH - 1::SCH]).then_inc(sem("ends"), 1)
                dve.wait_ge(sem("pe_ends"), b + 1)
                link(v.tensor_copy(endsf[:].rearrange("p q a g -> p (q a g)"), bank[6][0:SS, 0:NQ * 2 * QG]))
                for q in range(NQ):
                    link(v.tensor_tensor_scan(carry[:, 1 + q * QG:1 + (q + 1) * QG], endsf[:, q, 0, :], endsf[:, q, 1, :],
                                              carry[:, q * QG:q * QG + 1], ALU.mult, ALU.add))
                dve.sem_inc(sem("carry"), 1)
                dve.wait_ge(sem("pe_carry"), b + 1)
                link(v.tensor_copy(carryq[:], bank[6][:, 128:128 + QG]))
                link(v.tensor_tensor(cw[:].rearrange("p (g t) -> p g t", g=QG),
                                     cum.rearrange("p (g t) -> p g t", g=QG),
                                     carryq[:].rearrange("p (g o) -> p g o", o=1).to_broadcast([P, QG, SCH]), ALU.mult))
                if not b:
                    dve.wait_ge(sem("states_zero"), 1)
                for q in range(NQ):
                    ps_ = slice(SS * q, SS * q + SS)
                    v.tensor_tensor(states[ps_, q * QT:(q + 1) * QT], cw[ps_, :], aw[ps_, :], ALU.add
                                    ).then_inc(sem("states"), 1)
                for c in range(NC):
                    i = b * NC + c
                    dve.wait_ge(sem("pe_y"), i + 1)
                    y = bank[6 + c].rearrange("p (n f) -> p n f", n=TC)
                    for n in range(TC):
                        last = v.bn_stats(bnc[:, n, :], y[:, n, :])
                    link(last)
                    for n in range(TC):
                        last = v.bn_aggr(bns[:, n, :], bnc[:, n, :])
                    link(last)
                    link(v.tensor_scalar(rv[:, 0:TC], bns[:, :, 1], EPS_LN, None, ALU.add))
                    rsqrt(rv[:, 0:TC], TC)
                    if i:
                        dve.wait_ge(sem("pe_xnT"), i)
                    for n in range(TC):
                        v.tensor_scalar(xn[:, n, :], y[:, n, :], bns[:, n, 0:1], rs[:, n:n + 1], ALU.subtract, ALU.mult
                                        ).then_inc(sem("xn"), 1)
                for l in range(NL):
                    for c in range(NC):
                        i = (b * NL + l) * NC + c
                        h = hT[:, (b * NC + c) * CT:(b * NC + c + 1) * CT]
                        dve.wait_ge(sem("mlp_silu"), i + 1)
                        dve.wait_ge(sem("pe_mlp"), i + 1)
                        v.tensor_tensor(h, h, act_s[:, c, :], ALU.add).then_inc(sem("mlp_add"), 1)
                dve.wait_ge(sem("pe_out"), b + 1)
                v.tensor_tensor(htok[:, b * NT:(b + 1) * NT, :], bank[3].rearrange("p (n e) -> p n e", n=NT),
                                row("bout", NT), ALU.add).then_inc(sem("htok"), 1)

            def norm(b, i, twice):
                dve.wait_ge(sem("htok"), (b + 1) if twice else B + NC * (b + 1))
                if i:
                    dve.wait_ge(sem("pe_lnT"), NC * i)
                h = htok[:, b * NT:(b + 1) * NT, :]
                m = lc[:].rearrange("p (n o) -> p n o", o=1).to_broadcast([P, NT, E])
                link(v.tensor_reduce(lc[:], h, AX.X, ALU.add))
                link(v.tensor_scalar(lc[:], lc[:], 1.0 / E, None, ALU.mult))
                v.tensor_tensor(la, h, m, ALU.subtract).then_inc(sem("centered"), 1)
                dve.wait_ge(sem("squared"), i + 1)
                dve.wait_ge(sem("centered"), i + 1)
                link(v.tensor_reduce(lc[:], lb, AX.X, ALU.add))
                if twice:
                    link(v.tensor_scalar(rv[:, 0:NT], lc[:], (1.0 + EPS_LN) / E, EPS_LN + EPS_LN ** 2, ALU.mult, ALU.add))
                else:
                    link(v.tensor_scalar(rv[:, 0:NT], lc[:], 1.0 / E, EPS_LN, ALU.mult, ALU.add))
                rsqrt(rv[:, 0:NT], NT)
                v.tensor_tensor(la, la, rs[:, 0:NT].rearrange("p (n o) -> p n o", o=1).to_broadcast([P, NT, E]),
                                ALU.mult).then_inc(sem("ln"), 1)

            for b in range(B):
                norm(b, b, True)
                dve.wait_ge(sem("pe_v"), b + 1)
                dve.wait_ge(sem("st_set"), 3)
                v.tensor_tensor(vt[:, b, :, :, 0:HD], bank[4].rearrange("p (n h d) -> p n h d", n=NT, h=NH),
                                rows[:, SROW["bv"][0]:SROW["bv"][1]].rearrange("p (o h d) -> p o h d", o=1, h=NH)
                                .to_broadcast([P, NT, NH, HD]), ALU.add).then_inc(sem("vt"), 1)
                dve.wait_ge(sem("qk32"), NC * (b + 1))
                if b:
                    dve.wait_ge(sem("stacked0"), 16 * 48)
                v.tensor_copy(part[0][:], qk32).then_inc(sem("parts"), 1)
                dve.wait_ge(sem("parts"), 3 * b + 1)
                link(v.tensor_tensor(qk32, qk32, part[0][:], ALU.subtract))
                v.tensor_copy(part[1][:], qk32).then_inc(sem("parts"), 1)
                dve.wait_ge(sem("parts"), 3 * b + 2)
                v.tensor_tensor(part[2][:], qk32, part[1][:], ALU.subtract).then_inc(sem("parts"), 1)

            def region_max(u, j):
                b, c = divmod(u, NC)
                h, n = j % NH, c * TC + j // NH
                i = 16 * u + j
                t0 = n * P
                lo, hi = max(0, t0 - EDGE), min(T, t0 - EDGE + WIN)
                dve.wait_ge(sem("pe_m"), i + 1)
                s1024 = ps[:, 2 * (i % 2):2 * (i % 2) + 2, :].rearrange("p a t -> p (a t)")
                if lo:
                    v.tensor_reduce(mx[:, b, n, h, 0:1], s1024[:, 0:lo], AX.X, ALU.max)
                if hi < T:
                    v.tensor_reduce(mx[:, b, n, h, 2:3], s1024[:, hi:T], AX.X, ALU.max)
                o = lo - (t0 - EDGE)
                if i >= 2:
                    dve.wait_ge(sem("mx"), i - 1)
                v.tensor_tensor_reduce(out=junk[:, i % 2, 0:hi - lo], in0=s1024[:, lo:hi],
                                       in1=bias[:, b, n, h, o:o + hi - lo], scale=1.0, scalar=-3.0e38,
                                       op0=ALU.add, op1=ALU.max, accum_out=mx[:, b, n, h, 1:2]).then_inc(sem("mx"), 1)

            def max_rows(u):
                b, c = divmod(u, NC)
                ns = slice(c * TC, (c + 1) * TC)
                far, m3 = pend[:, b, ns], mx[:, b, ns]
                dve.wait_ge(sem("mx"), 16 * (u + 1))
                if u:
                    dve.wait_ge(sem("pe_rows"), u)
                link(v.tensor_tensor(m3[:, :, :, 0], m3[:, :, :, 0], far[:, :, :, 0], ALU.add))
                link(v.tensor_tensor(m3[:, :, :, 2], m3[:, :, :, 2], far[:, :, :, 1], ALU.add))
                link(v.tensor_reduce(tv[:, 0], m3, AX.X, ALU.max, negate=True))
                link(v.tensor_copy(tv[:, 1], far[:, :, :, 0]))
                link(v.tensor_tensor(tv[:, 2], far[:, :, :, 1], far[:, :, :, 0], ALU.subtract))
                p3 = [tp[:, :, q].rearrange("p a n h -> p a (n h)") for q in range(3)]
                x, r = tv[:].rearrange("p a n h -> p a (n h)"), tr[:].rearrange("p a n h -> p a (n h)")
                link(v.tensor_copy(p3[0], x))
                link(v.tensor_tensor(r, x, p3[0], ALU.subtract))
                link(v.tensor_copy(p3[1], r))
                v.tensor_tensor(p3[2], r, p3[1], ALU.subtract).then_inc(sem("tp"), 1)
                dve.wait_ge(sem("pe_rows"), u + 1)
                for h in range(1, NH, 2):
                    v.tensor_copy(qst[NP6:NP6 + 9, b, h, c * CT:(c + 1) * CT], bank[h][NP6:NP6 + 9, :]
                                  ).then_inc(sem("rows_dve"), 1)

            def normalize(u):
                dve.wait_ge(sem("pe_ctx"), u + 1)
                t4 = bank[7].rearrange("p (n h d) -> p n h d", n=TC, h=NH)
                link(v.reciprocal(den[:], t4[:, :, :, HD]))
                for n in range(TC):
                    v.tensor_tensor(ctxn[:, n].rearrange("p (h d) -> p h d", h=NH), t4[:, n, :, 0:HD],
                                    den[:, n].rearrange("p (h o) -> p h o", o=1).to_broadcast([P, NH, HD]),
                                    ALU.mult).then_inc(sem("ctxn"), 1)

            def residual(u):
                h = htok[:, u * TC:(u + 1) * TC, :]
                link(v.tensor_tensor(h, h, row("ao_b", TC), ALU.add))
                dve.wait_ge(sem("pe_ao"), u + 1)
                v.tensor_tensor(h, h, bank[7][:, 0:TC * E].rearrange("p (n e) -> p n e", n=TC), ALU.add
                                ).then_inc(sem("htok"), 1)

            dve.wait_ge(sem("biased"), 32 * NT * B)
            dve.wait_ge(sem("padded"), 6 * NT * B)
            for s in range(B * NC + 2):
                for j in range(16):
                    if s < B * NC:
                        region_max(s, j)
                    if s >= 2 and j == 1:
                        normalize(s - 2)
                    if s >= 2 and j == 4:
                        residual(s - 2)
                if s < B * NC:
                    max_rows(s)

            for b in range(B):
                norm(b, B + b, False)
            dve.wait_ge(sem("pe_r"), 1)
            link(v.tensor_scalar(rw[:].rearrange("p n e -> p (n e)"), bank[2][:, 0:NT * NE], 0.5, None, ALU.mult))
            link(v.tensor_tensor(rw[:], rw[:], row("br", NT), ALU.add))
            link(v.tensor_reduce(rwm[:], rw[:], AX.X, ALU.max))
            rb = rwm[:].rearrange("p (n o) -> p n o", o=1).to_broadcast([P, NT, NE])
            v.tensor_tensor(rw[:], rw[:], rb, ALU.subtract).then_inc(sem("rw_shift"), 1)
            dve.wait_ge(sem("rw_exp"), 1)
            link(v.tensor_reduce(rwm[:], rw[:], AX.X, ALU.add))
            link(v.reciprocal(rwm[:], rwm[:]))
            v.tensor_tensor(rw[:], rw[:], rb, ALU.mult).then_inc(sem("rw"), 1)
            for u in range(B * NC):
                for p in range(NPAIR):
                    i = u * NPAIR + p
                    dve.wait_ge(sem("f2"), i + 1)
                    if i >= NPAIR:
                        dve.wait_ge(sem("pe_f3"), u)
                    v.tensor_tensor(f3[:, p, :], f2[:, i % 2, :], bank[4 + i % 2], ALU.mult).then_inc(sem("f3"), 1)
                dve.wait_ge(sem("pe_f3"), u + 1)
                v.tensor_tensor(fin[:, u * TC:(u + 1) * TC, :], htok[:, u * TC:(u + 1) * TC, :],
                                bank[6][:, 0:TC * E].rearrange("p (n e) -> p n e", n=TC), ALU.add
                                ).then_inc(sem("fin"), 1)

        @block.tensor
        def _(pe):
            mm = nc.tensor.matmul

            def tr_(out, in_, n=P):
                return nc.tensor.transpose(out, in_, ident[0:n, 0:n])

            pe.wait_ge(sem("ld_ident"), 16)
            pe.wait_ge(sem("xf"), 1)
            tr_(bank[0][:, 0:B * NT], xf[:], B * NT).then_inc(sem("pe_x"), 1)
            pe.wait_ge(sem("ld_band"), 16)
            pe.wait_ge(sem("xcol"), 1)
            for k in range(NW):
                o = bank[1][:, k * B * NT:(k + 1) * B * NT].rearrange("p (b n) -> p b n", b=B)
                mm(o, band[:, 0, k, :], xcol[:, :, 1:NT + 1], start=True, stop=False)
                last = mm(o, band[:, 1, k, :], xcol[:, :, 0:NT], start=False, stop=True)
            last.then_inc(sem("pe_hash"), 1)
            pe.wait_ge(sem("ld_emb"), 32)
            mm(bank[2][0:V, 0:H + E], emb3[:, 0:V], emb3[:, V:V + H + E], start=True, stop=True)
            pe.wait_ge(sem("ld_w"), 16 * 4)
            mm(bank[2][0:E, 256:256 + NR], c64("wpos"), c64("encT"), start=True, stop=True).then_inc(sem("pe_tab"), 1)
            pe.wait_ge(sem("tab"), 17)
            pe.wait_ge(sem("onehot"), 2)
            for b in range(B):
                for c in range(NC):
                    i = b * NC + c
                    if i:
                        pe.wait_ge(sem("prod"), TC * i)
                    for n in range(TC):
                        t0 = (i * TC + n) * P
                        last = mm(bank[5][:, n * E:(n + 1) * E], onehot[0:V, t0:t0 + P], qtab[:], start=True, stop=True)
                    last.then_inc(sem("pe_q"), 1)
                    pe.wait_ge(sem("hf"), i + 1)
                    if i:
                        pe.wait_ge(sem("hfT"), i)
                    if b and not c:
                        pe.wait_ge(sem("mlp_silu"), NL * NC * b)
                    for n in range(TC):
                        last = tr_(bank[1][0:E, n * P:(n + 1) * P], hf[:, n, :])
                    last.then_inc(sem("pe_hfT"), 1)
                    pe.wait_ge(sem("hfT"), i + 1)
                    if i:
                        pe.wait_ge(sem("cf"), i)
                    for j in range(KC):
                        last = mm(bank[2][0:E, :], cdiag[:, j, :], hfT[:, b, c * CT + j:c * CT + j + CT],
                                  start=(j == 0), stop=(j == KC - 1))
                    last.then_inc(sem("pe_conv"), 1)
                    if i:
                        pe.wait_ge(sem("h0"), i)
                    if b and not c:
                        pe.wait_ge(sem("htok"), b)
                    mm(bank[3], gtab[:], onehot[:, i * CT:(i + 1) * CT], start=True, stop=False)
                    pe.wait_ge(sem("cf"), i + 1)
                    mm(bank[3], c64("winh"), cf[:], start=False, stop=True).then_inc(sem("pe_h0"), 1)
                pe.wait_ge(sem("h0"), NC * (b + 1))
                if b:
                    pe.wait_ge(sem("states"), NQ * b)
                for o, w in ((0, "wg"), (QT, "wi")):
                    for q in range(NQ):
                        last = mm(bank[4][SS * q:SS * q + SS, o:o + QT], c128(w),
                                  hT[:, b * T + q * QT:b * T + (q + 1) * QT], start=True, stop=True)
                last.then_inc(sem("pe_gd"), 1)
                pe.wait_ge(sem("ends"), b + 1)
                for q in range(NQ):
                    last = mm(bank[6][0:SS, q * 2 * QG:(q + 1) * 2 * QG], ident[:, SS * q:SS * q + SS],
                              ends[:].rearrange("p a g -> p (a g)"), start=True, stop=True)
                last.then_inc(sem("pe_ends"), 1)
                pe.wait_ge(sem("carry"), b + 1)
                for q in range(NQ):
                    last = mm(bank[6][SS * q:SS * q + SS, 128:128 + QG], ident[0:SS, 0:SS],
                              carry[:, q * QG:(q + 1) * QG], start=True, stop=True)
                last.then_inc(sem("pe_carry"), 1)
                pe.wait_ge(sem("h_bo"), b + 1)
                pe.wait_ge(sem("states"), NQ * (b + 1))
                for c in range(NC):
                    for n in range(TC):
                        t0 = c * CT + n * P
                        o = bank[6 + c][:, n * H:(n + 1) * H]
                        mm(o, hT[:, b * T + t0:b * T + t0 + P], ident[:], start=True, stop=False)
                        last = mm(o, states[:, t0:t0 + P], c128("wo4"), start=False, stop=True)
                    last.then_inc(sem("pe_y"), 1)
                for c in range(NC):
                    i = b * NC + c
                    pe.wait_ge(sem("xn"), TC * (i + 1))
                    if i:
                        pe.wait_ge(sem("hn"), i)
                    for n in range(TC):
                        last = tr_(bank[0][:, n * P:(n + 1) * P], xn[:, n, :])
                    last.then_inc(sem("pe_xnT"), 1)
                for l in range(NL):
                    for c in range(NC):
                        i = b * NC + c
                        if l:
                            pe.wait_ge(sem("mlp_add"), (b * NL + l - 1) * NC + c + 1)
                        else:
                            pe.wait_ge(sem("hn"), i + 1)
                        mm(bank[1 + c], c128("mlp")[:, l * H:(l + 1) * H], hT[:, i * CT:(i + 1) * CT],
                           start=True, stop=True).then_inc(sem("pe_mlp"), 1)
                pe.wait_ge(sem("mlp_add"), NL * NC * (b + 1))
                for n in range(NT):
                    last = mm(bank[3][:, n * E:(n + 1) * E], hT[:, b * T + n * P:b * T + (n + 1) * P], c128("wout"),
                              start=True, stop=True)
                last.then_inc(sem("pe_out"), 1)

            def ln_transposes(i):
                pe.wait_ge(sem("ln"), i + 1)
                for c in range(NC):
                    if i:
                        pe.wait_ge(sem("lnT"), NC * (i - 1) + c + 1)
                    for n in range(TC):
                        last = tr_(bank[c][0:E, n * P:(n + 1) * P], la[:, c * TC + n, :])
                    last.then_inc(sem("pe_lnT"), 1)

            for b in range(B):
                ln_transposes(b)
                for c in range(NC):
                    i = b * NC + c
                    pe.wait_ge(sem("lnT"), i + 1)
                    if b:
                        pe.wait_ge(sem("qv"), NC * (b - 1) + c + 1)
                    else:
                        pe.wait_ge(sem("htok"), B)
                    mm(bank[2 + c], c64("aqk"), lnT[:, i * CT:(i + 1) * CT], start=True, stop=True
                       ).then_inc(sem("pe_qk"), 1)
                if b:
                    pe.wait_ge(sem("vt"), b)
                for n in range(NT):
                    last = mm(bank[4][:, n * E:(n + 1) * E], lnT[:, b * T + n * P:b * T + (n + 1) * P], c64("av"),
                              start=True, stop=True)
                last.then_inc(sem("pe_v"), 1)
                pe.wait_ge(sem("qv"), NC * (b + 1))
                for n in range(NT):
                    i = b * NT + n
                    if i >= 2:
                        pe.wait_ge(sem("padmid"), i - 1)
                    mm(bank[5 + i % 2][:, 0:NH * NR], qv[:, n * P:(n + 1) * P], posb[:].rearrange("e h r -> e (h r)"),
                       start=True, stop=True).then_inc(sem("pe_pos"), 1)

            def max_scores(u, j):
                b, c = divmod(u, NC)
                h, n = j % NH, c * TC + j // NH
                i = 16 * u + j
                if i >= 2:
                    pe.wait_ge(sem("mx"), i - 1)
                for a_ in range(2):
                    last = mm(bank[2 * (i % 2) + a_], qst[0:NP6, b, h, n * P:(n + 1) * P],
                              kst[0:NP6, b, h, a_ * 512:(a_ + 1) * 512], start=True, stop=True)
                last.then_inc(sem("pe_m"), 1)

            def key_scores(u, i):
                b, c = divmod(u, NC)
                k, h = divmod(i, NH)
                e = u * NT * NH + i
                if e >= 3:
                    pe.wait_ge(sem("exp"), e - 2)
                o = bank[4 + e % 3]
                t0 = c * CT
                left, right = min(max(k * P, t0), t0 + CT), min(max((k + 1) * P, t0), t0 + CT)

                def product(rows_, s0, s1, q0, q1, at, stop):
                    return mm(o[at:at + s1 - s0, q0 - t0:q1 - t0], kst[0:rows_, b, h, s0:s1], qst[0:rows_, b, h, q0:q1],
                              start=True, stop=stop)

                def position(j0, j1, n, at):
                    return mm(o[at:at + j1 - j0, n * P - t0:(n + 1) * P - t0], bias[:, b, n, h, j0:j1], ident[:],
                              start=False, stop=True)

                if left > t0:
                    last = product(NP6 + 9, k * P, (k + 1) * P, t0, left, 0, True)
                if right < t0 + CT:
                    last = product(NP6 + 6, k * P, (k + 1) * P, right, t0 + CT, 0, True)
                if left < right:
                    product(NP6 + 3, k * P, (k + 1) * P, left, right, 0, False)
                    last = position(EDGE, EDGE + P, k, 0)
                if t0 <= (k - 1) * P < t0 + CT:
                    product(NP6 + 3, k * P, k * P + EDGE, (k - 1) * P, k * P, 0, False)
                    last = position(EDGE + P, WIN, k - 1, 0)
                if t0 <= (k + 1) * P < t0 + CT:
                    product(NP6 + 3, (k + 1) * P - EDGE, (k + 1) * P, (k + 1) * P, (k + 2) * P, P - EDGE, False)
                    last = position(0, EDGE, k + 1, P - EDGE)
                last.then_inc(sem("pe_s"), 1)

            def weigh(u, k):
                b = u // NC
                pe.wait_ge(sem("exp"), (u * NT + k + 1) * NH)
                if u and k == 0:
                    pe.wait_ge(sem("htok"), B + u)
                for h in range(NH):
                    last = mm(bank[7][32 * h:32 * h + 32, :], vt[:, b, k, h, :], prob[:, ((u * NT + k) * NH + h) % RING, :],
                              start=(k == 0), stop=(k == NT - 1))
                last.then_inc(sem("pe_pv"), 1)

            def finish(u, step):
                if step == 0:
                    pe.wait_ge(sem("ctxs"), u + 1)
                    for n in range(TC):
                        last = tr_(bank[7][:, n * P:(n + 1) * P], ctxs[:, n * P:(n + 1) * P])
                    last.then_inc(sem("pe_ctx"), 1)
                elif step == 1:
                    pe.wait_ge(sem("ctxn"), TC * (u + 1))
                    for n in range(TC):
                        last = tr_(bank[7][0:E, n * P:(n + 1) * P], ctxn[:, n, :])
                    last.then_inc(sem("pe_ctxnT"), 1)
                else:
                    pe.wait_ge(sem("ctxT"), u + 1)
                    for n in range(TC):
                        last = mm(bank[7][:, n * E:(n + 1) * E], ctxT[:, n * P:(n + 1) * P], c64("ao"),
                                  start=True, stop=True)
                    last.then_inc(sem("pe_ao"), 1)

            for b in range(B):
                pe.wait_ge(sem(f"stacked{b}"), 16 * 48)
            pe.wait_ge(sem("st_set"), 3)
            pe.wait_ge(sem("qv"), NC * B)
            pe.wait_ge(sem("vt"), B)
            pe.wait_ge(sem("padmid"), B * NT)
            pe.wait_ge(sem("padded"), 6 * B * NT)
            pe.wait_ge(sem("biased"), 32 * B * NT)
            for s in range(B * NC + 2):
                for j in range(16):
                    if s < B * NC:
                        max_scores(s, j)
                    if 1 <= s <= B * NC:
                        key_scores(s - 1, 2 * j)
                        key_scores(s - 1, 2 * j + 1)
                    if s >= 2 and j in (0, 2, 4):
                        finish(s - 2, j // 2)
                    if 1 <= s <= B * NC and j >= 6 and j % 2 == 0:
                        weigh(s - 1, (j - 6) // 2)
                if 1 <= s <= B * NC:
                    for k in range(5, NT):
                        weigh(s - 1, k)
                if s < B * NC:
                    pe.wait_ge(sem("tp"), s + 1)
                    for h in range(NH):
                        for n in range(TC):
                            last = mm(bank[h][NP6:NP6 + 9, n * P:(n + 1) * P],
                                      tp[:, :, :, n, h].rearrange("p a q -> p (a q)"), identb[:], start=True, stop=True)
                    last.then_inc(sem("pe_rows"), 1)
                    pe.wait_ge(sem("rows_act"), 2 * (s + 1))
                    pe.wait_ge(sem("rows_dve"), 2 * (s + 1))

            for b in range(B):
                ln_transposes(B + b)
            pe.wait_ge(sem("lnT"), 2 * NC * B)
            for n in range(NT):
                o = bank[2][:, n * NE:(n + 1) * NE]
                mm(o, lnT[:, n * P:(n + 1) * P], c64("wr"), start=True, stop=False)
                last = mm(o, lnT[:, T + n * P:T + (n + 1) * P], c64("wr"), start=False, stop=True)
            last.then_inc(sem("pe_r"), 1)
            pe.wait_ge(sem("rw"), 1)
            for n in range(NT):
                last = tr_(bank[3 + n // TC][0:NE, n % TC * P:(n % TC + 1) * P], rw[:, n, :])
            last.then_inc(sem("pe_wT"), 1)
            pe.wait_ge(sem("wT"), 2)
            pe.wait_ge(sem("ld_f"), 16 * 4)
            for u in range(B * NC):
                t0 = (u % NC) * CT
                for p in range(NPAIR):
                    i = u * NPAIR + p
                    if i >= 2:
                        pe.wait_ge(sem("f1"), i - 1)
                    mm(bank[i % 2], c64("w1")[:, p * P:(p + 1) * P], lnT[:, u * CT:(u + 1) * CT],
                       start=True, stop=True).then_inc(sem("pe_f1"), 1)
                    if i >= 2:
                        pe.wait_ge(sem("f3"), i - 1)
                    mm(bank[4 + i % 2], pair[:, p, :], wT[:, t0:t0 + CT], start=True, stop=True)
                    pe.wait_ge(sem("f1"), i + 1)
                    if i >= 2:
                        pe.wait_ge(sem("f2"), i - 1)
                    mm(bank[2 + i % 2], w2bd[:, p, :], f1[:, i % 2, :], start=True, stop=True).then_inc(sem("pe_f2"), 1)
                if u:
                    pe.wait_ge(sem("fin"), u)
                pe.wait_ge(sem("f3"), NPAIR * (u + 1))
                for n in range(TC):
                    o = bank[6][:, n * E:(n + 1) * E]
                    mm(o, wT[:, t0 + n * P:t0 + (n + 1) * P], bo8[:], start=True, stop=False)
                    for p in range(NPAIR):
                        last = mm(o, f3[:, p, n * P:(n + 1) * P], c128("fwo")[:, p * E:(p + 1) * E],
                                  start=False, stop=(p == NPAIR - 1))
                last.then_inc(sem("pe_f3"), 1)


def skewed(skew, b, n, g):
    flat = skew[b, n].rearrange("h p c -> h (p c)")
    at = HALF * g * PW + LPAD - 2
    return flat[:, at:at + HALF * (PW - 1)].rearrange("h (i c) -> i h c", c=PW - 1)[:, :, 0:2 * HALF]


def layout(inputs):
    w = {k: np.asarray(v) for k, v in inputs.items()}
    t = lambda n: w["L0_tok_" + n]
    a = lambda n: w["L0_attn_" + n]
    f = lambda n: w["L0_ffn_" + n]
    k = constants()
    tall = lambda x, n=P: np.concatenate([x, np.zeros((n - x.shape[0], x.shape[1]), np.float32)])
    pairs = lambda x: x.reshape(NPAIR, 2 * E).T
    v1 = lambda x: x.reshape(-1, 1)
    w128 = {
        "mlp": t("mlp_w").transpose(1, 0, 2).reshape(H, NL * H), "wg": t("Wg"), "wi": t("Wi"), "wout": t("Wout"),
        "wo4": np.tile(t("Wo"), (NQ, 1)),
        "fwo": f("Wo").reshape(NPAIR, 2 * E, E).transpose(1, 0, 2).reshape(P, NPAIR * E), "start": k["start"],
    }
    w64 = {
        "winh": t("Win")[E:2 * E], "aqk": np.concatenate([a("Wq").T, a("Wk").T], 1), "av": a("Wv").T,
        "wpos": a("Wpos").T, "encT": k["encT"], "ao": a("Wo").T, "wr": f("Wr"),
        "w1": f("W1").transpose(1, 0, 2).reshape(E, NE * E), "heads": k["heads"], "convw": t("conv_w")[:, 0, :],
    }
    cols = {
        "b_in": v1(t("b_in")), "ln_g": v1(t("ln_g")), "ln_b": v1(t("ln_b")), "mlp_b": t("mlp_b").T,
        "bg": np.tile(v1(t("bg")), (NQ, 1)), "bi": np.tile(v1(t("bi")), (NQ, 1)), "conv_b": tall(v1(t("conv_b"))),
        "gamma": tall(v1(a("ln_gamma"))), "beta": tall(v1(a("ln_beta"))),
        "bqk": np.concatenate([v1(a("bq")), v1(a("bk"))]), "u": tall(v1(a("u_bias"))), "v": tall(v1(a("v_bias"))),
        "bpos": tall(v1(a("bpos"))), "bo": v1(t("bo")),
        "f1": np.concatenate([pairs(f(n)) for n in ("b1", "g1", "be1", "m1", "v1")], 1),
        "f2": np.concatenate([pairs(f(n)) for n in ("b2", "g2", "be2", "m2", "v2")], 1),
    }
    rows = {"bq": t("bq"), "bout": t("bout"), "bv": a("bv"), "ao_b": a("bo"), "br": f("br")}
    side = lambda pack, d: np.concatenate([d[n] for n, _ in pack], 1)
    return {
        "x": w["x"], "ident": k["ident"], "band": k["band"], "iota": k["iota"], "pair": k["pair"],
        "emb3": np.concatenate([t("emb_byte").T, t("Win")[0:E], t("Wq")], 1), "winm": t("Win")[2 * E:],
        "w128": side(PACK128, w128), "w64": side(PACK64, w64), "cols": side(COLS, cols),
        "rows": np.concatenate([rows[n] for n, _ in ROWS])[None, :], "bo8": f("bo"),
        "w2": f("W2").reshape(NPAIR, 2, E, E).transpose(1, 2, 0, 3), "table": t("hash_tables").reshape(NW * MOD, E),
    }


def kernel(**inputs):
    import concourse.bacc as bacc
    from concourse.bass_utils import run_bass_kernel_spmd

    nc = bacc.Bacc("TRN2", target_bir_lowering=False, num_devices=1)
    arrays = {k: np.ascontiguousarray(v) for k, v in layout(inputs).items()}
    tensors = {k: nc.dram_tensor("in_" + k, v.shape, mybir.dt.from_np(v.dtype), kind="ExternalInput").ap()
               for k, v in arrays.items()}
    tensors["out"] = nc.dram_tensor("result", (B, T, E), F32, kind="ExternalOutput").ap()
    tensors["skew"] = nc.dram_tensor("skewed", (B, NT, NH, P, PW), F32).ap()
    tower(nc, tensors)
    return run_bass_kernel_spmd(nc, [{"in_" + k: v for k, v in arrays.items()}], core_ids=[0]).results[0]["result"]
```

```python
from contextlib import ExitStack

import numpy as np

import concourse.bass as bass
from concourse import mybir

F32 = mybir.dt.float32
BF16 = mybir.dt.bfloat16
I32 = mybir.dt.int32
U32 = mybir.dt.uint32
ALU = mybir.AluOpType
ACT = mybir.ActivationFunctionType
AX = mybir.AxisListType

P = 128
B, T = 2, 1024
NT = T // P
NC = 2
CT = T // NC
TC = CT // P
V = 64
E = 64
H = 128
SS = 32
NW = 4
WINDOWS = (2, 4, 8, 16)
OFFSETS = (1, 2, 4, 8)
BASE, MOD = 257, 1024
KC = 4
SCH = 32
NQ = 4
QT = T // NQ
QG = QT // SCH
NL = 3
NH, HD = 4, 16
REL = 30
NR = 2 * REL + 1
HALF = 64
LPAD = HALF + 1
PW = 192
WIN = 192
EDGE = 32
NP6 = 96
NE, NPAIR = 8, 4
EPS_LN, EPS_BN = 1e-5, 1e-3
RING = 12
EXPERT_UNITS = tuple(b * NC + c for c in range(NC) for b in range(B))
QKG = ((0, 0), (0, 1), (1, 0), (0, 2), (2, 0), (1, 1))


UNITS = B * NC
PROLOGUE = (
    ("weigh", 0, 0), ("hidden", 0, 0), ("weigh", 0, 1), ("hidden", 0, 1), ("tail", 0, 0), ("tail", 0, 1),
    ("weigh", 1, 0), ("tail", 0, 2), ("tail", 0, 3), ("hidden", 1, 0), ("tail", 0, 4), ("tail", 0, 5), ("tail", 0, 6),
    ("weigh", 1, 1), ("tail", 0, 7), ("hidden", 1, 1), ("tail", 0, 8), ("tail", 1, 0), ("setup", 0, 0), ("tail", 1, 1),
    ("setup", 0, 1), ("tail", 1, 2), ("setup", 0, 2), ("tail", 1, 3), ("setup", 0, 3), ("tail", 1, 4), ("tail", 1, 5))
SIDE = (("tail", 1, 6), ("tail", 1, 7), ("tail", 1, 8), *(("setup", 1, k) for k in range(4)))
BESIDE = {(0, 1 + j): (step,) for j, step in enumerate(SIDE)} | {
    (UNITS, 6 + k): (("route", 0, k),) for k in range(4)} | {
    (UNITS, 10 + g): (("pair", g),) for g in range(5)} | {
    (UNITS, 15): tuple(("pair", g) for g in range(5, B * NPAIR))}
EPILOGUE = (*(("route", 1, k) for k in range(4)), *(("pair", g) for g in range(B * NPAIR, 2 * B * NPAIR)))


def tail_bank(b, k):
    return 0 if b and k <= 5 else 4


def f2_bank(g):
    return 2 if g < B * NPAIR or g % 2 else 4


def constants():
    power = [1]
    for _ in range(max(WINDOWS) - 1):
        power.append(power[-1] * BASE % MOD)
    band = np.zeros((P, 2, NW, P), np.float32)
    for k, w in enumerate(WINDOWS):
        for j in range(w):
            for t in range(P):
                src = t - j
                band[src % P, 0 if src >= 0 else 1, k, t] = power[j]
    n = np.arange(NR, dtype=np.float32)[:, None]
    div = np.exp(np.arange(0, E, 2, dtype=np.float32) * np.float32(-np.log(10000.0) / E)).astype(np.float32)
    ang = n * div
    enc = np.stack([np.sin(ang), np.cos(ang)], axis=-1).reshape(NR, E).astype(np.float32)
    heads = (np.arange(E)[:, None] // HD == np.arange(NH)[None, :]).astype(np.float32)
    start = (np.arange(QT) % SCH == 0).astype(np.float32)
    pair = (np.arange(NE)[:, None, None] == 2 * np.arange(NPAIR)[None, :, None] + np.arange(P)[None, None, :] // E)
    return {
        "band": band.reshape(P, -1),
        "ident": np.eye(P, dtype=np.float32),
        "encT": np.ascontiguousarray(enc.T),
        "heads": heads,
        "start": np.broadcast_to(start, (P, QT)).copy(),
        "pair": pair.astype(np.float32).reshape(NE, NPAIR * P),
        "iota": np.arange(P, dtype=np.float32)[:, None],
    }


PACK128 = (("mlp", NL * H), ("wg", SS), ("wi", SS), ("wout", E), ("wo4", H), ("fwo", NPAIR * E), ("start", QT))
PACK64 = (("winh", H), ("aqk", 2 * E), ("av", E), ("wpos", E), ("encT", NR), ("ao", E), ("wr", NE), ("w1", NE * E),
          ("heads", NH))
COLS = (("b_in", 1), ("ln_g", 1), ("ln_b", 1), ("mlp_b", NL), ("bg", 1), ("bi", 1), ("conv_b", 1), ("gamma", 1),
        ("beta", 1), ("bqk", 1), ("u", 1), ("v", 1), ("bpos", 1), ("bo", 1), ("convw", KC // 2), ("f1", 5 * NPAIR), ("f2", 5 * NPAIR))
ROWS = (("bq", E), ("bout", E), ("bv", E), ("ao_b", E), ("br", NE))


def spans(pack):
    at, out = 0, {}
    for name, n in pack:
        out[name] = (at, at + n)
        at += n
    return out, at


S128, N128 = spans(PACK128)
S64, N64 = spans(PACK64)
SCOL, NCOL = spans(COLS)
SROW, NROW = spans(ROWS)


def tower(nc, a):
    with ExitStack() as ctx:
        def sb(name, shape, dt=F32):
            return ctx.enter_context(nc.sbuf_tensor(name, shape, dt))

        made = {}

        def sem(name):
            if name not in made:
                made[name] = ctx.enter_context(nc.semaphore(name))
            return made[name]

        ps = ctx.enter_context(nc.psum_tensor("ps", [P, 8, 512], F32))
        bank = [ps[:, i, :] for i in range(8)]

        w128, w64, cols, rows = sb("w128", [P, N128]), sb("w64", [P, N64]), sb("cols", [P, NCOL]), sb("rows", [P, NROW])
        ident, band = sb("ident", [P, P]), sb("band", [P, 2, NW, P])
        emb3 = sb("emb3", [E, V + H + E])
        iota, pair = sb("iota", [P, 1]), sb("pair", [P, NPAIR, P])
        xi, xf = sb("xi", [B * NT, P], I32), sb("xf", [B * NT, P])
        xcol = sb("xcol", [P, B, NT + 1])
        hi32 = sb("hi32", [P, NW, B * NT], I32)
        idx = sb("idx", [P, NW, B * NT], I32)
        prob = sb("prob", [P, RING, CT])
        probf = prob[:].rearrange("p r t -> p (r t)")
        emb = probf[:, 0:B * NT * NW * E].rearrange("p (n k e) -> p n k e", k=NW, e=E)
        onehot = probf[0:V + NW, B * NT * NW * E:B * NT * NW * E + B * T]
        gtab = sb("gtab", [V + NW, H])
        qtab = sb("qtab", [V, E])
        cdiag = sb("cdiag", [P, KC // 2, E])
        posb = sb("posb", [P, NH, NR])
        prod = sb("prod", [P, TC, NW, E])
        sc, sm = sb("sc", [P, TC, NW]), sb("sm", [P, TC])
        hf = sb("hf", [P, TC, E])
        hfT = sb("hfT", [P, B, KC - 1 + T])
        cf = sb("cf", [E, CT])
        hT = sb("hT", [H, B * T])
        scan = sb("scan", [P, 6, QT])
        th, ga, gd, d0, d1, cum = (scan[:, i, :] for i in range(6))
        nstart = sb("nstart", [P, QT])
        cw, aw = sb("cw", [P, QT]), sb("aw", [P, QT])
        ends = sb("ends", [P, 2, QG])
        endsf = sb("endsf", [SS, NQ, 2, QG])
        carry = sb("carry", [SS, 1 + NQ * QG])
        carryq = sb("carryq", [P, QG])
        bnc, bns = sb("bnc", [P, TC, 6]), sb("bns", [P, TC, 2])
        rs, rt, rv = sb("rs", [P, 32]), sb("rt", [P, 32]), sb("rv", [P, 32])
        xn = sb("xn", [P, NC, TC, H])
        act_s = sb("act_s", [H, NC, CT])
        qsc, qbi, vbi, bgh = sb("qsc", [P, 1]), sb("qbi", [P, 1]), sb("vbi", [E, 1]), sb("bgh", [P, 1])
        htok = sb("htok", [P, B * NT, E])
        prodf = prod[:].rearrange("p n k e -> p (n k e)")
        la, lb = (prodf[:, i * NT * E:(i + 1) * NT * E].rearrange("p (n e) -> p n e", e=E) for i in range(2))
        lc = sb("lc", [P, NT])
        states = band[:].rearrange("p a k t -> p (a k t)")
        lnT = sb("lnT", [P, B * T])[:]
        qk32 = act_s[:].rearrange("p c t -> p (c t)")
        hfTf = hfT[:].rearrange("p b t -> p (b t)")
        qv, wT = hfTf[:, 0:T], hfTf[:, T:2 * T]
        fin = hT[:, 0:B * NT * E].rearrange("p (n e) -> p n e", e=E)
        ctxs, ctxT = hT[:, B * NT * E:B * NT * E + CT], hT[0:E, B * NT * E + CT:B * NT * E + 2 * CT]
        part = [sb(f"part{i}", [P, T], BF16) for i in range(3)]
        qst, kst = sb("qst", [P, B, NH, T], BF16), sb("kst", [P, B, NH, T], BF16)
        vt = sb("vt", [P, B, NT, NH, 32])
        pad = probf.rearrange("p (c n h w) -> p c n h w", c=NC, n=TC, h=NH)
        bias = sb("bias", [P, B, NT, NH, WIN])
        pend = sb("pend", [P, B, NT, NH, 2])
        mx = sb("mx", [P, B, NT, NH, 3])
        junk = sb("junk", [P, 2, WIN], BF16)
        tv = sb("tv", [P, 3, TC, NH])
        tr = sb("tr", [P, 3, TC, NH])
        tp = sb("tp", [P, 3, 3, TC, NH], BF16)
        identb = sb("identb", [P, P], BF16)
        den = sb("den", [P, TC, NH])
        xnf = xn[:].rearrange("p c n h -> p (c n h)")
        ctxn = xnf[:, 0:TC * E].rearrange("p (n e) -> p n e", e=E)
        rw = xnf[:, TC * E:TC * (E + NE)].rearrange("p (n e) -> p n e", e=NE)
        rwf = rw.rearrange("p n e -> p (n e)")
        w2bd = scan[:, 0:2, :].rearrange("p a (b t) -> p (a b) t", t=P)
        fsc, fbi = sb("fsc", [P, 2, NPAIR]), sb("fbi", [P, 2, NPAIR])
        bo8 = sb("bo8", [NE, E])
        rwm = sb("rwm", [P, TC])
        ff = bias[:, 0].rearrange("p n h w -> p (n h w)").rearrange("p (s t) -> p s t", t=CT)
        f1, f2, f3, wbc = ff[:, 0:2], ff[:, 2:4], ff[:, 4:4 + NPAIR], ff[:, 4 + NPAIR:4 + 2 * NPAIR]
        spare = bias[:, 1].rearrange("p n h w -> p (n h w)").bitcast(I32)
        xrep, xsh = spare[0:V + NW, 0:B * T], spare[0:V + NW, B * T:2 * B * T]

        def c128(name):
            return w128[:, S128[name][0]:S128[name][1]]

        def c64(name, n=E):
            return w64[0:n, S64[name][0]:S64[name][1]]

        def col(name, i=0, n=P):
            return cols[0:n, SCOL[name][0] + i:SCOL[name][0] + i + 1]

        def row(name, *mid):
            r = rows[:, SROW[name][0]:SROW[name][1]]
            for k in mid:
                r = r.rearrange("p (o n) -> p o n", o=1).to_broadcast([P, k, r.shape[-1]])
            return r

        def padding(c, at, to, of):
            rows_ = pad[:, c].rearrange("p n h w -> p (n h) w")
            return rows_[:, :, at:to], rows_[:, :, of:of + 1].to_broadcast([P, TC * NH, to - at])

        skew = a["skew"]
        block = ctx.enter_context(nc.Block())

        @block.sync
        def _(sp):
            def load(name, dst, src):
                sp.dma_start(dst, src).then_inc(sem(name), 16)

            load("ld_x", xi[:], a["x"].rearrange("b (n p) -> (b n) p", p=P))
            load("ld_ident", ident[:], a["ident"])
            load("ld_band", band[:].rearrange("p a k t -> p (a k t)"), a["band"])
            flat = a["x"].rearrange("b t -> (b t)").rearrange("(o n) -> o n", o=1)
            load("ld_oh", xrep, flat.to_broadcast([V + NW, B * T]))
            load("ld_oh", iota[:], a["iota"])
            sp.wait_ge(sem("xsh_set"), 1)
            for k, o in enumerate(OFFSETS):
                for b in range(B):
                    load("ld_sh", xsh[V + k:V + k + 1, b * T + o:(b + 1) * T], flat[:, b * T:(b + 1) * T - o])
            load("ld_emb", emb3[:], a["emb3"])
            load("ld_emb", gtab[V:V + NW, :], a["winm"])
            load("ld_w", w64[:], a["w64"])
            load("ld_w", cols[:], a["cols"])
            load("ld_w", rows[:], a["rows"].to_broadcast([P, NROW]))
            load("ld_w", w128[:], a["w128"])
            load("ld_f", pair[:].rearrange("e a p -> e (a p)"), a["pair"])
            load("ld_f", bo8[:], a["bo8"])

            for b in range(B):
                for i in range(3):
                    sp.wait_ge(sem("parts"), 3 * b + i + 1)
                    sp.dma_start(a["parts"][b, i].rearrange("s h d t -> (s h d) t"), part[i][:]
                                 ).then_inc(sem(f"part_out{i}"), 16)
                for i in range(3):
                    sp.wait_ge(sem(f"part_out{i}"), 16 * (b + 1))
                    for g, pair_ in enumerate(QKG):
                        for side, st in enumerate((qst, kst)):
                            if pair_[side] == i:
                                load(f"stacked{b}", st[HD * g:HD * g + HD, b, :, :],
                                     a["parts"][b, i, side].rearrange("h d t -> d h t"))
                for c in range(NC):
                    i = b * NC + c
                    ns = slice(c * TC, (c + 1) * TC)
                    sp.wait_ge(sem("padded_left"), i + 1)
                    sp.wait_ge(sem("padded_right"), i + 1)
                    sp.wait_ge(sem("padmid"), TC * (i + 1))
                    sp.dma_start(skew[b, ns].rearrange("n h p c -> p (n h) c"),
                                 pad[:, c].rearrange("p n h c -> p (n h) c")).then_inc(sem(f"skew_out{c}"), 16)
                for c in range(NC):
                    ns = slice(c * TC, (c + 1) * TC)
                    sp.wait_ge(sem(f"skew_out{c}"), 16 * (b + 1))
                    for g in range(2):
                        rows_, half = slice(HALF * g, HALF * g + HALF), bias[HALF * g:HALF * g + HALF, b, ns]
                        half = half.rearrange("p n h w -> p (n h) w")
                        sp.dma_start(half[:, :, HALF * g:HALF * g + 2 * HALF], skewed(skew, b, ns, g)
                                     ).then_inc(sem(f"biased{b}"), 16)
                        at = LPAD + NR if g == 0 else 0
                        sp.dma_start(half[:, :, 2 * HALF:WIN] if g == 0 else half[:, :, 0:HALF],
                                     skew[b, ns].rearrange("n h p c -> p (n h) c")[rows_, :, at:at + HALF]
                                     ).then_inc(sem(f"biased{b}"), 16)

            sp.wait_ge(sem("w2_zero"), 1)
            for e in range(2):
                load("ld_f", w2bd[E * e:E * e + E, :, E * e:E * e + E], a["w2"][e])
            for i, u in enumerate(EXPERT_UNITS):
                sp.wait_ge(sem("fin"), i + 1)
                sp.dma_start(a["out"][u // NC, (u % NC) * CT:(u % NC + 1) * CT, :].rearrange("(n p) e -> p n e", p=P),
                             fin[:, u * TC:(u + 1) * TC, :]).then_inc(sem("stored"), 16)
            sp.wait_ge(sem("stored"), 16 * 2 * B)

        @block.gpsimd
        def _(pool):
            def after(ins, name, n):
                ins.then_inc(sem(name), 1)
                pool.wait_ge(sem(name), n)

            after(nc.gpsimd.memset(xsh[V:V + NW, :], -1), "xsh_set", 1)
            after(nc.gpsimd.memset(xcol[:], 0.0), "xcol_set", 1)
            after(nc.gpsimd.memset(hfT[:, :, 0:KC - 1], 0.0), "pool_set", 1)
            after(nc.gpsimd.memset(hfT[:, :, KC - 2 + T:KC - 1 + T], 0.0), "pool_set", 2)
            after(nc.gpsimd.memset(carry[:, 0:1], 0.0), "pool_set", 3)
            pool.wait_ge(sem("idx"), 1)
            for n in range(B * NT):
                for k in range(NW):
                    pool.indirect_dma_start(emb[:, n, k, :], None, a["table"],
                                            bass.IndirectOffsetOnAxis(ap=idx[:, k, n:n + 1].bitcast(U32), axis=0)
                                            ).then_inc(sem(f"gathered{n // TC}"), 16)
            after(nc.gpsimd.memset(lnT[E:P, :], 0.0), "lnT_zero", 1)
            after(nc.gpsimd.memset(kst[NP6:P, :, :, :], 1.0), "st_set", 1)
            after(nc.gpsimd.memset(vt[:, :, :, :, HD:32], 0.0), "vt_zero", 1)
            after(nc.gpsimd.memset(vt[:, :, :, :, HD:HD + 1], 1.0), "st_set", 2)
            after(nc.gpsimd.memset(mx[:], -3.0e38), "st_set", 3)
            pool.wait_ge(sem("states"), NQ * B)
            nc.gpsimd.memset(w2bd, 0.0).then_inc(sem("w2_zero"), 1)

        @block.scalar
        def _(act):
            def af(out, in_, func, done, **kw):
                nc.scalar.activation(out, in_, func, **kw).then_inc(sem(done), 1)

            act.wait_ge(sem("ld_w"), 16 * 4)

            def weigh_windows(b, c):
                i = b * NC + c
                act.wait_ge(sem("sc_shift"), i + 1)
                af(sc[:].rearrange("p n k -> p (n k)"), sc[:].rearrange("p n k -> p (n k)"), ACT.Exp, "sc_exp",
                   scale=E ** -0.5)

            def hidden(b, c):
                i = b * NC + c
                act.wait_ge(sem("pe_hfT"), i + 1)
                if i == 0:
                    act.wait_ge(sem("pool_set"), 3)
                for half in range(2):
                    at = KC - 1 - half + c * CT
                    af(hfT[E * half:E * half + E, b, at:at + CT], bank[1][E * half:E * half + E, :], ACT.Copy, "hfT")
                act.wait_ge(sem("pe_conv"), i + 1)
                if i:
                    act.wait_ge(sem("pe_h0"), i)
                af(cf[:], bank[1][0:E, :], ACT.Silu, "cf", bias=col("conv_b", 0, E))
                act.wait_ge(sem("pe_h0"), i + 1)
                af(hT[:, i * CT:(i + 1) * CT], bank[3], ACT.Silu, "h0", bias=col("b_in"))

            def tail(b, k):
                if k == 0:
                    act.wait_ge(sem("pe_gd"), b + 1)
                    if b:
                        act.wait_ge(sem("ends"), b)
                    af(th, bank[tail_bank(b, k)][:, 0:QT], ACT.Tanh, "th", bias=bgh[:], scale=0.5)
                elif k == 4:
                    for c in range(NC):
                        i = b * NC + c
                        act.wait_ge(sem("pe_xnT"), i + 1)
                        af(hT[:, i * CT:(i + 1) * CT], bank[tail_bank(b, k) + c], ACT.Identity, "hn", scale=col("ln_g"),
                           bias=col("ln_b"))
                elif 5 <= k < 5 + NL:
                    l = k - 5
                    if b and not l:
                        act.wait_ge(sem("parts"), 3 * b)
                    for c in range(NC):
                        i = (b * NL + l) * NC + c
                        act.wait_ge(sem("pe_mlp"), i + 1)
                        if i >= NC:
                            act.wait_ge(sem("mlp_add"), i - 1)
                        af(act_s[:, c, :], bank[tail_bank(b, k) + 2 - 2 * (l % 2) + c], ACT.Silu, "mlp_silu", bias=col("mlp_b", l))

            def square(i):
                act.wait_ge(sem("centered"), i + 1)
                af(lb.rearrange("p n e -> p (n e)"), la.rearrange("p n e -> p (n e)"), ACT.Square, "squared")

            def setup(b, k):
                if k == 0:
                    square(b)
                    for c in range(NC):
                        i = b * NC + c
                        act.wait_ge(sem("pe_lnT"), i + 1)
                        af(lnT[0:E, i * CT:(i + 1) * CT], bank[6 + c][0:E, :], ACT.Identity, "lnT",
                           scale=col("gamma", 0, E), bias=col("beta", 0, E))
                elif k == 1:
                    for c in range(NC):
                        act.wait_ge(sem("pe_qk"), b * NC + c + 1)
                        af(qk32[:, c * CT:(c + 1) * CT], bank[4 + c], ACT.Identity, "qk32", scale=qsc[:], bias=qbi[:])
                    if b:
                        act.wait_ge(sem("pe_pos"), b * NT)
                    for c in range(NC):
                        af(qv[0:E, c * CT:(c + 1) * CT], bank[4 + c][0:E, :], ACT.Identity, "qv", scale=0.25, bias=vbi[:])
                else:
                    c = k - 2
                    if b:
                        act.wait_ge(sem(f"skew_out{c}"), 16 * b)
                    for n in range(c * TC, (c + 1) * TC):
                        act.wait_ge(sem("pe_pos"), b * NT + n + 1)
                        af(pad[:, c, n % TC, :, LPAD:LPAD + NR],
                           bank[4 + n % 2][:, 0:NH * NR].rearrange("p (h r) -> p h r", h=NH), ACT.Copy, "padmid")
                    act.wait_ge(sem("padmid"), b * NT + (c + 1) * TC)
                    af(*padding(c, LPAD + NR, PW, LPAD + NR - 1), ACT.Copy, "padded_right")

            def exps(u, i):
                for e in (u * NT * NH + i, u * NT * NH + i + 1):
                    act.wait_ge(sem("pe_s"), e + 1)
                    if e >= RING:
                        act.wait_ge(sem("pe_pv"), (e - RING) // NH + 1)
                    af(prob[:, e % RING, :], bank[4 + e % 3], ACT.Exp, "exp")

            def finish(u, k):
                if k == 0:
                    act.wait_ge(sem("pe_pv"), NT * (u + 1))
                    af(ctxs, bank[7], ACT.Copy, "ctxs")
                elif k == 2:
                    act.wait_ge(sem("pe_ctxnT"), u + 1)
                    af(ctxT, bank[7][0:E, :], ACT.Copy, "ctxT")

            def route(c, k):
                if k == 0:
                    square(B + c)
                    for b in range(B):
                        act.wait_ge(sem("pe_lnT"), (B + c) * 2 + b + 1)
                        u = b * NC + c
                        af(lnT[0:E, u * CT:(u + 1) * CT], bank[b][0:E, :], ACT.Copy, "lnT")
                elif k == 1:
                    act.wait_ge(sem("rw_shift"), c + 1)
                    af(rwf, rwf, ACT.Exp, "rw_exp")
                elif k == 2:
                    act.wait_ge(sem("pe_wT"), c + 1)
                    af(wT[0:NE, c * CT:(c + 1) * CT], bank[3][0:NE, :], ACT.Copy, "wT")
                elif k == 3:
                    for p in range(NPAIR):
                        act.wait_ge(sem("pe_wbc"), c * NPAIR + p + 1)
                        if c and not p:
                            act.wait_ge(sem("f3"), B * NPAIR * c)
                        af(wbc[:, p, :], bank[p % 2], ACT.Copy, "wbc")

            def first_activation(g):
                p = g % NPAIR
                act.wait_ge(sem("pe_f1"), g + 1)
                if g >= 2:
                    act.wait_ge(sem("pe_f2"), g - 1)
                af(f1[:, g % 2, :], bank[g % 2], ACT.Relu, "f1", scale=fsc[:, 0, p:p + 1], bias=fbi[:, 0, p:p + 1])

            def pair_step(g):
                act.wait_ge(sem("fcols"), 1)
                p = g % NPAIR
                if g % (B * NPAIR) == 0:
                    first_activation(g)
                if (g + 1) % (B * NPAIR):
                    first_activation(g + 1)
                act.wait_ge(sem("pe_f2"), g + 1)
                if g >= 2:
                    act.wait_ge(sem("f3"), g - 1)
                af(f2[:, g % 2, :], bank[f2_bank(g)], ACT.Relu, "f2", scale=fsc[:, 1, p:p + 1], bias=fbi[:, 1, p:p + 1])

            steps = {"weigh": weigh_windows, "hidden": hidden, "tail": tail, "setup": setup, "route": route}
            for what, *at in PROLOGUE:
                steps[what](*at)
            for s in range(UNITS + 1):
                if s == 1:
                    for c in range(NC):
                        act.wait_ge(sem(f"skew_out{c}"), 16 * B)
                for j in range(16):
                    if s:
                        exps(s - 1, 2 * j)
                    if s >= 2 and j == 2:
                        finish(s - 2, 2)
                    for what, *at in BESIDE.get((s, j), ()):
                        pair_step(*at) if what == "pair" else steps[what](*at)
                if s:
                    finish(s - 1, 0)
                if s < UNITS:
                    act.wait_ge(sem("pe_rows"), s + 1)
                    b, c = divmod(s, NC)
                    for h in range(NH):
                        af(qst[NP6:NP6 + 9, b, h, c * CT:(c + 1) * CT], bank[3][32 * h:32 * h + 9, :], ACT.Copy, "rows_in")
            finish(UNITS - 1, 2)
            for what, *at in EPILOGUE:
                pair_step(*at) if what == "pair" else steps[what](*at)

        @block.vector
        def _(dve):
            n_chain = [0]
            v = nc.vector

            def link(ins):
                n_chain[0] += 1
                ins.then_inc(sem("dve_chain"), 1)
                dve.wait_ge(sem("dve_chain"), n_chain[0])

            def rsqrt(x, n):
                y, t = rs[:, 0:n], rt[:, 0:n]
                link(v.tensor_scalar(t.bitcast(I32), x.bitcast(I32), 1, None, ALU.logical_shift_right))
                link(v.tensor_scalar(y.bitcast(I32), t.bitcast(I32), -1.0, float(0x5F3759DF), ALU.mult, ALU.add))
                for _ in range(3):
                    link(v.tensor_tensor(t, y, y, ALU.mult))
                    link(v.tensor_tensor(t, t, x, ALU.mult))
                    link(v.tensor_scalar(t, t, -0.5, 1.5, ALU.mult, ALU.add))
                    link(v.tensor_tensor(y, y, t, ALU.mult))

            dve.wait_ge(sem("ld_x"), 16)
            v.tensor_copy(xf[:], xi[:]).then_inc(sem("xf"), 1)
            dve.wait_ge(sem("pe_x"), 1)
            dve.wait_ge(sem("xcol_set"), 1)
            v.tensor_copy(xcol[:, :, 1:NT + 1], bank[0][:, 0:B * NT].rearrange("p (b n) -> p b n", b=B)
                          ).then_inc(sem("xcol"), 1)
            dve.wait_ge(sem("pe_hash"), 1)
            link(v.tensor_copy(hi32[:].rearrange("p k n -> p (k n)"), bank[1][:, 0:NW * B * NT]))
            for k in range(NW):
                last = v.tensor_scalar(idx[:, k, :], hi32[:, k, :], MOD - 1, k * MOD, ALU.bitwise_and, ALU.bitwise_or)
            last.then_inc(sem("idx"), 1)
            link(v.memset(states, 0.0))
            dve.wait_ge(sem("ld_oh"), 32)
            v.tensor_scalar(onehot[0:V, :], xrep[0:V, :], iota[0:V, :], None, ALU.is_equal).then_inc(sem("onehot"), 1)
            dve.wait_ge(sem("ld_sh"), 16 * 8)
            v.tensor_tensor(onehot[V:V + NW, :], xrep[V:V + NW, :], xsh[V:V + NW, :], ALU.is_equal
                            ).then_inc(sem("onehot"), 1)
            dve.wait_ge(sem("ld_w"), 16 * 4)
            dve.wait_ge(sem("pe_tab"), 1)
            v.tensor_copy(gtab[0:V, :], bank[2][0:V, 0:H]).then_inc(sem("tab"), 1)
            v.tensor_tensor(qtab[:], bank[2][0:V, H:H + E], row("bq")[0:V, :], ALU.add).then_inc(sem("tab"), 1)
            for half in range(2):
                r = slice(E * half, E * half + E)
                for j in range(KC // 2):
                    v.tensor_scalar(cdiag[r, j, :], ident[r, r], col("convw", j)[r, :], None, ALU.mult
                                    ).then_inc(sem("tab"), 1)
            for h in range(NH):
                v.tensor_scalar(posb[0:E, h, :], bank[2][0:E, 256:256 + NR], col("bpos", 0, E),
                                c64("heads")[:, h:h + 1], ALU.add, ALU.mult).then_inc(sem("tab"), 1)
            v.memset(posb[E:P], 0.0).then_inc(sem("tab"), 1)
            v.tensor_copy(identb[:], ident[:]).then_inc(sem("tab"), 1)
            v.tensor_scalar(nstart[:], c128("start"), -1.0, 1.0, ALU.mult, ALU.add).then_inc(sem("tab"), 1)
            v.tensor_scalar(bgh[:], col("bg"), 0.5, None, ALU.mult).then_inc(sem("tab"), 1)
            v.memset(qsc[0:E, :], 0.25).then_inc(sem("tab"), 1)
            v.memset(qsc[E:P, :], 1.0).then_inc(sem("tab"), 1)
            link(v.tensor_tensor(qbi[:], col("bqk"), col("u"), ALU.add))
            v.tensor_tensor(vbi[:], col("bqk", 0, E), col("v", 0, E), ALU.add).then_inc(sem("tabx"), 1)
            dve.wait_ge(sem("tabx"), 1)
            v.tensor_scalar(qbi[0:E, :], qbi[0:E, :], 0.25, None, ALU.mult).then_inc(sem("tab"), 1)
            v.tensor_scalar(vbi[:], vbi[:], 0.25, None, ALU.mult).then_inc(sem("tab"), 1)
            for l, name in enumerate(("f1", "f2")):
                o = SCOL[name][0]
                fb, fg, fbe, fm, fv = (cols[:, o + NPAIR * j:o + NPAIR * (j + 1)] for j in range(5))
                link(v.tensor_scalar(rv[:, 0:NPAIR], fv, EPS_BN, None, ALU.add))
                rsqrt(rv[:, 0:NPAIR], NPAIR)
                link(v.tensor_tensor(fsc[:, l, :], fg, rs[:, 0:NPAIR], ALU.mult))
                link(v.tensor_tensor(fbi[:, l, :], fb, fm, ALU.subtract))
                link(v.tensor_tensor(fbi[:, l, :], fbi[:, l, :], fsc[:, l, :], ALU.mult))
                link(v.tensor_tensor(fbi[:, l, :], fbi[:, l, :], fbe, ALU.add))
            dve.sem_inc(sem("fcols"), 1)

            def hidden(b, c):
                pass

            def weigh_windows(b, c):
                i = b * NC + c
                es = emb[:, i * TC:(i + 1) * TC]
                dve.wait_ge(sem("pe_q"), i + 1)
                if i:
                    dve.wait_ge(sem("hf"), i)
                dve.wait_ge(sem(f"gathered{i}"), 16 * NW * TC)
                link(v.tensor_tensor(prod[:], es, bank[i % 2 * 2][:, 0:TC * E].rearrange("p (n o e) -> p n o e", n=TC, o=1)
                                     .to_broadcast([P, TC, NW, E]), ALU.mult))
                link(v.tensor_reduce(sc[:], prod[:], AX.X, ALU.add))
                link(v.tensor_reduce(sm[:], sc[:], AX.X, ALU.max))
                over = sm[:].rearrange("p (n o) -> p n o", o=1).to_broadcast([P, TC, NW])
                v.tensor_tensor(sc[:], sc[:], over, ALU.subtract).then_inc(sem("sc_shift"), 1)
                dve.wait_ge(sem("sc_exp"), i + 1)
                link(v.tensor_reduce(sm[:], sc[:], AX.X, ALU.add))
                link(v.reciprocal(sm[:], sm[:]))
                link(v.tensor_tensor(sc[:], sc[:], over, ALU.mult))
                link(v.tensor_tensor(prod[:], es, sc[:].rearrange("p n (k o) -> p n k o", o=1)
                                     .to_broadcast([P, TC, NW, E]), ALU.mult))
                if i:
                    dve.wait_ge(sem("pe_hfT"), i)
                v.tensor_reduce(hf[:], prod[:].rearrange("p n k e -> p n e k"), AX.X, ALU.add).then_inc(sem("hf"), 1)

            def tail(b, k):
                if k == 0:
                    dve.wait_ge(sem("pe_gd"), b + 1)
                    hb = hT[:, b * T:(b + 1) * T]
                    v.tensor_scalar(hb, hb, col("bo"), None, ALU.add).then_inc(sem("h_bo"), 1)
                    dve.wait_ge(sem("th"), b + 1)
                    link(v.tensor_scalar(ga, th, -0.5, 0.5, ALU.mult, ALU.add))
                    link(v.scalar_tensor_tensor(gd, bank[tail_bank(b, k)][:, QT:2 * QT], col("bi"), ga, ALU.add, ALU.mult))
                    link(v.tensor_scalar(ga, th, 0.5, 0.5, ALU.mult, ALU.add))
                    link(v.tensor_scalar(ga, ga, 1e-6, None, ALU.max))
                    link(v.tensor_tensor(d1, ga, c128("start"), ALU.mult))
                    link(v.tensor_tensor(d0, ga, nstart[:], ALU.mult))
                    link(v.tensor_tensor_scan(cum, d0, d1, 0.0, ALU.mult, ALU.add))
                    link(v.tensor_scalar(d0, cum, 1e-8, None, ALU.max))
                    link(v.reciprocal(d0, d0))
                    link(v.tensor_tensor(d0, gd, d0, ALU.mult))
                    link(v.tensor_tensor_scan(cw[:], nstart[:], d0, 0.0, ALU.mult, ALU.add))
                    link(v.tensor_tensor(aw[:], cum, cw[:], ALU.mult))
                    v.tensor_copy(ends[:, 0, :], cum[:, SCH - 1::SCH])
                    v.tensor_copy(ends[:, 1, :], aw[:, SCH - 1::SCH]).then_inc(sem("ends"), 1)
                elif k == 1:
                    dve.wait_ge(sem("pe_ends"), b + 1)
                    if b:
                        dve.wait_ge(sem("pe_carry"), b)
                    link(v.tensor_copy(endsf[:].rearrange("p q a g -> p (q a g)"), bank[tail_bank(b, k) + 2][0:SS, 0:NQ * 2 * QG]))
                    for q in range(NQ):
                        link(v.tensor_tensor_scan(carry[:, 1 + q * QG:1 + (q + 1) * QG], endsf[:, q, 0, :],
                                                  endsf[:, q, 1, :], carry[:, q * QG:q * QG + 1], ALU.mult, ALU.add))
                    dve.sem_inc(sem("carry"), 1)
                elif k == 2:
                    dve.wait_ge(sem("pe_carry"), b + 1)
                    link(v.tensor_copy(carryq[:], bank[tail_bank(b, k) + 2][:, 128:128 + QG]))
                    link(v.tensor_tensor(cw[:].rearrange("p (g t) -> p g t", g=QG), cum.rearrange("p (g t) -> p g t", g=QG),
                                         carryq[:].rearrange("p (g o) -> p g o", o=1).to_broadcast([P, QG, SCH]),
                                         ALU.mult))
                    if b:
                        dve.wait_ge(sem("pe_y"), NC * b)
                    for q in range(NQ):
                        r = slice(SS * q, SS * q + SS)
                        v.tensor_tensor(states[r, q * QT:(q + 1) * QT], cw[r, :], aw[r, :], ALU.add
                                        ).then_inc(sem("states"), 1)
                elif k == 3:
                    for c in range(NC):
                        i = b * NC + c
                        dve.wait_ge(sem("pe_y"), i + 1)
                        y = bank[tail_bank(b, k) + 2 + c].rearrange("p (n f) -> p n f", n=TC)
                        for n in range(TC):
                            last = v.bn_stats(bnc[:, n, :], y[:, n, :])
                        link(last)
                        for n in range(TC):
                            last = v.bn_aggr(bns[:, n, :], bnc[:, n, :])
                        link(last)
                        link(v.tensor_scalar(rv[:, 0:TC], bns[:, :, 1], EPS_LN, None, ALU.add))
                        rsqrt(rv[:, 0:TC], TC)
                        if b:
                            dve.wait_ge(sem("pe_xnT"), NC * b)
                        for n in range(TC):
                            v.tensor_scalar(xn[:, c, n, :], y[:, n, :], bns[:, n, 0:1], rs[:, n:n + 1],
                                            ALU.subtract, ALU.mult).then_inc(sem("xn"), 1)
                elif 5 <= k < 5 + NL:
                    for c in range(NC):
                        i = (b * NL + k - 5) * NC + c
                        h = hT[:, (b * NC + c) * CT:(b * NC + c + 1) * CT]
                        dve.wait_ge(sem("mlp_silu"), i + 1)
                        dve.wait_ge(sem("pe_mlp"), i + 1)
                        v.tensor_tensor(h, h, act_s[:, c, :], ALU.add).then_inc(sem("mlp_add"), 1)
                elif k == 5 + NL:
                    dve.wait_ge(sem("pe_out"), b + 1)
                    v.tensor_tensor(htok[:, b * NT:(b + 1) * NT, :], bank[4].rearrange("p (n e) -> p n e", n=NT),
                                    row("bout", NT), ALU.add).then_inc(sem("htok"), 1)

            def norm(i, h, twice):
                if i:
                    dve.wait_ge(sem("pe_lnT"), NC * i)
                over = lambda x: x.rearrange("p (b n o) -> p b n o", b=2, o=1).to_broadcast([P, 2, TC, E])
                la4, lc2 = la.rearrange("p (b n) e -> p b n e", b=2), lc[:].rearrange("p (b n) -> p b n", b=2)
                link(v.tensor_reduce(lc2, h, AX.X, ALU.add))
                link(v.tensor_scalar(lc[:], lc[:], 1.0 / E, None, ALU.mult))
                v.tensor_tensor(la4, h, over(lc[:]), ALU.subtract).then_inc(sem("centered"), 1)
                dve.wait_ge(sem("squared"), i + 1)
                dve.wait_ge(sem("centered"), i + 1)
                link(v.tensor_reduce(lc[:], lb, AX.X, ALU.add))
                if twice:
                    link(v.tensor_scalar(rv[:, 0:NT], lc[:], (1.0 + EPS_LN) / E, EPS_LN + EPS_LN ** 2, ALU.mult, ALU.add))
                else:
                    link(v.tensor_scalar(rv[:, 0:NT], lc[:], 1.0 / E, EPS_LN, ALU.mult, ALU.add))
                rsqrt(rv[:, 0:NT], NT)
                v.tensor_tensor(la4, la4, over(rs[:, 0:NT]), ALU.mult).then_inc(sem("ln"), 1)

            def setup(b, k):
                if k == 0:
                    dve.wait_ge(sem("htok"), b + 1)
                    norm(b, htok[:, b * NT:(b + 1) * NT, :].rearrange("p (c n) e -> p c n e", c=NC), True)
                elif k == 1:
                    dve.wait_ge(sem("qk32"), NC * (b + 1))
                    if b:
                        dve.wait_ge(sem("stacked0"), 16 * 12)
                    v.tensor_copy(part[0][:], qk32).then_inc(sem("parts"), 1)
                    dve.wait_ge(sem("parts"), 3 * b + 1)
                    link(v.tensor_tensor(qk32, qk32, part[0][:], ALU.subtract))
                    v.tensor_copy(part[1][:], qk32).then_inc(sem("parts"), 1)
                    dve.wait_ge(sem("parts"), 3 * b + 2)
                    v.tensor_tensor(part[2][:], qk32, part[1][:], ALU.subtract).then_inc(sem("parts"), 1)
                    dve.wait_ge(sem("pe_v"), b + 1)
                    dve.wait_ge(sem("st_set"), 3)
                    v.tensor_tensor(vt[:, b, :, :, 0:HD], bank[6].rearrange("p (n h d) -> p n h d", n=NT, h=NH),
                                    rows[:, SROW["bv"][0]:SROW["bv"][1]].rearrange("p (o h d) -> p o h d", o=1, h=NH)
                                    .to_broadcast([P, NT, NH, HD]), ALU.add).then_inc(sem("vt"), 1)
                if k == 2:
                    dve.wait_ge(sem("pe_far"), b + 1)
                    v.tensor_copy(pend[:, b].rearrange("p n h f -> p (n h f)"), bank[7][:, 0:NT * NH * 2]
                                  ).then_inc(sem("far"), 1)
                if k >= 2:
                    c = k - 2
                    dve.wait_ge(sem("padmid"), b * NT + (c + 1) * TC)
                    v.tensor_copy(*padding(c, 0, LPAD, LPAD)).then_inc(sem("padded_left"), 1)

            def region_max(u, j):
                b, c = divmod(u, NC)
                h, n = j % NH, c * TC + j // NH
                i = 16 * u + j
                t0 = n * P
                lo, hi = max(0, t0 - EDGE), min(T, t0 - EDGE + WIN)
                dve.wait_ge(sem("pe_m"), i + 1)
                s1024 = ps[:, 2 * (i % 2):2 * (i % 2) + 2, :].rearrange("p a t -> p (a t)")
                if lo:
                    v.tensor_reduce(mx[:, b, n, h, 0:1], s1024[:, 0:lo], AX.X, ALU.max)
                if hi < T:
                    v.tensor_reduce(mx[:, b, n, h, 2:3], s1024[:, hi:T], AX.X, ALU.max)
                o = lo - (t0 - EDGE)
                if i >= 2:
                    dve.wait_ge(sem("mx"), i - 1)
                v.tensor_tensor_reduce(out=junk[:, i % 2, 0:hi - lo], in0=s1024[:, lo:hi],
                                       in1=bias[:, b, n, h, o:o + hi - lo], scale=1.0, scalar=-3.0e38,
                                       op0=ALU.add, op1=ALU.max, accum_out=mx[:, b, n, h, 1:2]).then_inc(sem("mx"), 1)

            def max_rows(u):
                b, c = divmod(u, NC)
                ns = slice(c * TC, (c + 1) * TC)
                far, m3 = pend[:, b, ns], mx[:, b, ns]
                dve.wait_ge(sem("mx"), 16 * (u + 1))
                if u:
                    dve.wait_ge(sem("pe_rows"), u)
                link(v.tensor_tensor(m3[:, :, :, 0], m3[:, :, :, 0], far[:, :, :, 0], ALU.add))
                link(v.tensor_tensor(m3[:, :, :, 2], m3[:, :, :, 2], far[:, :, :, 1], ALU.add))
                link(v.tensor_reduce(tv[:, 0], m3, AX.X, ALU.max, negate=True))
                link(v.tensor_copy(tv[:, 1], far[:, :, :, 0]))
                link(v.tensor_tensor(tv[:, 2], far[:, :, :, 1], far[:, :, :, 0], ALU.subtract))
                p3 = [tp[:, :, q].rearrange("p a n h -> p a (n h)") for q in range(3)]
                x, r = tv[:].rearrange("p a n h -> p a (n h)"), tr[:].rearrange("p a n h -> p a (n h)")
                link(v.tensor_copy(p3[0], x))
                link(v.tensor_tensor(r, x, p3[0], ALU.subtract))
                link(v.tensor_copy(p3[1], r))
                v.tensor_tensor(p3[2], r, p3[1], ALU.subtract).then_inc(sem("tp"), 1)

            def normalize(u):
                dve.wait_ge(sem("pe_ctx"), u + 1)
                t4 = bank[7].rearrange("p (n h d) -> p n h d", n=TC, h=NH)
                link(v.reciprocal(den[:], t4[:, :, :, HD]))
                for n in range(TC):
                    v.tensor_tensor(ctxn[:, n].rearrange("p (h d) -> p h d", h=NH), t4[:, n, :, 0:HD],
                                    den[:, n].rearrange("p (h o) -> p h o", o=1).to_broadcast([P, NH, HD]),
                                    ALU.mult).then_inc(sem("ctxn"), 1)

            def residual(u):
                h = htok[:, u * TC:(u + 1) * TC, :]
                link(v.tensor_tensor(h, h, row("ao_b", TC), ALU.add))
                dve.wait_ge(sem("pe_ao"), u + 1)
                v.tensor_tensor(h, h, bank[7][:, 0:TC * E].rearrange("p (n e) -> p n e", n=TC), ALU.add
                                ).then_inc(sem("htok"), 1)

            def route(c, k):
                if k == 0:
                    dve.wait_ge(sem("htok"), B + (B - 1) * NC + c + 1)
                    norm(B + c, htok[:].rearrange("p (b m) e -> p b m e", b=B)[:, :, c * TC:(c + 1) * TC, :], False)
                elif k == 1:
                    dve.wait_ge(sem("pe_r"), c + 1)
                    over = rwm[:].rearrange("p (n o) -> p n o", o=1).to_broadcast([P, TC, NE])
                    if c:
                        dve.wait_ge(sem("pe_wT"), c)
                    link(v.tensor_scalar(rwf, bank[2][:, 0:TC * NE], 0.5, None, ALU.mult))
                    link(v.tensor_tensor(rw, rw, row("br", TC), ALU.add))
                    link(v.tensor_reduce(rwm[:], rw, AX.X, ALU.max))
                    v.tensor_tensor(rw, rw, over, ALU.subtract).then_inc(sem("rw_shift"), 1)
                    dve.wait_ge(sem("rw_exp"), c + 1)
                    link(v.tensor_reduce(rwm[:], rw, AX.X, ALU.add))
                    link(v.reciprocal(rwm[:], rwm[:]))
                    v.tensor_tensor(rw, rw, over, ALU.mult).then_inc(sem("rw"), 1)

            def combine(e):
                u = EXPERT_UNITS[e]
                dve.wait_ge(sem("pe_f3"), e + 1)
                v.tensor_tensor(fin[:, u * TC:(u + 1) * TC, :], htok[:, u * TC:(u + 1) * TC, :],
                                bank[3][:, 0:TC * E].rearrange("p (n e) -> p n e", n=TC), ALU.add
                                ).then_inc(sem("fin"), 1)

            def pair_step(g):
                e, p = divmod(g, NPAIR)
                dve.wait_ge(sem("wbc"), NPAIR * (e // B) + p + 1)
                dve.wait_ge(sem("f2"), g + 1)
                if e % B and not p:
                    combine(e - 1)
                v.tensor_tensor(f3[:, p, :], f2[:, g % 2, :], wbc[:, p, :], ALU.mult).then_inc(sem("f3"), 1)
                if g % (B * NPAIR) == B * NPAIR - 1:
                    combine(e)

            steps = {"weigh": weigh_windows, "hidden": hidden, "tail": tail, "setup": setup, "route": route}
            for what, *at in PROLOGUE:
                steps[what](*at)
            for s in range(UNITS + 1):
                if s < UNITS and s % NC == 0:
                    b = s // NC
                    dve.wait_ge(sem(f"biased{b}"), 16 * 4 * NC)
                    dve.wait_ge(sem("far"), b + 1)
                for j in range(16):
                    if s < UNITS:
                        region_max(s, j)
                    if s >= 2 and j == 1:
                        normalize(s - 2)
                    if s >= 2 and j == 4:
                        residual(s - 2)
                    for what, *at in BESIDE.get((s, j), ()):
                        pair_step(*at) if what == "pair" else steps[what](*at)
                if s < UNITS:
                    max_rows(s)
            normalize(UNITS - 1)
            residual(UNITS - 1)
            for what, *at in EPILOGUE:
                pair_step(*at) if what == "pair" else steps[what](*at)

        @block.tensor
        def _(pe):
            mm = nc.tensor.matmul

            def tr_(out, in_, n=P):
                return nc.tensor.transpose(out, in_, ident[0:n, 0:n])

            pe.wait_ge(sem("ld_ident"), 16)
            pe.wait_ge(sem("xf"), 1)
            tr_(bank[0][:, 0:B * NT], xf[:], B * NT).then_inc(sem("pe_x"), 1)
            pe.wait_ge(sem("ld_band"), 16)
            pe.wait_ge(sem("xcol"), 1)
            for k in range(NW):
                o = bank[1][:, k * B * NT:(k + 1) * B * NT].rearrange("p (b n) -> p b n", b=B)
                mm(o, band[:, 0, k, :], xcol[:, :, 1:NT + 1], start=True, stop=False)
                last = mm(o, band[:, 1, k, :], xcol[:, :, 0:NT], start=False, stop=True)
            last.then_inc(sem("pe_hash"), 1)
            pe.wait_ge(sem("ld_emb"), 32)
            mm(bank[2][0:V, 0:H + E], emb3[:, 0:V], emb3[:, V:V + H + E], start=True, stop=True)
            pe.wait_ge(sem("ld_w"), 16 * 4)
            mm(bank[2][0:E, 256:256 + NR], c64("wpos"), c64("encT"), start=True, stop=True).then_inc(sem("pe_tab"), 1)
            pe.wait_ge(sem("tab"), 18)
            pe.wait_ge(sem("onehot"), 2)

            def weigh_windows(b, c):
                i = b * NC + c
                for q in ((0, 1) if i == 0 else (i + 1,) if i + 1 < B * NC else ()):
                    if q >= 2:
                        pe.wait_ge(sem("sc_shift"), q - 1)
                    for n in range(TC):
                        t0 = (q * TC + n) * P
                        last = mm(bank[q % 2 * 2][:, n * E:(n + 1) * E], onehot[0:V, t0:t0 + P], qtab[:], start=True, stop=True)
                    last.then_inc(sem("pe_q"), 1)

            def hidden(b, c):
                i = b * NC + c
                if i:
                    pe.wait_ge(sem("h0"), i)
                mm(bank[3], gtab[:], onehot[:, i * CT:(i + 1) * CT], start=True, stop=False)
                pe.wait_ge(sem("hf"), i + 1)
                for n in range(TC):
                    for half in range(2):
                        last = mm(bank[1][E * half:E * half + E, n * P:(n + 1) * P], hf[:, n, :], ident[:],
                                  start=True, stop=True)
                last.then_inc(sem("pe_hfT"), 1)
                pe.wait_ge(sem("hfT"), 2 * (i + 1))
                for j in range(KC // 2):
                    last = mm(bank[1][0:E, :], cdiag[:, j, :], hfT[:, b, c * CT + 2 * j:c * CT + 2 * j + CT],
                              start=(j == 0), stop=(j == KC // 2 - 1))
                last.then_inc(sem("pe_conv"), 1)
                pe.wait_ge(sem("cf"), i + 1)
                mm(bank[3], c64("winh"), cf[:], start=False, stop=True).then_inc(sem("pe_h0"), 1)

            def tail(b, k):
                if k == 0:
                    pe.wait_ge(sem("h0"), NC * (b + 1))
                    if b:
                        pe.wait_ge(sem("sc_shift"), NC * B)
                    for o, w in ((0, "wg"), (QT, "wi")):
                        for q in range(NQ):
                            last = mm(bank[tail_bank(b, k)][SS * q:SS * q + SS, o:o + QT], c128(w),
                                      hT[:, b * T + q * QT:b * T + (q + 1) * QT], start=True, stop=True)
                    last.then_inc(sem("pe_gd"), 1)
                elif k == 1:
                    pe.wait_ge(sem("ends"), b + 1)
                    for q in range(NQ):
                        last = mm(bank[tail_bank(b, k) + 2][0:SS, q * 2 * QG:(q + 1) * 2 * QG], ident[:, SS * q:SS * q + SS],
                                  ends[:].rearrange("p a g -> p (a g)"), start=True, stop=True)
                    last.then_inc(sem("pe_ends"), 1)
                elif k == 2:
                    pe.wait_ge(sem("carry"), b + 1)
                    for q in range(NQ):
                        last = mm(bank[tail_bank(b, k) + 2][SS * q:SS * q + SS, 128:128 + QG], ident[0:SS, 0:SS],
                                  carry[:, q * QG:(q + 1) * QG], start=True, stop=True)
                    last.then_inc(sem("pe_carry"), 1)
                elif k == 3:
                    pe.wait_ge(sem("h_bo"), b + 1)
                    pe.wait_ge(sem("states"), NQ * (b + 1))
                    for c in range(NC):
                        for n in range(TC):
                            t0 = c * CT + n * P
                            o = bank[tail_bank(b, k) + 2 + c][:, n * H:(n + 1) * H]
                            mm(o, hT[:, b * T + t0:b * T + t0 + P], ident[:], start=True, stop=False)
                            last = mm(o, states[:, t0:t0 + P], c128("wo4"), start=False, stop=True)
                        last.then_inc(sem("pe_y"), 1)
                elif k == 4:
                    for c in range(NC):
                        i = b * NC + c
                        pe.wait_ge(sem("xn"), TC * (i + 1))
                        for n in range(TC):
                            last = tr_(bank[tail_bank(b, k) + c][:, n * P:(n + 1) * P], xn[:, c, n, :])
                        last.then_inc(sem("pe_xnT"), 1)
                elif k < 5 + NL:
                    l = k - 5
                    if b and l == 1:
                        pe.wait_ge(sem("padmid"), NT)
                    if b and l == 2:
                        pe.wait_ge(sem("vt"), 1)
                        pe.wait_ge(sem("far"), 1)
                    for c in range(NC):
                        i = b * NC + c
                        if l:
                            pe.wait_ge(sem("mlp_add"), (b * NL + l - 1) * NC + c + 1)
                        else:
                            pe.wait_ge(sem("hn"), i + 1)
                        mm(bank[tail_bank(b, k) + 2 - 2 * (l % 2) + c], c128("mlp")[:, l * H:(l + 1) * H], hT[:, i * CT:(i + 1) * CT],
                           start=True, stop=True).then_inc(sem("pe_mlp"), 1)
                else:
                    pe.wait_ge(sem("mlp_add"), NL * NC * (b + 1))
                    for n in range(NT):
                        last = mm(bank[4][:, n * E:(n + 1) * E], hT[:, b * T + n * P:b * T + (n + 1) * P], c128("wout"),
                                  start=True, stop=True)
                    last.then_inc(sem("pe_out"), 1)

            def ln_transposes(i, first):
                pe.wait_ge(sem("ln"), i + 1)
                for c in range(2):
                    for n in range(TC):
                        last = tr_(bank[first + c][0:E, n * P:(n + 1) * P], la[:, c * TC + n, :])
                    last.then_inc(sem("pe_lnT"), 1)

            def setup(b, k):
                if k == 0:
                    ln_transposes(b, 6)
                elif k == 1:
                    pe.wait_ge(sem("lnT_zero"), 1)
                    for c in range(NC):
                        i = b * NC + c
                        pe.wait_ge(sem("lnT"), i + 1)
                        mm(bank[4 + c], c64("aqk", P), lnT[:, i * CT:(i + 1) * CT], start=True, stop=True
                           ).then_inc(sem("pe_qk"), 1)
                    for n in range(NT):
                        last = mm(bank[6][:, n * E:(n + 1) * E], lnT[:, b * T + n * P:b * T + (n + 1) * P], c64("av", P),
                                  start=True, stop=True)
                    last.then_inc(sem("pe_v"), 1)
                else:
                    c = k - 2
                    if not c:
                        pe.wait_ge(sem("qv"), NC * (b + 1))
                        for n in range(NT):
                            last = mm(bank[7][:, n * 2 * NH:(n + 1) * 2 * NH], qv[:, n * P:(n + 1) * P],
                                      posb[:, :, 0::NR - 1], start=True, stop=True)
                        last.then_inc(sem("pe_far"), 1)
                    for n in range(c * TC, (c + 1) * TC):
                        if n >= 2:
                            pe.wait_ge(sem("padmid"), b * NT + n - 1)
                        mm(bank[4 + n % 2][:, 0:NH * NR], qv[:, n * P:(n + 1) * P],
                           posb[:].rearrange("e h r -> e (h r)"), start=True, stop=True).then_inc(sem("pe_pos"), 1)

            def max_scores(u, j):
                b, c = divmod(u, NC)
                h, n = j % NH, c * TC + j // NH
                i = 16 * u + j
                if i >= 2:
                    pe.wait_ge(sem("mx"), i - 1)
                if u and j == 1:
                    pe.wait_ge(sem("rows_in"), NH * u)
                for a_ in range(2):
                    last = mm(bank[2 * (i % 2) + a_], qst[0:NP6, b, h, n * P:(n + 1) * P],
                              kst[0:NP6, b, h, a_ * 512:(a_ + 1) * 512], start=True, stop=True)
                last.then_inc(sem("pe_m"), 1)

            def key_scores(u, i):
                b, c = divmod(u, NC)
                k, h = divmod(i, NH)
                e = u * NT * NH + i
                if e >= 3:
                    pe.wait_ge(sem("exp"), e - 2)
                o = bank[4 + e % 3]
                t0 = c * CT
                left, right = min(max(k * P, t0), t0 + CT), min(max((k + 1) * P, t0), t0 + CT)

                def product(rows_, s0, s1, q0, q1, at, stop):
                    return mm(o[at:at + s1 - s0, q0 - t0:q1 - t0], kst[0:rows_, b, h, s0:s1], qst[0:rows_, b, h, q0:q1],
                              start=True, stop=stop)

                def position(j0, j1, n, at):
                    return mm(o[at:at + j1 - j0, n * P - t0:(n + 1) * P - t0], bias[:, b, n, h, j0:j1], ident[:],
                              start=False, stop=True)

                if left > t0:
                    last = product(NP6 + 9, k * P, (k + 1) * P, t0, left, 0, True)
                if right < t0 + CT:
                    last = product(NP6 + 6, k * P, (k + 1) * P, right, t0 + CT, 0, True)
                before, after = t0 <= (k - 1) * P < t0 + CT, t0 <= (k + 1) * P < t0 + CT
                if left < right:
                    product(NP6 + 3, k * P, (k + 1) * P, left, right, 0, False)
                    last = position(EDGE, EDGE + P, k, 0)
                if before:
                    product(NP6 + 3, k * P, k * P + EDGE, (k - 1) * P, k * P, 0, False)
                if after:
                    product(NP6 + 3, (k + 1) * P - EDGE, (k + 1) * P, (k + 1) * P, (k + 2) * P, P - EDGE, False)
                if before:
                    last = position(EDGE + P, WIN, k - 1, 0)
                if after:
                    last = position(0, EDGE, k + 1, P - EDGE)
                last.then_inc(sem("pe_s"), 1)

            def weigh(u, k):
                b = u // NC
                pe.wait_ge(sem("exp"), (u * NT + k + 1) * NH)
                if u and k == 0:
                    pe.wait_ge(sem("htok"), B + u)
                for h in range(NH):
                    last = mm(bank[7][32 * h:32 * h + 32, :], vt[:, b, k, h, :], prob[:, ((u * NT + k) * NH + h) % RING, :],
                              start=(k == 0), stop=(k == NT - 1))
                last.then_inc(sem("pe_pv"), 1)

            def finish(u, step):
                if step == 0:
                    pe.wait_ge(sem("ctxs"), u + 1)
                    for n in range(TC):
                        last = tr_(bank[7][:, n * P:(n + 1) * P], ctxs[:, n * P:(n + 1) * P])
                    last.then_inc(sem("pe_ctx"), 1)
                elif step == 1:
                    pe.wait_ge(sem("ctxn"), TC * (u + 1))
                    for n in range(TC):
                        last = tr_(bank[7][0:E, n * P:(n + 1) * P], ctxn[:, n, :])
                    last.then_inc(sem("pe_ctxnT"), 1)
                else:
                    pe.wait_ge(sem("ctxT"), u + 1)
                    for n in range(TC):
                        last = mm(bank[7][:, n * E:(n + 1) * E], ctxT[:, n * P:(n + 1) * P], c64("ao"),
                                  start=True, stop=True)
                    last.then_inc(sem("pe_ao"), 1)

            def route(c, k):
                if k == 0:
                    if c:
                        pe.wait_ge(sem("f1"), B * NPAIR * c)
                    ln_transposes(B + c, 0)
                elif k == 1:
                    pe.wait_ge(sem("lnT"), 2 * (B + c + 1))
                    if c:
                        pe.wait_ge(sem("f2"), B * NPAIR * c)
                    for n in range(TC):
                        o, t0 = bank[2][:, n * NE:(n + 1) * NE], c * CT + n * P
                        mm(o, lnT[:, t0:t0 + P], c64("wr", P), start=True, stop=False)
                        last = mm(o, lnT[:, T + t0:T + t0 + P], c64("wr", P), start=False, stop=True)
                    last.then_inc(sem("pe_r"), 1)
                elif k == 2:
                    pe.wait_ge(sem("rw"), c + 1)
                    if c:
                        pe.wait_ge(sem("fin"), B * c)
                    for n in range(TC):
                        last = tr_(bank[3][0:NE, n * P:(n + 1) * P], rw[:, n, :])
                    last.then_inc(sem("pe_wT"), 1)
                else:
                    pe.wait_ge(sem("wT"), c + 1)
                    pe.wait_ge(sem("ld_f"), 16 * 4)
                    for p in range(NPAIR):
                        if p >= 2:
                            pe.wait_ge(sem("wbc"), NPAIR * c + p - 1)
                        mm(bank[p % 2], pair[:, p, :], wT[:, c * CT:(c + 1) * CT], start=True, stop=True
                           ).then_inc(sem("pe_wbc"), 1)
                    pe.wait_ge(sem("wbc"), NPAIR * (c + 1))

            def first_layer(g):
                u, p = EXPERT_UNITS[g // NPAIR], g % NPAIR
                if g >= 2:
                    pe.wait_ge(sem("f1"), g - 1)
                mm(bank[g % 2], c64("w1", P)[:, p * P:(p + 1) * P], lnT[:, u * CT:(u + 1) * CT],
                   start=True, stop=True).then_inc(sem("pe_f1"), 1)

            def third_layer(e):
                t0 = EXPERT_UNITS[e] % NC * CT
                pe.wait_ge(sem("f3"), NPAIR * (e + 1))
                if e:
                    pe.wait_ge(sem("fin"), e)
                for n in range(TC):
                    o = bank[3][:, n * E:(n + 1) * E]
                    mm(o, wT[0:NE, t0 + n * P:t0 + (n + 1) * P], bo8[:], start=True, stop=False)
                    for p in range(NPAIR):
                        last = mm(o, f3[:, p, n * P:(n + 1) * P], c128("fwo")[:, p * E:(p + 1) * E],
                                  start=False, stop=(p == NPAIR - 1))
                last.then_inc(sem("pe_f3"), 1)

            def pair_step(g):
                e, p = divmod(g, NPAIR)
                if g % (B * NPAIR) == 0:
                    first_layer(g)
                if (g + 1) % (B * NPAIR):
                    first_layer(g + 1)
                pe.wait_ge(sem("f1"), g + 1)
                if g:
                    pe.wait_ge(sem("f2"), g)
                mm(bank[f2_bank(g)], w2bd[:, p, :], f1[:, g % 2, :], start=True, stop=True).then_inc(sem("pe_f2"), 1)
                if e % B and not p:
                    third_layer(e - 1)
                if g % (B * NPAIR) == B * NPAIR - 1:
                    third_layer(e)

            steps = {"weigh": weigh_windows, "hidden": hidden, "tail": tail, "setup": setup, "route": route}
            for what, *at in PROLOGUE:
                steps[what](*at)
            for s in range(UNITS + 1):
                if s < UNITS and s % NC == 0:
                    b = s // NC
                    pe.wait_ge(sem(f"stacked{b}"), 16 * 12)
                    pe.wait_ge(sem("st_set"), 3)
                if s == 0:
                    pe.wait_ge(sem("mlp_silu"), NC * (NL + 1))
                    max_scores(0, 0)
                if s == 1:
                    pe.wait_ge(sem("vt"), B)
                    pe.wait_ge(sem("far"), B)
                    pe.wait_ge(sem("padmid"), B * NT)
                if s and (s - 1) % NC == 0:
                    pe.wait_ge(sem(f"biased{(s - 1) // NC}"), 16 * 4 * NC)
                for j in range(16):
                    if s < UNITS and (s or j < 15):
                        max_scores(s, j + (s == 0))
                    if s:
                        if j == 0:
                            pe.wait_ge(sem("rows_in"), NH * s)
                        key_scores(s - 1, 2 * j)
                        key_scores(s - 1, 2 * j + 1)
                    if s >= 2 and j in (0, 2, 4):
                        finish(s - 2, j // 2)
                    if s and j >= 5 and j % 2 == 1:
                        weigh(s - 1, (j - 5) // 2)
                    for what, *at in BESIDE.get((s, j), ()):
                        pair_step(*at) if what == "pair" else steps[what](*at)
                if s:
                    for k in range(6, NT):
                        weigh(s - 1, k)
                if s < UNITS:
                    pe.wait_ge(sem("tp"), s + 1)
                    for h in range(NH):
                        for n in range(TC):
                            last = mm(bank[3][32 * h:32 * h + 9, n * P:(n + 1) * P],
                                      tp[:, :, :, n, h].rearrange("p a q -> p (a q)"), identb[:], start=True, stop=True)
                    last.then_inc(sem("pe_rows"), 1)
            for k in range(3):
                finish(UNITS - 1, k)
            for what, *at in EPILOGUE:
                pair_step(*at) if what == "pair" else steps[what](*at)


def skewed(skew, b, ns, g):
    flat = skew[b, ns].rearrange("n h p c -> (n h) (p c)")
    at = HALF * g * PW + LPAD - 2
    return flat[:, at:at + HALF * (PW - 1)].rearrange("m (i c) -> i m c", c=PW - 1)[:, :, 0:2 * HALF]


def layout(inputs):
    w = {k: np.asarray(v) for k, v in inputs.items()}
    t = lambda n: w["L0_tok_" + n]
    a = lambda n: w["L0_attn_" + n]
    f = lambda n: w["L0_ffn_" + n]
    k = constants()
    tall = lambda x, n=P: np.concatenate([x, np.zeros((n - x.shape[0], x.shape[1]), np.float32)])
    pairs = lambda x: x.reshape(NPAIR, 2 * E).T
    v1 = lambda x: x.reshape(-1, 1)
    w128 = {
        "mlp": t("mlp_w").transpose(1, 0, 2).reshape(H, NL * H), "wg": t("Wg"), "wi": t("Wi"), "wout": t("Wout"),
        "wo4": np.tile(t("Wo"), (NQ, 1)),
        "fwo": f("Wo").reshape(NPAIR, 2 * E, E).transpose(1, 0, 2).reshape(P, NPAIR * E), "start": k["start"],
    }
    w64 = {
        "winh": t("Win")[E:2 * E], "aqk": np.concatenate([a("Wq").T, a("Wk").T], 1), "av": a("Wv").T,
        "wpos": a("Wpos").T, "encT": k["encT"], "ao": a("Wo").T, "wr": f("Wr"),
        "w1": f("W1").transpose(1, 0, 2).reshape(E, NE * E), "heads": k["heads"],
    }
    cols = {
        "b_in": v1(t("b_in")), "ln_g": v1(t("ln_g")), "ln_b": v1(t("ln_b")), "mlp_b": t("mlp_b").T,
        "bg": np.tile(v1(t("bg")), (NQ, 1)), "bi": np.tile(v1(t("bi")), (NQ, 1)), "conv_b": tall(v1(t("conv_b"))),
        "gamma": tall(v1(a("ln_gamma"))), "beta": tall(v1(a("ln_beta"))),
        "bqk": np.concatenate([v1(a("bq")), v1(a("bk"))]), "u": tall(v1(a("u_bias"))), "v": tall(v1(a("v_bias"))),
        "bpos": tall(v1(a("bpos"))), "bo": v1(t("bo")),
        "convw": t("conv_w")[:, 0, :].reshape(E, KC // 2, 2).transpose(2, 0, 1).reshape(P, KC // 2),
        "f1": np.concatenate([pairs(f(n)) for n in ("b1", "g1", "be1", "m1", "v1")], 1),
        "f2": np.concatenate([pairs(f(n)) for n in ("b2", "g2", "be2", "m2", "v2")], 1),
    }
    rows = {"bq": t("bq"), "bout": t("bout"), "bv": a("bv"), "ao_b": a("bo"), "br": f("br")}
    side = lambda pack, d: np.concatenate([d[n] for n, _ in pack], 1)
    return {
        "x": w["x"], "ident": k["ident"], "band": k["band"], "iota": k["iota"], "pair": tall(k["pair"]),
        "emb3": np.concatenate([t("emb_byte").T, t("Win")[0:E], t("Wq")], 1), "winm": t("Win")[2 * E:],
        "w128": side(PACK128, w128), "w64": tall(side(PACK64, w64)), "cols": side(COLS, cols),
        "rows": np.concatenate([rows[n] for n, _ in ROWS])[None, :], "bo8": f("bo"),
        "w2": f("W2").reshape(NPAIR, 2, E, E).transpose(1, 2, 0, 3), "table": t("hash_tables").reshape(NW * MOD, E),
    }


def kernel(**inputs):
    import concourse.bacc as bacc
    from concourse.bass_utils import run_bass_kernel_spmd

    nc = bacc.Bacc("TRN2", target_bir_lowering=False, num_devices=1)
    arrays = {k: np.ascontiguousarray(v) for k, v in layout(inputs).items()}
    tensors = {k: nc.dram_tensor("in_" + k, v.shape, mybir.dt.from_np(v.dtype), kind="ExternalInput").ap()
               for k, v in arrays.items()}
    tensors["out"] = nc.dram_tensor("result", (B, T, E), F32, kind="ExternalOutput").ap()
    tensors["skew"] = nc.dram_tensor("skewed", (B, NT, NH, P, PW), F32).ap()
    tensors["parts"] = nc.dram_tensor("query_key_parts", (B, 3, 2, NH, HD, T), BF16).ap()
    tower(nc, tensors)
    return run_bass_kernel_spmd(nc, [{"in_" + k: v for k, v in arrays.items()}], core_ids=[0]).results[0]["result"]
```

```python
from contextlib import ExitStack

import numpy as np

import concourse.bass as bass
from concourse import mybir

F32 = mybir.dt.float32
BF16 = mybir.dt.bfloat16
I32 = mybir.dt.int32
U32 = mybir.dt.uint32
ALU = mybir.AluOpType
ACT = mybir.ActivationFunctionType
AX = mybir.AxisListType

P = 128
B, T = 2, 1024
NT = T // P
NC = 2
CT = T // NC
TC = CT // P
V = 64
E = 64
H = 128
SS = 32
NW = 4
WINDOWS = (2, 4, 8, 16)
OFFSETS = (1, 2, 4, 8)
BASE, MOD = 257, 1024
KC = 4
SCH = 32
NQ = 4
QT = T // NQ
QG = QT // SCH
NL = 3
NH, HD = 4, 16
REL = 30
NR = 2 * REL + 1
HALF = 64
LPAD = HALF + 1
PW = 192
WIN = 192
EDGE = 32
NP6 = 96
NE, NPAIR = 8, 4
EPS_LN, EPS_BN = 1e-5, 1e-3
RING = 12
EXPERT_UNITS = tuple(b * NC + c for c in range(NC) for b in range(B))
LAG = 3
QKG = ((0, 0), (0, 1), (1, 0), (0, 2), (2, 0), (1, 1))


UNITS = B * NC
STEPS = 16
EARLY = 4
LAST = UNITS * NPAIR
NORMS = ((0, 1), (2,), (3,))
PROLOGUE = (
    ("windows", 0, 0), ("hidden", 0, 0), ("windows", 0, 1), ("hidden", 0, 1), ("tail", 0, 0), ("tail", 0, 1),
    ("tail", 0, 2), ("windows", 1, 0), ("tail", 0, 3), ("hidden", 1, 0), ("windows", 1, 1), ("tail", 0, 4), ("tail", 0, 5),
    ("tail", 0, 6), ("hidden", 1, 1), ("tail", 0, 7), ("tail", 0, 8), ("setup", 0, 0), ("setup", 0, 1), ("tail", 1, 0),
    ("setup", 0, 2), ("setup", 0, 3), ("tail", 1, 1), ("setup", 0, 4), ("tail", 1, 2), ("setup", 0, 5), ("tail", 1, 3),
    ("setup", 0, 6), ("tail", 1, 4))
SLOT = STEPS * UNITS
BESIDE = {k: (("tail", 1, 5 + k),) for k in range(4)} | {4 + k: (("setup", 1, k),) for k in range(7)} | {
    SLOT - 3: (("norm", 0, 0),), SLOT - 2: (("norm", 0, 1),), SLOT: (("norm", 0, 2),),
    SLOT + 2: (("route", 0, 1),), SLOT + 4: (("route", 0, 2),), SLOT + 5: (("route", 0, 3),),
    SLOT + 6: (("first", 0),), SLOT + 7: (("relu", 0), ("first", 1))} | {
    SLOT + 8 + 2 * g: (("relu", g + 1), ("second", g), *((("third", g - 1),) if g else ())) for g in range(EARLY)} | {
    SLOT + 9 + 2 * g: (("out", g), ("mix", g), ("first", g + 2), *((("norm", 1, 0),) if g == EARLY - 1 else ()))
    for g in range(EARLY)} | {SLOT + 16: (("norm", 1, 1),), SLOT + 18: (("norm", 1, 2),)}
KEYS = ((0, 5, 1, 6, 2, 7, 3, 4), (4, 0, 5, 1, 6, 2, 7, 3))
EPILOGUE = (
    ("weigh", 3, 6), ("weigh", 3, 7), ("kept", 3), ("relu", 5), ("second", 4), ("third", 3), ("combine", 0), ("out", 4),
    ("mix", 4), ("finish", 3, 0), ("finish", 3, 1), ("first", 6), ("relu", 6), ("second", 5), ("third", 4), ("out", 5),
    ("mix", 5), ("finish", 3, 2), ("finish", 3, 3), ("first", 7), ("relu", 7), ("finish", 3, 4), ("norm", 2, 0),
    ("second", 6), ("third", 5), ("out", 6), ("mix", 6), ("norm", 2, 1), ("first", 8), ("relu", 8), ("second", 7),
    ("out", 7), ("mix", 7), ("first", 9), ("relu", 9), ("second", 8),
    ("out", 8), ("norm", 2, 2), ("first", 10), ("relu", 10), ("second", 9), ("out", 9), ("route", 1, 1), ("first", 11),
    ("relu", 11), ("second", 10), ("out", 10), ("third", 6), ("route", 1, 2), ("first", 12), ("relu", 12), ("second", 11), ("out", 11), ("third", 7), ("combine", 1),
    ("route", 1, 3), *((what, g) for g in range(8, 12) for what in ("mix", "third")), ("combine", 2),
    *(step for g in range(12, LAST) for step in (
        *((("first", g + 1), ("relu", g + 1)) if g + 1 < LAST else ()), ("second", g), ("out", g), ("mix", g),
        *((("third", g - 1),) if g > 12 else ()))),
    ("third", LAST - 1), ("combine", 3))
FINISH = (4, 5, 6, 8, 9)


def order():
    steps = list(PROLOGUE)
    for t in range(STEPS * (UNITS + 1) + LAG):
        if t < STEPS * UNITS:
            steps.append(("maxima", *divmod(t, STEPS)))
        e = t - STEPS - LAG
        if e >= 0:
            steps.append(("exps", *divmod(e, STEPS)))
            u, k = divmod(e - 4, STEPS)
            if u >= 0 and k % 2 == 0:
                steps.append(("weigh", u, k // 2))
            u, k = divmod(e - STEPS, STEPS)
            if u >= 0 and k == 3:
                steps.append(("kept", u))
            if u >= 0 and k in FINISH:
                steps.append(("finish", u, FINISH.index(k)))
        u, k = divmod(t - STEPS, STEPS)
        if k == LAG - 1 and 0 <= u < UNITS:
            steps.append(("rows", u))
        steps += BESIDE.get(t, ())
    return (*steps, *EPILOGUE)


def tower_bank(b):
    return 0 if b else 4


def max_bank(u):
    return 0 if u else 4


def f2_bank(g):
    return 2 if g < 12 or g % 2 else 6


def norm_units(i):
    return range(NC) if i < B else NORMS[i - B]


def normed(i):
    return sum(len(norm_units(k)) for k in range(i))


def constants():
    power = [1]
    for _ in range(max(WINDOWS) - 1):
        power.append(power[-1] * BASE % MOD)
    band = np.zeros((P, 2, NW, P), np.float32)
    for k, w in enumerate(WINDOWS):
        for j in range(w):
            for t in range(P):
                src = t - j
                band[src % P, 0 if src >= 0 else 1, k, t] = power[j]
    n = np.arange(NR, dtype=np.float32)[:, None]
    div = np.exp(np.arange(0, E, 2, dtype=np.float32) * np.float32(-np.log(10000.0) / E)).astype(np.float32)
    ang = n * div
    enc = np.stack([np.sin(ang), np.cos(ang)], axis=-1).reshape(NR, E).astype(np.float32)
    heads = (np.arange(E)[:, None] // HD == np.arange(NH)[None, :]).astype(np.float32)
    start = (np.arange(QT) % SCH == 0).astype(np.float32)
    pair = (np.arange(NE)[:, None, None] == 2 * np.arange(NPAIR)[None, :, None] + np.arange(P)[None, None, :] // E)
    return {
        "band": band.reshape(P, -1),
        "ident": np.eye(P, dtype=np.float32),
        "encT": np.ascontiguousarray(enc.T),
        "heads": heads,
        "start": np.broadcast_to(start, (P, QT)).copy(),
        "pair": pair.astype(np.float32).reshape(NE, NPAIR * P),
        "iota": np.arange(P, dtype=np.float32)[:, None],
    }


PACK128 = (("mlp", NL * H), ("wg", SS), ("wi", SS), ("wout", E), ("wo4", H), ("fwo", NPAIR * E), ("start", QT))
PACK64 = (("winh", H), ("aqk", 2 * E), ("av", E), ("wpos", E), ("encT", NR), ("ao", E), ("wr", NE), ("w1", NE * E),
          ("heads", NH))
COLS = (("b_in", 1), ("ln_g", 1), ("ln_b", 1), ("mlp_b", NL), ("bg", 1), ("bi", 1), ("conv_b", 1), ("gamma", 1),
        ("beta", 1), ("bqk", 1), ("u", 1), ("v", 1), ("bpos", 1), ("bo", 1), ("convw", KC // 2), ("f1", 5 * NPAIR), ("f2", 5 * NPAIR))
ROWS = (("bq", E), ("bout", E), ("bv", E), ("ao_b", E), ("br", NE))


def spans(pack):
    at, out = 0, {}
    for name, n in pack:
        out[name] = (at, at + n)
        at += n
    return out, at


S128, N128 = spans(PACK128)
S64, N64 = spans(PACK64)
SCOL, NCOL = spans(COLS)
SROW, NROW = spans(ROWS)


def tower(nc, a):
    with ExitStack() as ctx:
        def sb(name, shape, dt=F32):
            return ctx.enter_context(nc.sbuf_tensor(name, shape, dt))

        made = {}

        def sem(name):
            if name not in made:
                made[name] = ctx.enter_context(nc.semaphore(name))
            return made[name]

        ps = ctx.enter_context(nc.psum_tensor("ps", [P, 8, 512], F32))
        bank = [ps[:, i, :] for i in range(8)]

        w128, w64, cols, rows = sb("w128", [P, N128]), sb("w64", [P, N64]), sb("cols", [P, NCOL]), sb("rows", [P, NROW])
        ident, band = sb("ident", [P, P]), sb("band", [P, 2, NW, P])
        emb3 = sb("emb3", [E, V + H + E])
        iota = sb("iota", [P, 1])
        xi, xf = sb("xi", [B * NT, P], I32), sb("xf", [B * NT, P])
        xcol = sb("xcol", [P, B, NT + 1])
        hi32 = sb("hi32", [P, NW, B * NT], I32)
        idx = sb("idx", [P, NW, B * NT], I32)
        prob = sb("prob", [P, RING, CT])
        probf = prob[:].rearrange("p r t -> p (r t)")
        emb = probf[:, 0:B * NT * NW * E].rearrange("p (n k e) -> p n k e", k=NW, e=E)
        onehot = probf[0:V + NW, B * NT * NW * E:B * NT * NW * E + B * T]
        gtab = sb("gtab", [V + NW, H])
        qtab = sb("qtab", [V, E])
        cdiag = sb("cdiag", [P, KC // 2, E])
        posb = sb("posb", [P, NH, NR])
        prod = sb("prod", [P, TC, NW, E])
        sc, sm = sb("sc", [P, TC, NW]), sb("sm", [P, TC])
        hf = sb("hf", [P, TC, E])
        hfT = sb("hfT", [P, B, KC - 1 + T])
        cf = sb("cf", [E, CT])
        hT = sb("hT", [H, B * T])
        scan = sb("scan", [P, 6, QT])
        th, ga, gd, d0, d1, cum = (scan[:, i, :] for i in range(6))
        nstart = sb("nstart", [P, QT])
        cw, aw = sb("cw", [P, QT]), sb("aw", [P, QT])
        ends = sb("ends", [P, 2, QG])
        endsf = sb("endsf", [SS, NQ, 2, QG])
        carry = sb("carry", [SS, 1 + NQ * QG])
        carryq = sb("carryq", [P, QG])
        bnc, bns = sb("bnc", [P, NC, TC, 6]), sb("bns", [P, NC, TC, 2])
        rs, rt, rv = sb("rs", [P, NT]), sb("rt", [P, NT]), sb("rv", [P, NT])
        xn = sb("xn", [P, NC, TC, H])
        act_s = sb("act_s", [H, NC, CT])
        qsc, qbi, vbi, bgh = sb("qsc", [P, 1]), sb("qbi", [P, 1]), sb("vbi", [E, 1]), sb("bgh", [P, 1])
        htok = sb("htok", [P, B * NT, E])
        prodf = prod[:].rearrange("p n k e -> p (n k e)")
        la, lb = (prodf[:, i * NT * E:(i + 1) * NT * E].rearrange("p (n e) -> p n e", e=E) for i in range(2))
        lc = sb("lc", [P, NT])
        states = band[:].rearrange("p a k t -> p (a k t)")
        lnT = sb("lnT", [P, B * T])[:]
        qk32 = act_s[:].rearrange("p c t -> p (c t)")
        hfTf = hfT[:].rearrange("p b t -> p (b t)")
        qv, wT = hfTf[:, 0:T], hfTf[0:3 * NE, T:2 * T]
        fin = hT[:, 0:B * NT * E].rearrange("p (n e) -> p n e", e=E)
        ctxs, ctxT = hT[:, B * NT * E:B * NT * E + CT], hT[0:E, B * NT * E + CT:B * NT * E + 2 * CT]
        pairb = sb("pairb", [P, NPAIR * P], BF16)
        part = [sb(f"part{i}", [P, T], BF16) for i in range(3)]
        qst, kst = sb("qst", [P, B, NH, T], BF16), sb("kst", [P, B, NH, T], BF16)
        pair32 = qst[0:3 * NE, 0, 0, :].bitcast(F32)
        vt = sb("vt", [P, B, NT, NH, 32])
        pad = probf.rearrange("p (c n h w) -> p c n h w", c=NC, n=TC, h=NH)
        bias = sb("bias", [P, B, NT, NH, WIN])
        pend = sb("pend", [P, B, NT, NH, 2])
        mx = sb("mx", [P, B, NT, NH, 3])
        junk = sb("junk", [P, 2, WIN], BF16)
        tv = sb("tv", [P, 3, TC, NH])
        tr = sb("tr", [P, 3, TC, NH])
        tp = sb("tp", [P, 3, 3, TC, NH], BF16)
        identb = sb("identb", [P, P], BF16)
        den = sb("den", [P, TC, NH])
        xnf = xn[:].rearrange("p c n h -> p (c n h)")
        ctxn = xnf[:, 0:TC * E].rearrange("p (n e) -> p n e", e=E)
        rw = xnf[:, TC * E:TC * (E + NE)].rearrange("p (n e) -> p n e", e=NE)
        rwf = rw.rearrange("p n e -> p (n e)")
        wTb = sb("wTb", [P, CT], BF16)
        rw3 = sb("rw3", [P, TC, 3, NE], BF16)
        w2bd = scan[:, 0:2, :].rearrange("p a (b t) -> p (a b) t", t=P)
        fsc, fbi = sb("fsc", [P, 2, NPAIR]), sb("fbi", [P, 2, NPAIR])
        bo8 = sb("bo8", [3 * NE, E])
        rwm = sb("rwm", [P, TC])
        ff = [bias[:, b, 0:TC].rearrange("p n h w -> p (n h w)")[:, k * CT:(k + 1) * CT] for b in range(B)
              for k in range(TC * NH * WIN // CT)]
        f1, f3 = ff[0:2], ff[6:6 + NPAIR]
        f2 = (ff[2], ff[3], act_s[:, 0, :], act_s[:, 1, :])
        wbc = ((ff[4], ff[5], ff[10], ff[11]), [sb(f"wbc1_{p}", [P, CT])[:] for p in range(NPAIR)])
        spare = bias[:, 1].rearrange("p n h w -> p (n h w)").bitcast(I32)
        xrep, xsh = spare[0:V + NW, 0:B * T], spare[0:V + NW, B * T:2 * B * T]

        def c128(name):
            return w128[:, S128[name][0]:S128[name][1]]

        def c64(name, n=E):
            return w64[0:n, S64[name][0]:S64[name][1]]

        def col(name, i=0, n=P):
            return cols[0:n, SCOL[name][0] + i:SCOL[name][0] + i + 1]

        def row(name, *mid):
            r = rows[:, SROW[name][0]:SROW[name][1]]
            for k in mid:
                r = r.rearrange("p (o n) -> p o n", o=1).to_broadcast([P, k, r.shape[-1]])
            return r

        def padding(c, at, to, of):
            rows_ = pad[:, c].rearrange("p n h w -> p (n h) w")
            return rows_[:, :, at:to], rows_[:, :, of:of + 1].to_broadcast([P, TC * NH, to - at])

        skew = a["skew"]
        block = ctx.enter_context(nc.Block())

        @block.sync
        def _(sp):
            def load(name, dst, src):
                sp.dma_start(dst, src).then_inc(sem(name), 16)

            load("ld_x", xi[:], a["x"].rearrange("b (n p) -> (b n) p", p=P))
            load("ld_ident", ident[:], a["ident"])
            load("ld_band", band[:].rearrange("p a k t -> p (a k t)"), a["band"])
            flat = a["x"].rearrange("b t -> (b t)").rearrange("(o n) -> o n", o=1)
            load("ld_oh", xrep, flat.to_broadcast([V + NW, B * T]))
            load("ld_oh", iota[:], a["iota"])
            sp.wait_ge(sem("xsh_set"), 1)
            for k, o in enumerate(OFFSETS):
                for b in range(B):
                    load("ld_sh", xsh[V + k:V + k + 1, b * T + o:(b + 1) * T], flat[:, b * T:(b + 1) * T - o])
            load("ld_emb", emb3[:], a["emb3"])
            load("ld_emb", gtab[V:V + NW, :], a["winm"])
            load("ld_w", w64[:], a["w64"])
            load("ld_w", cols[:], a["cols"])
            load("ld_w", rows[:], a["rows"].to_broadcast([P, NROW]))
            load("ld_w", w128[:], a["w128"])
            load("ld_pair", pair32, a["pair"])
            load("ld_f", bo8[:], a["bo8"])

            for b in range(B):
                for i in range(3):
                    sp.wait_ge(sem("parts"), 3 * b + i + 1)
                    sp.dma_start(a["parts"][b, i].rearrange("s h d t -> (s h d) t"), part[i][:]
                                 ).then_inc(sem(f"part_out{i}"), 16)
                def stack(parts):
                    for i in parts:
                        sp.wait_ge(sem(f"part_out{i}"), 16 * (b + 1))
                        for g, pair_ in enumerate(QKG):
                            for side, st in enumerate((qst, kst)):
                                if pair_[side] == i:
                                    load(f"stacked{b}", st[HD * g:HD * g + HD, b, :, :],
                                         a["parts"][b, i, side].rearrange("h d t -> d h t"))

                stack((0,))
                for c in range(NC):
                    i = b * NC + c
                    ns = slice(c * TC, (c + 1) * TC)
                    sp.wait_ge(sem("padded"), 2 * (i + 1))
                    sp.wait_ge(sem("padmid"), TC * (i + 1))
                    sp.dma_start(skew[b, ns].rearrange("n h p c -> p (n h) c"),
                                 pad[:, c].rearrange("p n h c -> p (n h) c")).then_inc(sem(f"skew_out{c}"), 16)
                    if c == 0:
                        stack((1, 2))
                    sp.wait_ge(sem(f"skew_out{c}"), 16 * (b + 1))
                    for g in range(2):
                        half = bias[HALF * g:HALF * g + HALF, b, ns].rearrange("p n h w -> p (n h) w")
                        sp.dma_start(half[:, :, HALF * g:HALF * g + 2 * HALF], skewed(skew, b, ns, g)
                                     ).then_inc(sem(f"biased{i}"), 16)

            sp.wait_ge(sem("w2_zero"), 1)
            for e in range(2):
                load("ld_f", w2bd[E * e:E * e + E, :, E * e:E * e + E], a["w2"][e])
            for i, u in enumerate(EXPERT_UNITS):
                sp.wait_ge(sem("fin"), i + 1)
                sp.dma_start(a["out"][u // NC, (u % NC) * CT:(u % NC + 1) * CT, :].rearrange("(n p) e -> p n e", p=P),
                             fin[:, u * TC:(u + 1) * TC, :]).then_inc(sem("stored"), 16)
            sp.wait_ge(sem("stored"), 16 * 2 * B)

        @block.gpsimd
        def _(pool):
            def after(ins, name, n):
                ins.then_inc(sem(name), 1)
                pool.wait_ge(sem(name), n)

            after(nc.gpsimd.memset(xsh[V:V + NW, :], -1), "xsh_set", 1)
            after(nc.gpsimd.memset(xcol[:], 0.0), "xcol_set", 1)
            after(nc.gpsimd.memset(hfT[:, :, 0:KC - 1], 0.0), "pool_set", 1)
            after(nc.gpsimd.memset(hfT[:, :, KC - 2 + T:KC - 1 + T], 0.0), "pool_set", 2)
            after(nc.gpsimd.memset(carry[:, 0:1], 0.0), "pool_set", 3)
            pool.wait_ge(sem("idx"), 1)
            for n in range(B * NT):
                for k in range(NW):
                    pool.indirect_dma_start(emb[:, n, k, :], None, a["table"],
                                            bass.IndirectOffsetOnAxis(ap=idx[:, k, n:n + 1].bitcast(U32), axis=0)
                                            ).then_inc(sem(f"gathered{n // TC}"), 16)
            after(nc.gpsimd.memset(lnT[E:P, :], 0.0), "lnT_zero", 1)
            after(nc.gpsimd.memset(kst[NP6:P, :, :, :], 1.0), "st_set", 1)
            after(nc.gpsimd.memset(vt[:, :, :, :, HD:32], 0.0), "vt_zero", 1)
            after(nc.gpsimd.memset(vt[:, :, :, :, HD:HD + 1], 1.0), "st_set", 2)
            after(nc.gpsimd.memset(mx[:], -3.0e38), "st_set", 3)
            after(nc.gpsimd.memset(wTb[:], 0.0), "wTb_zero", 1)
            n_corners = 0
            for b in range(B):
                for c in range(NC):
                    pool.wait_ge(sem("padmid"), b * NT + (c + 1) * TC)
                    for g, at, of in ((0, 2 * HALF, LPAD + NR - 1), (1, 0, LPAD)):
                        r = slice(HALF * g, HALF * g + HALF)
                        corner = bias[r, b, c * TC:(c + 1) * TC].rearrange("p n h w -> p (n h) w")[:, :, at:at + HALF]
                        score = pad[r, c].rearrange("p n h w -> p (n h) w")[:, :, of:of + 1]
                        n_corners += 1
                        after(nc.gpsimd.tensor_copy(corner, score.to_broadcast([HALF, TC * NH, HALF])), "corners", n_corners)
            pool.wait_ge(sem("states"), NQ * B)
            nc.gpsimd.memset(w2bd, 0.0).then_inc(sem("w2_zero"), 1)

        @block.scalar
        def _(act):
            def af(out, in_, func, done, **kw):
                nc.scalar.activation(out, in_, func, **kw).then_inc(sem(done), 1)

            act.wait_ge(sem("ld_w"), 16 * 4)

            def windows(b, c):
                i = b * NC + c
                act.wait_ge(sem("sc_shift"), i + 1)
                af(sc[:].rearrange("p n k -> p (n k)"), sc[:].rearrange("p n k -> p (n k)"), ACT.Exp, "sc_exp",
                   scale=E ** -0.5)

            def hidden(b, c):
                i = b * NC + c
                act.wait_ge(sem("pe_hfT"), i + 1)
                if i == 0:
                    act.wait_ge(sem("pool_set"), 3)
                for half in range(2):
                    at = KC - 1 - half + c * CT
                    af(hfT[E * half:E * half + E, b, at:at + CT], bank[1][0:E, :], ACT.Copy, "hfT")
                act.wait_ge(sem("pe_conv"), i + 1)
                if i:
                    act.wait_ge(sem("pe_h0"), i)
                af(cf[:], bank[1][0:E, :], ACT.Silu, "cf", bias=col("conv_b", 0, E))
                act.wait_ge(sem("pe_h0"), i + 1)
                af(hT[:, i * CT:(i + 1) * CT], bank[3], ACT.Silu, "h0", bias=col("b_in"))

            def tail(b, k):
                if k == 0:
                    act.wait_ge(sem("pe_gd"), b + 1)
                    if b:
                        act.wait_ge(sem("ends"), b)
                    af(th, bank[tower_bank(b)][:, 0:QT], ACT.Tanh, "th", bias=bgh[:], scale=0.5)
                    hb = hT[:, b * T:(b + 1) * T]
                    af(hb, hb, ACT.Identity, "h_bo", bias=col("bo"))
                elif k == 4:
                    for c in range(NC):
                        i = b * NC + c
                        act.wait_ge(sem("pe_xnT"), i + 1)
                        af(hT[:, i * CT:(i + 1) * CT], bank[tower_bank(b) + 2 * c], ACT.Identity, "hn", scale=col("ln_g"),
                           bias=col("ln_b"))
                elif 5 <= k < 5 + NL:
                    l = k - 5
                    if b and not l:
                        act.wait_ge(sem("parts"), 3 * b)
                    for c in range(NC):
                        i = (b * NL + l) * NC + c
                        act.wait_ge(sem("pe_mlp"), i + 1)
                        if i >= NC:
                            act.wait_ge(sem("mlp_add"), i - 1)
                        af(act_s[:, c, :], bank[tower_bank(b) + 1 - l % 2 + 2 * c], ACT.Silu, "mlp_silu", bias=col("mlp_b", l))

            def square(i):
                act.wait_ge(sem("centered"), i + 1)
                n = len(norm_units(i)) * TC
                af(lb[:, 0:n].rearrange("p n e -> p (n e)"), la[:, 0:n].rearrange("p n e -> p (n e)"), ACT.Square,
                   "squared")

            def setup(b, k):
                if k == 0:
                    square(b)
                elif k == 2:
                    for c in range(NC):
                        i = b * NC + c
                        act.wait_ge(sem("pe_lnT"), i + 1)
                        af(lnT[0:E, i * CT:(i + 1) * CT], bank[tower_bank(b) + 2 + c][0:E, :], ACT.Identity, "lnT",
                           scale=col("gamma", 0, E), bias=col("beta", 0, E))
                elif k == 3:
                    for c in range(NC):
                        act.wait_ge(sem("pe_qk"), b * NC + c + 1)
                        af(qk32[:, c * CT:(c + 1) * CT], bank[tower_bank(b) + c], ACT.Identity, "qk32", scale=qsc[:],
                           bias=qbi[:])
                    if b:
                        act.wait_ge(sem("pe_pos"), b * NT)
                    for c in range(NC):
                        af(qv[0:E, c * CT:(c + 1) * CT], bank[tower_bank(b) + c][0:E, :], ACT.Identity, "qv", scale=0.25,
                           bias=vbi[:])
                elif k >= 5:
                    c = k - 5
                    if b:
                        act.wait_ge(sem(f"skew_out{c}"), 16 * b)
                        act.wait_ge(sem("corners"), 2 * (c + 1))
                    for n in range(c * TC, (c + 1) * TC):
                        act.wait_ge(sem("pe_pos"), b * NT + n + 1)
                        af(pad[:, c, n % TC, :, LPAD:LPAD + NR],
                           bank[tower_bank(b) + n % 2][:, 0:NH * NR].rearrange("p (h r) -> p h r", h=NH), ACT.Copy, "padmid")
                    act.wait_ge(sem("padmid"), b * NT + (c + 1) * TC)
                    af(*padding(c, 0, LPAD, LPAD), ACT.Copy, "padded")
                    af(*padding(c, LPAD + NR, PW, LPAD + NR - 1), ACT.Copy, "padded")

            def exps(u, j):
                if u == 0 and j == 0:
                    act.wait_ge(sem("corners"), 2 * UNITS)
                    for c in range(NC):
                        act.wait_ge(sem(f"skew_out{c}"), 16 * B)
                for e in (2 * (STEPS * u + j), 2 * (STEPS * u + j) + 1):
                    act.wait_ge(sem("pe_s"), e + 1)
                    if e >= RING:
                        act.wait_ge(sem("pe_pv"), (e - RING) // NH + 1)
                    af(prob[:, e % RING, :], bank[4 + e % 2], ACT.Exp, "exp")

            def rows(u):
                act.wait_ge(sem("pe_rows"), u + 1)
                c, b = divmod(u, B)
                for h in range(NH):
                    af(qst[NP6:NP6 + 9, b, h, c * CT:(c + 1) * CT], bank[6][32 * h:32 * h + 9, :], ACT.Copy, "rows_in")

            def kept(u):
                act.wait_ge(sem("pe_pv"), NT * (u + 1))
                if u:
                    act.wait_ge(sem("pe_ctx"), u)
                af(ctxs, bank[7], ACT.Copy, "ctxs")

            def finish(u, k):
                if k == 2:
                    act.wait_ge(sem("pe_ctxnT"), u + 1)
                    af(ctxT, bank[6][0:E, :], ACT.Copy, "ctxT")

            def norm_step(j, k):
                if k == 0:
                    square(B + j)
                elif k == 2:
                    for m, u in enumerate(NORMS[j]):
                        act.wait_ge(sem("pe_lnT"), normed(B + j) + m + 1)
                        c, b = divmod(u, B)
                        t0 = b * T + c * CT
                        af(lnT[0:E, t0:t0 + CT], bank[6 if j else m][0:E, :], ACT.Copy, "lnT")

            def route(c, k):
                if k == 1:
                    act.wait_ge(sem("rw_shift"), c + 1)
                    af(rwf, rwf, ACT.Exp, "rw_exp")
                elif k == 2:
                    act.wait_ge(sem("pe_wT"), c + 1)
                    if c:
                        act.wait_ge(sem("pe_wbc"), NPAIR)
                    else:
                        act.wait_ge(sem("wTb_zero"), 1)
                    af(wTb[0:3 * NE, :], bank[4 * c + 3][0:3 * NE, :], ACT.Copy, "wTb")
                    af(wT[:, c * CT:(c + 1) * CT], bank[4 * c + 3][0:3 * NE, :], ACT.Copy, "wT")
                elif k == 3:
                    for p in range(NPAIR):
                        act.wait_ge(sem("pe_wbc"), c * NPAIR + p + 1)
                        af(wbc[c][p], bank[4 * c + p % 2], ACT.Copy, "wbc")

            def first_activation(g):
                p = g % NPAIR
                if g == 0:
                    act.wait_ge(sem("fcols"), 1)
                act.wait_ge(sem("pe_f1"), g + 1)
                if g >= 2:
                    act.wait_ge(sem("pe_f2"), g - 1)
                af(f1[g % 2], bank[g % 2], ACT.Relu, "f1", scale=fsc[:, 0, p:p + 1], bias=fbi[:, 0, p:p + 1])

            def second_activation(g):
                p = g % NPAIR
                act.wait_ge(sem("pe_f2"), g + 1)
                if g >= 4:
                    act.wait_ge(sem("f3"), g - 3)
                af(f2[g % 4], bank[f2_bank(g)], ACT.Relu, "f2", scale=fsc[:, 1, p:p + 1], bias=fbi[:, 1, p:p + 1])

            steps = {"windows": windows, "hidden": hidden, "tail": tail, "setup": setup, "exps": exps, "rows": rows,
                     "kept": kept, "finish": finish, "norm": norm_step, "route": route, "relu": first_activation,
                     "out": second_activation}
            for what, *at in order():
                if what in steps:
                    steps[what](*at)

        @block.vector
        def _(dve):
            n_chain = [0]
            v = nc.vector

            def link(ins):
                n_chain[0] += 1
                ins.then_inc(sem("dve_chain"), 1)
                dve.wait_ge(sem("dve_chain"), n_chain[0])

            def rsqrt(x, n):
                y, t = rs[:, 0:n], rt[:, 0:n]
                link(v.tensor_scalar(t.bitcast(I32), x.bitcast(I32), 1, None, ALU.logical_shift_right))
                link(v.tensor_scalar(y.bitcast(I32), t.bitcast(I32), -1.0, float(0x5F3759DF), ALU.mult, ALU.add))
                for _ in range(3):
                    link(v.scalar_tensor_tensor(t, y, -0.5, y, ALU.mult, ALU.mult))
                    link(v.tensor_tensor(t, t, x, ALU.mult))
                    link(v.scalar_tensor_tensor(y, t, 1.5, y, ALU.add, ALU.mult))

            dve.wait_ge(sem("ld_x"), 16)
            v.tensor_copy(xf[:], xi[:]).then_inc(sem("xf"), 1)
            dve.wait_ge(sem("pe_x"), 1)
            dve.wait_ge(sem("xcol_set"), 1)
            v.tensor_copy(xcol[:, :, 1:NT + 1], bank[0][:, 0:B * NT].rearrange("p (b n) -> p b n", b=B)
                          ).then_inc(sem("xcol"), 1)
            dve.wait_ge(sem("pe_hash"), 1)
            link(v.tensor_copy(hi32[:].rearrange("p k n -> p (k n)"), bank[1][:, 0:NW * B * NT]))
            for k in range(NW):
                last = v.tensor_scalar(idx[:, k, :], hi32[:, k, :], MOD - 1, k * MOD, ALU.bitwise_and, ALU.bitwise_or)
            last.then_inc(sem("idx"), 1)
            link(v.memset(states, 0.0))
            dve.wait_ge(sem("ld_oh"), 32)
            v.tensor_scalar(onehot[0:V, :], xrep[0:V, :], iota[0:V, :], None, ALU.is_equal).then_inc(sem("onehot"), 1)
            dve.wait_ge(sem("ld_sh"), 16 * 8)
            v.tensor_tensor(onehot[V:V + NW, :], xrep[V:V + NW, :], xsh[V:V + NW, :], ALU.is_equal
                            ).then_inc(sem("onehot"), 1)
            dve.wait_ge(sem("ld_w"), 16 * 4)
            dve.wait_ge(sem("pe_tab"), 1)
            v.tensor_copy(gtab[0:V, :], bank[2][0:V, 0:H]).then_inc(sem("tab"), 1)
            v.tensor_tensor(qtab[:], bank[2][0:V, H:H + E], row("bq")[0:V, :], ALU.add).then_inc(sem("tab"), 1)
            for half in range(2):
                r = slice(E * half, E * half + E)
                for j in range(KC // 2):
                    v.tensor_scalar(cdiag[r, j, :], ident[r, r], col("convw", j)[r, :], None, ALU.mult
                                    ).then_inc(sem("tab"), 1)
            for h in range(NH):
                v.tensor_scalar(posb[0:E, h, :], bank[2][0:E, 256:256 + NR], col("bpos", 0, E),
                                c64("heads")[:, h:h + 1], ALU.add, ALU.mult).then_inc(sem("tab"), 1)
            v.memset(posb[E:P], 0.0).then_inc(sem("tab"), 1)
            v.tensor_copy(identb[:], ident[:]).then_inc(sem("tab"), 1)
            dve.wait_ge(sem("ld_pair"), 16)
            link(v.memset(pairb[:], 0.0))
            v.tensor_copy(pairb[0:3 * NE, :], pair32).then_inc(sem("tab"), 1)
            v.tensor_scalar(nstart[:], c128("start"), -1.0, 1.0, ALU.mult, ALU.add).then_inc(sem("tab"), 1)
            v.tensor_scalar(bgh[:], col("bg"), 0.5, None, ALU.mult).then_inc(sem("tab"), 1)
            v.memset(qsc[0:E, :], 0.25).then_inc(sem("tab"), 1)
            v.memset(qsc[E:P, :], 1.0).then_inc(sem("tab"), 1)
            link(v.tensor_tensor(qbi[:], col("bqk"), col("u"), ALU.add))
            v.tensor_tensor(vbi[:], col("bqk", 0, E), col("v", 0, E), ALU.add).then_inc(sem("tabx"), 1)
            dve.wait_ge(sem("tabx"), 1)
            v.tensor_scalar(qbi[0:E, :], qbi[0:E, :], 0.25, None, ALU.mult).then_inc(sem("tab"), 1)
            v.tensor_scalar(vbi[:], vbi[:], 0.25, None, ALU.mult).then_inc(sem("tab"), 1)
            for l, name in enumerate(("f1", "f2")):
                o = SCOL[name][0]
                fb, fg, fbe, fm, fv = (cols[:, o + NPAIR * j:o + NPAIR * (j + 1)] for j in range(5))
                link(v.tensor_scalar(rv[:, 0:NPAIR], fv, EPS_BN, None, ALU.add))
                rsqrt(rv[:, 0:NPAIR], NPAIR)
                link(v.tensor_tensor(fsc[:, l, :], fg, rs[:, 0:NPAIR], ALU.mult))
                link(v.tensor_tensor(fbi[:, l, :], fb, fm, ALU.subtract))
                link(v.tensor_tensor(fbi[:, l, :], fbi[:, l, :], fsc[:, l, :], ALU.mult))
                link(v.tensor_tensor(fbi[:, l, :], fbi[:, l, :], fbe, ALU.add))
            dve.sem_inc(sem("fcols"), 1)

            def windows(b, c):
                i = b * NC + c
                es = emb[:, i * TC:(i + 1) * TC]
                dve.wait_ge(sem("pe_q"), i + 1)
                if i:
                    dve.wait_ge(sem("hf"), i)
                dve.wait_ge(sem(f"gathered{i}"), 16 * NW * TC)
                link(v.tensor_tensor(prod[:], es, bank[i % 2 * 2][:, 0:TC * E].rearrange("p (n o e) -> p n o e", n=TC, o=1)
                                     .to_broadcast([P, TC, NW, E]), ALU.mult))
                link(v.tensor_reduce(sc[:], prod[:], AX.X, ALU.add))
                link(v.tensor_reduce(sm[:], sc[:], AX.X, ALU.max))
                over = sm[:].rearrange("p (n o) -> p n o", o=1).to_broadcast([P, TC, NW])
                v.tensor_tensor(sc[:], sc[:], over, ALU.subtract).then_inc(sem("sc_shift"), 1)
                dve.wait_ge(sem("sc_exp"), i + 1)
                link(v.tensor_reduce(sm[:], sc[:], AX.X, ALU.add))
                link(v.reciprocal(sm[:], sm[:]))
                link(v.tensor_tensor(sc[:], sc[:], over, ALU.mult))
                link(v.tensor_tensor(prod[:], es, sc[:].rearrange("p n (k o) -> p n k o", o=1)
                                     .to_broadcast([P, TC, NW, E]), ALU.mult))
                if i:
                    dve.wait_ge(sem("pe_hfT"), i)
                v.tensor_reduce(hf[:], prod[:].rearrange("p n k e -> p n e k"), AX.X, ALU.add).then_inc(sem("hf"), 1)

            def tail(b, k):
                if k == 0:
                    dve.wait_ge(sem("th"), b + 1)
                    link(v.tensor_scalar(ga, th, -0.5, 0.5, ALU.mult, ALU.add))
                    link(v.scalar_tensor_tensor(gd, bank[tower_bank(b)][:, QT:2 * QT], col("bi"), ga, ALU.add, ALU.mult))
                    link(v.tensor_scalar(ga, th, 0.5, 0.5, ALU.mult, ALU.add))
                    v.scalar_tensor_tensor(d1, ga, 1e-6, c128("start"), ALU.max, ALU.mult)
                    link(v.scalar_tensor_tensor(d0, ga, 1e-6, nstart[:], ALU.max, ALU.mult))
                    link(v.tensor_tensor_scan(cum, d0, d1, 0.0, ALU.mult, ALU.add))
                    link(v.tensor_scalar(d0, cum, 1e-8, None, ALU.max))
                    link(v.reciprocal(d0, d0))
                    link(v.tensor_tensor(d0, gd, d0, ALU.mult))
                    link(v.tensor_tensor_scan(cw[:], nstart[:], d0, 0.0, ALU.mult, ALU.add))
                    link(v.tensor_tensor(aw[:], cum, cw[:], ALU.mult))
                    v.tensor_copy(ends[:, 0, :], cum[:, SCH - 1::SCH])
                    v.tensor_copy(ends[:, 1, :], aw[:, SCH - 1::SCH]).then_inc(sem("ends"), 1)
                elif k == 1:
                    dve.wait_ge(sem("pe_ends"), b + 1)
                    if b:
                        dve.wait_ge(sem("pe_carry"), b)
                    link(v.tensor_copy(endsf[:].rearrange("p q a g -> p (q a g)"), bank[tower_bank(b) + 2][0:SS, 0:NQ * 2 * QG]))
                    for q in range(NQ):
                        link(v.tensor_tensor_scan(carry[:, 1 + q * QG:1 + (q + 1) * QG], endsf[:, q, 0, :],
                                                  endsf[:, q, 1, :], carry[:, q * QG:q * QG + 1], ALU.mult, ALU.add))
                    dve.sem_inc(sem("carry"), 1)
                elif k == 2:
                    dve.wait_ge(sem("pe_carry"), b + 1)
                    link(v.tensor_copy(carryq[:], bank[tower_bank(b) + 2][:, 128:128 + QG]))
                    link(v.tensor_tensor(cw[:].rearrange("p (g t) -> p g t", g=QG), cum.rearrange("p (g t) -> p g t", g=QG),
                                         carryq[:].rearrange("p (g o) -> p g o", o=1).to_broadcast([P, QG, SCH]),
                                         ALU.mult))
                    if b:
                        dve.wait_ge(sem("pe_y"), NC * b)
                    for q in range(NQ):
                        r = slice(SS * q, SS * q + SS)
                        v.tensor_tensor(states[r, q * QT:(q + 1) * QT], cw[r, :], aw[r, :], ALU.add
                                        ).then_inc(sem("states"), 1)
                elif k == 3:
                    y = [bank[tower_bank(b) + 1 + 2 * c].rearrange("p (n f) -> p n f", n=TC) for c in range(NC)]
                    for c in range(NC):
                        dve.wait_ge(sem("pe_y"), b * NC + c + 1)
                        for n in range(TC):
                            last = v.bn_stats(bnc[:, c, n, :], y[c][:, n, :])
                    link(last)
                    for c in range(NC):
                        for n in range(TC):
                            last = v.bn_aggr(bns[:, c, n, :], bnc[:, c, n, :])
                    link(last)
                    link(v.tensor_scalar(rv[:, 0:NT], bns[:, :, :, 1].rearrange("p c n -> p (c n)"), EPS_LN, None, ALU.add))
                    rsqrt(rv[:, 0:NT], NT)
                    if b:
                        dve.wait_ge(sem("pe_xnT"), NC * b)
                    for c in range(NC):
                        for n in range(TC):
                            v.tensor_scalar(xn[:, c, n, :], y[c][:, n, :], bns[:, c, n, 0:1],
                                            rs[:, c * TC + n:c * TC + n + 1], ALU.subtract, ALU.mult
                                            ).then_inc(sem("xn"), 1)
                elif 5 <= k < 5 + NL:
                    for c in range(NC):
                        i = (b * NL + k - 5) * NC + c
                        h = hT[:, (b * NC + c) * CT:(b * NC + c + 1) * CT]
                        dve.wait_ge(sem("mlp_silu"), i + 1)
                        dve.wait_ge(sem("pe_mlp"), i + 1)
                        v.tensor_tensor(h, h, act_s[:, c, :], ALU.add).then_inc(sem("mlp_add"), 1)
                elif k == 5 + NL:
                    dve.wait_ge(sem("pe_out"), b + 1)
                    v.tensor_tensor(htok[:, b * NT:(b + 1) * NT, :], bank[tower_bank(b)].rearrange("p (n e) -> p n e", n=NT),
                                    row("bout", NT), ALU.add).then_inc(sem("htok"), 1)

            def views(i):
                m = len(norm_units(i))
                return (m * TC, la[:, 0:m * TC].rearrange("p (b n) e -> p b n e", b=m),
                        lc[:, 0:m * TC].rearrange("p (b n) -> p b n", b=m),
                        lambda x: x[:, 0:m * TC].rearrange("p (b n o) -> p b n o", b=m, o=1).to_broadcast([P, m, TC, E]))

            def center(i, h):
                n, la4, lc2, over = views(i)
                if i:
                    dve.wait_ge(sem("pe_lnT"), normed(i))
                link(v.tensor_reduce(lc2, h, AX.X, ALU.add))
                link(v.tensor_scalar(lc[:, 0:n], lc[:, 0:n], 1.0 / E, None, ALU.mult))
                v.tensor_tensor(la4, h, over(lc), ALU.subtract).then_inc(sem("centered"), 1)

            def scale(i, twice):
                dve.wait_ge(sem("squared"), i + 1)
                dve.wait_ge(sem("centered"), i + 1)
                n, la4, _, over = views(i)
                link(v.tensor_reduce(lc[:, 0:n], lb[:, 0:n], AX.X, ALU.add))
                x = rv[:, 0:n]
                if twice:
                    link(v.tensor_scalar(x, lc[:, 0:n], (1.0 + EPS_LN) / E, EPS_LN + EPS_LN ** 2, ALU.mult, ALU.add))
                else:
                    link(v.tensor_scalar(x, lc[:, 0:n], 1.0 / E, EPS_LN, ALU.mult, ALU.add))
                rsqrt(x, n)
                v.tensor_tensor(la4, la4, over(rs), ALU.mult).then_inc(sem("ln"), 1)

            def setup(b, k):
                if k == 0:
                    dve.wait_ge(sem("htok"), b + 1)
                    center(b, htok[:, b * NT:(b + 1) * NT, :].rearrange("p (c n) e -> p c n e", c=NC))
                elif k == 1:
                    scale(b, True)
                elif k == 4:
                    dve.wait_ge(sem("qk32"), NC * (b + 1))
                    if b:
                        dve.wait_ge(sem("stacked0"), 16 * 12)
                    v.tensor_copy(part[0][:], qk32).then_inc(sem("parts"), 1)
                    dve.wait_ge(sem("parts"), 3 * b + 1)
                    link(v.tensor_tensor(qk32, qk32, part[0][:], ALU.subtract))
                    v.tensor_copy(part[1][:], qk32).then_inc(sem("parts"), 1)
                    dve.wait_ge(sem("parts"), 3 * b + 2)
                    v.tensor_tensor(part[2][:], qk32, part[1][:], ALU.subtract).then_inc(sem("parts"), 1)
                    dve.wait_ge(sem("pe_v"), b + 1)
                    dve.wait_ge(sem("st_set"), 3)
                    v.tensor_tensor(vt[:, b, :, :, 0:HD], bank[tower_bank(b) + 2].rearrange("p (n h d) -> p n h d", n=NT, h=NH),
                                    rows[:, SROW["bv"][0]:SROW["bv"][1]].rearrange("p (o h d) -> p o h d", o=1, h=NH)
                                    .to_broadcast([P, NT, NH, HD]), ALU.add).then_inc(sem("vt"), 1)
                elif k == 5:
                    dve.wait_ge(sem("pe_far"), b + 1)
                    v.tensor_copy(pend[:, b].rearrange("p n h f -> p (n h f)"), bank[tower_bank(b) + 3][:, 0:NT * NH * 2]
                                  ).then_inc(sem("far"), 1)

            def region_max(u, j):
                c, b = divmod(u, B)
                if j == 0:
                    dve.wait_ge(sem(f"biased{b * NC + c}"), 16 * 2)
                    dve.wait_ge(sem("corners"), 2 * (b * NC + c + 1))
                    dve.wait_ge(sem("far"), b + 1)
                h, n = j % NH, c * TC + j // NH
                i = STEPS * u + j
                t0 = n * P
                lo, hi = max(0, t0 - EDGE), min(T, t0 - EDGE + WIN)
                dve.wait_ge(sem("pe_m"), i + 1)
                s1024 = ps[:, max_bank(u) + 2 * (i % 2):max_bank(u) + 2 * (i % 2) + 2, :].rearrange("p a t -> p (a t)")
                if lo:
                    v.tensor_reduce(mx[:, b, n, h, 0:1], s1024[:, 0:lo], AX.X, ALU.max)
                if hi < T:
                    v.tensor_reduce(mx[:, b, n, h, 2:3], s1024[:, hi:T], AX.X, ALU.max)
                o = lo - (t0 - EDGE)
                if i >= 2:
                    dve.wait_ge(sem("mx"), i - 1)
                v.tensor_tensor_reduce(out=junk[:, i % 2, 0:hi - lo], in0=s1024[:, lo:hi],
                                       in1=bias[:, b, n, h, o:o + hi - lo], scale=1.0, scalar=-3.0e38,
                                       op0=ALU.add, op1=ALU.max, accum_out=mx[:, b, n, h, 1:2]).then_inc(sem("mx"), 1)
                if j == STEPS - 1:
                    max_rows(u)

            def max_rows(u):
                c, b = divmod(u, B)
                ns = slice(c * TC, (c + 1) * TC)
                far, m3 = pend[:, b, ns], mx[:, b, ns]
                dve.wait_ge(sem("mx"), 16 * (u + 1))
                if u:
                    dve.wait_ge(sem("pe_rows"), u)
                link(v.tensor_tensor(m3[:, :, :, 0], m3[:, :, :, 0], far[:, :, :, 0], ALU.add))
                link(v.tensor_tensor(m3[:, :, :, 2], m3[:, :, :, 2], far[:, :, :, 1], ALU.add))
                link(v.tensor_reduce(tv[:, 0], m3, AX.X, ALU.max, negate=True))
                link(v.tensor_copy(tv[:, 1], far[:, :, :, 0]))
                link(v.tensor_tensor(tv[:, 2], far[:, :, :, 1], far[:, :, :, 0], ALU.subtract))
                p3 = [tp[:, :, q].rearrange("p a n h -> p a (n h)") for q in range(3)]
                x, r = tv[:].rearrange("p a n h -> p a (n h)"), tr[:].rearrange("p a n h -> p a (n h)")
                link(v.tensor_copy(p3[0], x))
                link(v.tensor_tensor(r, x, p3[0], ALU.subtract))
                link(v.tensor_copy(p3[1], r))
                v.tensor_tensor(p3[2], r, p3[1], ALU.subtract).then_inc(sem("tp"), 1)

            def normalize(u):
                dve.wait_ge(sem("pe_ctx"), u + 1)
                t4 = bank[6].rearrange("p (n h d) -> p n h d", n=TC, h=NH)
                link(v.reciprocal(den[:], t4[:, :, :, HD]))
                for n in range(TC):
                    v.tensor_tensor(ctxn[:, n].rearrange("p (h d) -> p h d", h=NH), t4[:, n, :, 0:HD],
                                    den[:, n].rearrange("p (h o) -> p h o", o=1).to_broadcast([P, NH, HD]),
                                    ALU.mult).then_inc(sem("ctxn"), 1)

            def residual(u):
                c, b = divmod(u, B)
                h = htok[:, (b * NC + c) * TC:(b * NC + c + 1) * TC, :]
                link(v.tensor_tensor(h, h, row("ao_b", TC), ALU.add))
                dve.wait_ge(sem("pe_ao"), u + 1)
                v.tensor_tensor(h, h, bank[6][:, 0:TC * E].rearrange("p (n e) -> p n e", n=TC), ALU.add
                                ).then_inc(sem("htok"), 1)

            def finish(u, k):
                if k == 1:
                    normalize(u)
                elif k == 4:
                    residual(u)

            def norm_step(j, k):
                if k == 0:
                    units = NORMS[j]
                    c, b = divmod(units[0], B)
                    dve.wait_ge(sem("htok"), B + units[-1] + 1)
                    h = htok[:].rearrange("p (b m) e -> p b m e", b=B)[:, b:b + len(units), c * TC:(c + 1) * TC, :]
                    center(B + j, h)
                elif k == 1:
                    scale(B + j, False)

            def route(c, k):
                if k == 1:
                    dve.wait_ge(sem("pe_r"), c + 1)
                    over = rwm[:].rearrange("p (n o) -> p n o", o=1).to_broadcast([P, TC, NE])
                    if c:
                        dve.wait_ge(sem("pe_wT"), c)
                    link(v.tensor_scalar(rwf, bank[4 * c + 2][:, 0:TC * NE], 0.5, None, ALU.mult))
                    link(v.tensor_tensor(rw, rw, row("br", TC), ALU.add))
                    link(v.tensor_reduce(rwm[:], rw, AX.X, ALU.max))
                    v.tensor_tensor(rw, rw, over, ALU.subtract).then_inc(sem("rw_shift"), 1)
                    dve.wait_ge(sem("rw_exp"), c + 1)
                    link(v.tensor_reduce(rwm[:], rw, AX.X, ALU.add))
                    link(v.reciprocal(rwm[:], rwm[:]))
                    link(v.tensor_tensor(rw, rw, over, ALU.mult))
                    link(v.tensor_copy(rw3[:, :, 0, :], rw))
                    link(v.tensor_tensor(rw, rw, rw3[:, :, 0, :], ALU.subtract))
                    link(v.tensor_copy(rw3[:, :, 1, :], rw))
                    v.tensor_tensor(rw3[:, :, 2, :], rw, rw3[:, :, 1, :], ALU.subtract).then_inc(sem("rw"), 1)

            def combine(e):
                u = EXPERT_UNITS[e]
                dve.wait_ge(sem("pe_f3"), NPAIR * (e + 1))
                v.tensor_tensor(fin[:, u * TC:(u + 1) * TC, :], htok[:, u * TC:(u + 1) * TC, :],
                                bank[3][:, 0:TC * E].rearrange("p (n e) -> p n e", n=TC), ALU.add
                                ).then_inc(sem("fin"), 1)

            def mix(g):
                e, p = divmod(g, NPAIR)
                dve.wait_ge(sem("wbc"), NPAIR * (e // B) + p + 1)
                dve.wait_ge(sem("f2"), g + 1)
                if e:
                    dve.wait_ge(sem("pe_f3"), g - NPAIR + 1)
                v.tensor_tensor(f3[p], f2[g % 4], wbc[e // B][p], ALU.mult).then_inc(sem("f3"), 1)

            steps = {"windows": windows, "tail": tail, "setup": setup, "maxima": region_max, "finish": finish,
                     "norm": norm_step, "route": route, "mix": mix, "combine": combine}
            for what, *at in order():
                if what in steps:
                    steps[what](*at)

        @block.tensor
        def _(pe):
            mm = nc.tensor.matmul

            def tr_(out, in_, n=P):
                return nc.tensor.transpose(out, in_, ident[0:n, 0:n])

            pe.wait_ge(sem("ld_ident"), 16)
            pe.wait_ge(sem("xf"), 1)
            tr_(bank[0][:, 0:B * NT], xf[:], B * NT).then_inc(sem("pe_x"), 1)
            pe.wait_ge(sem("ld_band"), 16)
            pe.wait_ge(sem("xcol"), 1)
            for k in range(NW):
                o = bank[1][:, k * B * NT:(k + 1) * B * NT].rearrange("p (b n) -> p b n", b=B)
                mm(o, band[:, 0, k, :], xcol[:, :, 1:NT + 1], start=True, stop=False)
                last = mm(o, band[:, 1, k, :], xcol[:, :, 0:NT], start=False, stop=True)
            last.then_inc(sem("pe_hash"), 1)
            pe.wait_ge(sem("ld_emb"), 32)
            mm(bank[2][0:V, 0:H + E], emb3[:, 0:V], emb3[:, V:V + H + E], start=True, stop=True)
            pe.wait_ge(sem("ld_w"), 16 * 4)
            mm(bank[2][0:E, 256:256 + NR], c64("wpos"), c64("encT"), start=True, stop=True).then_inc(sem("pe_tab"), 1)
            pe.wait_ge(sem("tab"), 19)
            pe.wait_ge(sem("onehot"), 2)

            def windows(b, c):
                i = b * NC + c
                for q in ((0, 1) if i == 0 else (i + 1,) if i + 1 < B * NC else ()):
                    if q >= 2:
                        pe.wait_ge(sem("sc_shift"), q - 1)
                    for n in range(TC):
                        t0 = (q * TC + n) * P
                        last = mm(bank[q % 2 * 2][:, n * E:(n + 1) * E], onehot[0:V, t0:t0 + P], qtab[:], start=True, stop=True)
                    last.then_inc(sem("pe_q"), 1)

            def hidden(b, c):
                i = b * NC + c
                if i:
                    pe.wait_ge(sem("h0"), i)
                mm(bank[3], gtab[:], onehot[:, i * CT:(i + 1) * CT], start=True, stop=False)
                pe.wait_ge(sem("hf"), i + 1)
                for n in range(TC):
                    last = tr_(bank[1][0:E, n * P:(n + 1) * P], hf[:, n, :])
                last.then_inc(sem("pe_hfT"), 1)
                pe.wait_ge(sem("hfT"), 2 * (i + 1))
                for j in range(KC // 2):
                    last = mm(bank[1][0:E, :], cdiag[:, j, :], hfT[:, b, c * CT + 2 * j:c * CT + 2 * j + CT],
                              start=(j == 0), stop=(j == KC // 2 - 1))
                last.then_inc(sem("pe_conv"), 1)
                pe.wait_ge(sem("cf"), i + 1)
                mm(bank[3], c64("winh"), cf[:], start=False, stop=True).then_inc(sem("pe_h0"), 1)

            def tail(b, k):
                if k == 0:
                    pe.wait_ge(sem("h0"), NC * (b + 1))
                    if b:
                        pe.wait_ge(sem("sc_shift"), NC * B)
                    for o, w in ((0, "wg"), (QT, "wi")):
                        for q in range(NQ):
                            last = mm(bank[tower_bank(b)][SS * q:SS * q + SS, o:o + QT], c128(w),
                                      hT[:, b * T + q * QT:b * T + (q + 1) * QT], start=True, stop=True)
                    last.then_inc(sem("pe_gd"), 1)
                    pe.wait_ge(sem("h_bo"), b + 1)
                    for c in range(NC):
                        for n in range(TC):
                            t0 = b * T + c * CT + n * P
                            mm(bank[tower_bank(b) + 1 + 2 * c][:, n * H:(n + 1) * H], hT[:, t0:t0 + P], ident[:],
                               start=(n == 0), stop=False)
                elif k == 1:
                    pe.wait_ge(sem("ends"), b + 1)
                    for q in range(NQ):
                        last = mm(bank[tower_bank(b) + 2][0:SS, q * 2 * QG:(q + 1) * 2 * QG], ident[:, SS * q:SS * q + SS],
                                  ends[:].rearrange("p a g -> p (a g)"), start=True, stop=True)
                    last.then_inc(sem("pe_ends"), 1)
                elif k == 2:
                    pe.wait_ge(sem("carry"), b + 1)
                    for q in range(NQ):
                        last = mm(bank[tower_bank(b) + 2][SS * q:SS * q + SS, 128:128 + QG], ident[0:SS, 0:SS],
                                  carry[:, q * QG:(q + 1) * QG], start=True, stop=True)
                    last.then_inc(sem("pe_carry"), 1)
                elif k == 3:
                    pe.wait_ge(sem("states"), NQ * (b + 1))
                    for c in range(NC):
                        for n in range(TC):
                            t0 = c * CT + n * P
                            last = mm(bank[tower_bank(b) + 1 + 2 * c][:, n * H:(n + 1) * H], states[:, t0:t0 + P],
                                      c128("wo4"), start=False, stop=(n == TC - 1))
                        last.then_inc(sem("pe_y"), 1)
                elif k == 4:
                    for c in range(NC):
                        i = b * NC + c
                        pe.wait_ge(sem("xn"), TC * (i + 1))
                        for n in range(TC):
                            last = tr_(bank[tower_bank(b) + 2 * c][:, n * P:(n + 1) * P], xn[:, c, n, :])
                        last.then_inc(sem("pe_xnT"), 1)
                elif k < 5 + NL:
                    l = k - 5
                    for c in range(NC):
                        i = b * NC + c
                        if l:
                            pe.wait_ge(sem("mlp_add"), (b * NL + l - 1) * NC + c + 1)
                        else:
                            pe.wait_ge(sem("hn"), i + 1)
                        mm(bank[tower_bank(b) + 1 - l % 2 + 2 * c], c128("mlp")[:, l * H:(l + 1) * H], hT[:, i * CT:(i + 1) * CT],
                           start=True, stop=True).then_inc(sem("pe_mlp"), 1)
                else:
                    pe.wait_ge(sem("mlp_add"), NL * NC * (b + 1))
                    for n in range(NT):
                        last = mm(bank[tower_bank(b)][:, n * E:(n + 1) * E], hT[:, b * T + n * P:b * T + (n + 1) * P], c128("wout"),
                                  start=True, stop=True)
                    last.then_inc(sem("pe_out"), 1)

            def ln_transposes(i, first):
                pe.wait_ge(sem("ln"), i + 1)
                for m in range(len(norm_units(i))):
                    for n in range(TC):
                        last = tr_(bank[first + m][0:E, n * P:(n + 1) * P], la[:, m * TC + n, :])
                    last.then_inc(sem("pe_lnT"), 1)

            def setup(b, k):
                if k == 2:
                    ln_transposes(b, tower_bank(b) + 2)
                elif k == 3:
                    pe.wait_ge(sem("lnT_zero"), 1)
                    for c in range(NC):
                        i = b * NC + c
                        pe.wait_ge(sem("lnT"), i + 1)
                        mm(bank[tower_bank(b) + c], c64("aqk", P), lnT[:, i * CT:(i + 1) * CT], start=True, stop=True
                           ).then_inc(sem("pe_qk"), 1)
                elif k == 4:
                    for n in range(NT):
                        last = mm(bank[tower_bank(b) + 2][:, n * E:(n + 1) * E], lnT[:, b * T + n * P:b * T + (n + 1) * P],
                                  c64("av", P), start=True, stop=True)
                    last.then_inc(sem("pe_v"), 1)
                elif k >= 5:
                    c = k - 5
                    if not c:
                        pe.wait_ge(sem("qv"), NC * (b + 1))
                        for n in range(NT):
                            last = mm(bank[tower_bank(b) + 3][:, n * 2 * NH:(n + 1) * 2 * NH], qv[:, n * P:(n + 1) * P],
                                      posb[:, :, 0::NR - 1], start=True, stop=True)
                        last.then_inc(sem("pe_far"), 1)
                    for n in range(c * TC, (c + 1) * TC):
                        if n >= 2:
                            pe.wait_ge(sem("padmid"), b * NT + n - 1)
                        mm(bank[tower_bank(b) + n % 2][:, 0:NH * NR], qv[:, n * P:(n + 1) * P],
                           posb[:].rearrange("e h r -> e (h r)"), start=True, stop=True).then_inc(sem("pe_pos"), 1)

            def max_scores(u, j):
                c, b = divmod(u, B)
                h, n = j % NH, c * TC + j // NH
                i = STEPS * u + j
                if c == 0 and j == 0:
                    pe.wait_ge(sem(f"stacked{b}"), 16 * 12)
                    pe.wait_ge(sem("st_set"), 3)
                if u <= 1 and j == 0:
                    pe.wait_ge(sem("vt"), u + 1)
                    pe.wait_ge(sem("far"), u + 1)
                    pe.wait_ge(sem("padmid"), NT * (u + 1))
                if i >= 2:
                    pe.wait_ge(sem("mx"), i - 1)
                for a_ in range(2):
                    last = mm(bank[max_bank(u) + 2 * (i % 2) + a_], qst[0:NP6, b, h, n * P:(n + 1) * P],
                              kst[0:NP6, b, h, a_ * 512:(a_ + 1) * 512], start=True, stop=True)
                last.then_inc(sem("pe_m"), 1)

            def key_scores(u, i):
                c, b = divmod(u, B)
                k, h = KEYS[c][i // NH], i % NH
                e = u * NT * NH + i
                if i < NH:
                    pe.wait_ge(sem("rows_in"), NH * u + i + 1)
                if i == 0:
                    pe.wait_ge(sem(f"biased{b * NC + c}"), 16 * 2)
                    pe.wait_ge(sem("corners"), 2 * (b * NC + c + 1))
                if e >= 2:
                    pe.wait_ge(sem("exp"), e - 1)
                o = bank[4 + e % 2]
                t0 = c * CT
                left, right = min(max(k * P, t0), t0 + CT), min(max((k + 1) * P, t0), t0 + CT)

                def product(rows_, s0, s1, q0, q1, at, stop):
                    return mm(o[at:at + s1 - s0, q0 - t0:q1 - t0], kst[0:rows_, b, h, s0:s1], qst[0:rows_, b, h, q0:q1],
                              start=True, stop=stop)

                def position(j0, j1, n, at, q0=0, q1=P):
                    return mm(o[at:at + j1 - j0, n * P + q0 - t0:n * P + q1 - t0], bias[:, b, n, h, j0:j1],
                              ident[:, q0:q1], start=False, stop=True)

                if left > t0:
                    last = product(NP6 + 9, k * P, (k + 1) * P, t0, left, 0, True)
                if right < t0 + CT:
                    last = product(NP6 + 6, k * P, (k + 1) * P, right, t0 + CT, 0, True)
                before, after = t0 <= (k - 1) * P < t0 + CT, t0 <= (k + 1) * P < t0 + CT
                if left < right:
                    product(NP6 + 3, k * P, (k + 1) * P, left, right, 0, False)
                    last = position(EDGE, EDGE + P, k, 0)
                if before:
                    product(NP6 + 3, k * P, k * P + EDGE, k * P - EDGE, k * P, 0, False)
                if after:
                    product(NP6 + 3, (k + 1) * P - EDGE, (k + 1) * P, (k + 1) * P, (k + 1) * P + EDGE, P - EDGE, False)
                if before:
                    last = position(EDGE + P, WIN, k - 1, 0, P - EDGE, P)
                if after:
                    last = position(0, EDGE, k + 1, P - EDGE, 0, EDGE)
                last.then_inc(sem("pe_s"), 1)

            def weigh(u, k):
                b = u % B
                pe.wait_ge(sem("exp"), (u * NT + k + 1) * NH)
                if u and k == 0:
                    pe.wait_ge(sem("ctxs"), u)
                for h in range(NH):
                    last = mm(bank[7][32 * h:32 * h + 32, :], vt[:, b, KEYS[u // B][k], h, :], prob[:, ((u * NT + k) * NH + h) % RING, :],
                              start=(k == 0), stop=(k == NT - 1))
                last.then_inc(sem("pe_pv"), 1)

            def exps(u, j):
                key_scores(u, 2 * j)
                key_scores(u, 2 * j + 1)

            def rows(u):
                if u >= 2:
                    pe.wait_ge(sem("htok"), B + u - 1)
                pe.wait_ge(sem("tp"), u + 1)
                for h in range(NH):
                    for n in range(TC):
                        last = mm(bank[6][32 * h:32 * h + 9, n * P:(n + 1) * P],
                                  tp[:, :, :, n, h].rearrange("p a q -> p (a q)"), identb[:], start=True, stop=True)
                last.then_inc(sem("pe_rows"), 1)

            def finish(u, k):
                if k == 0:
                    pe.wait_ge(sem("ctxs"), u + 1)
                    pe.wait_ge(sem("rows_in"), NH * min(u + 2, UNITS))
                    pe.wait_ge(sem("htok"), B + u)
                    if u == UNITS - 1:
                        pe.wait_ge(sem("lnT"), normed(B + 2))
                    for n in range(TC):
                        last = tr_(bank[6][:, n * P:(n + 1) * P], ctxs[:, n * P:(n + 1) * P])
                    last.then_inc(sem("pe_ctx"), 1)
                elif k == 2:
                    pe.wait_ge(sem("ctxn"), TC * (u + 1))
                    for n in range(TC):
                        last = tr_(bank[6][0:E, n * P:(n + 1) * P], ctxn[:, n, :])
                    last.then_inc(sem("pe_ctxnT"), 1)
                elif k == 3:
                    pe.wait_ge(sem("ctxT"), u + 1)
                    for n in range(TC):
                        last = mm(bank[6][:, n * E:(n + 1) * E], ctxT[:, n * P:(n + 1) * P], c64("ao"),
                                  start=True, stop=True)
                    last.then_inc(sem("pe_ao"), 1)

            def norm_step(j, k):
                if k == 2:
                    if j == 0:
                        pe.wait_ge(sem("mx"), UNITS * STEPS)
                    ln_transposes(B + j, 6 if j else 0)

            def route(c, k):
                if k == 1:
                    pe.wait_ge(sem("lnT"), normed(B + 1 + 2 * c))
                    if c:
                        pe.wait_ge(sem("exp"), UNITS * NT * NH)
                    for n in range(TC):
                        o, t0 = bank[4 * c + 2][:, n * NE:(n + 1) * NE], c * CT + n * P
                        mm(o, lnT[:, t0:t0 + P], c64("wr", P), start=True, stop=False)
                        last = mm(o, lnT[:, T + t0:T + t0 + P], c64("wr", P), start=False, stop=True)
                    last.then_inc(sem("pe_r"), 1)
                elif k == 2:
                    pe.wait_ge(sem("rw"), c + 1)
                    for n in range(TC):
                        last = mm(bank[4 * c + 3][0:3 * NE, n * P:(n + 1) * P], rw3[:, n].rearrange("p q e -> p (q e)"),
                                  identb[:], start=True, stop=True)
                    last.then_inc(sem("pe_wT"), 1)
                elif k == 3:
                    pe.wait_ge(sem("wTb"), c + 1)
                    pe.wait_ge(sem("ld_f"), 16 * 3)
                    for p in range(NPAIR):
                        if p >= 2:
                            pe.wait_ge(sem("wbc"), NPAIR * c + p - 1)
                        mm(bank[4 * c + p % 2], pairb[:, p * P:(p + 1) * P], wTb[:], start=True, stop=True
                           ).then_inc(sem("pe_wbc"), 1)

            def first_layer(g):
                u, p = EXPERT_UNITS[g // NPAIR], g % NPAIR
                if g >= B * NPAIR and not p:
                    pe.wait_ge(sem("lnT"), normed(B + g // NPAIR))
                if g == 0:
                    pe.wait_ge(sem("wbc"), NPAIR)
                if g >= 2:
                    pe.wait_ge(sem("f1"), g - 1)
                mm(bank[g % 2], c64("w1", P)[:, p * P:(p + 1) * P], lnT[:, u * CT:(u + 1) * CT],
                   start=True, stop=True).then_inc(sem("pe_f1"), 1)

            def third_layer(g):
                e, p = divmod(g, NPAIR)
                t0 = EXPERT_UNITS[e] % NC * CT
                pe.wait_ge(sem("f3"), g + 1)
                if e and not p:
                    pe.wait_ge(sem("fin"), e)
                for n in range(TC):
                    o = bank[3][:, n * E:(n + 1) * E]
                    if not p:
                        pe.wait_ge(sem("wT"), e // B + 1)
                    if not p:
                        mm(o, wT[:, t0 + n * P:t0 + (n + 1) * P], bo8[:], start=(n == 0), stop=False)
                    last = mm(o, f3[p][:, n * P:(n + 1) * P], c128("fwo")[:, p * E:(p + 1) * E],
                              start=False, stop=(p == NPAIR - 1 and n == TC - 1))
                last.then_inc(sem("pe_f3"), 1)

            def second_layer(g):
                e, p = divmod(g, NPAIR)
                pe.wait_ge(sem("f1"), g + 1)
                if g:
                    pe.wait_ge(sem("f2"), g)
                mm(bank[f2_bank(g)], w2bd[:, p, :], f1[g % 2], start=True, stop=True).then_inc(sem("pe_f2"), 1)

            steps = {"windows": windows, "hidden": hidden, "tail": tail, "setup": setup, "maxima": max_scores,
                     "exps": exps, "rows": rows, "weigh": weigh, "finish": finish, "norm": norm_step, "route": route,
                     "first": first_layer, "second": second_layer, "third": third_layer}
            for what, *at in order():
                if what in steps:
                    steps[what](*at)


def skewed(skew, b, ns, g):
    flat = skew[b, ns].rearrange("n h p c -> (n h) (p c)")
    at = HALF * g * PW + LPAD - 2
    return flat[:, at:at + HALF * (PW - 1)].rearrange("m (i c) -> i m c", c=PW - 1)[:, :, 0:2 * HALF]


def layout(inputs):
    w = {k: np.asarray(v) for k, v in inputs.items()}
    t = lambda n: w["L0_tok_" + n]
    a = lambda n: w["L0_attn_" + n]
    f = lambda n: w["L0_ffn_" + n]
    k = constants()
    tall = lambda x, n=P: np.concatenate([x, np.zeros((n - x.shape[0], x.shape[1]), np.float32)])
    pairs = lambda x: x.reshape(NPAIR, 2 * E).T
    v1 = lambda x: x.reshape(-1, 1)
    w128 = {
        "mlp": t("mlp_w").transpose(1, 0, 2).reshape(H, NL * H), "wg": t("Wg"), "wi": t("Wi"), "wout": t("Wout"),
        "wo4": np.tile(t("Wo"), (NQ, 1)),
        "fwo": f("Wo").reshape(NPAIR, 2 * E, E).transpose(1, 0, 2).reshape(P, NPAIR * E), "start": k["start"],
    }
    w64 = {
        "winh": t("Win")[E:2 * E], "aqk": np.concatenate([a("Wq").T, a("Wk").T], 1), "av": a("Wv").T,
        "wpos": a("Wpos").T, "encT": k["encT"], "ao": a("Wo").T, "wr": f("Wr"),
        "w1": f("W1").transpose(1, 0, 2).reshape(E, NE * E), "heads": k["heads"],
    }
    cols = {
        "b_in": v1(t("b_in")), "ln_g": v1(t("ln_g")), "ln_b": v1(t("ln_b")), "mlp_b": t("mlp_b").T,
        "bg": np.tile(v1(t("bg")), (NQ, 1)), "bi": np.tile(v1(t("bi")), (NQ, 1)), "conv_b": tall(v1(t("conv_b"))),
        "gamma": tall(v1(a("ln_gamma"))), "beta": tall(v1(a("ln_beta"))),
        "bqk": np.concatenate([v1(a("bq")), v1(a("bk"))]), "u": tall(v1(a("u_bias"))), "v": tall(v1(a("v_bias"))),
        "bpos": tall(v1(a("bpos"))), "bo": v1(t("bo")),
        "convw": t("conv_w")[:, 0, :].reshape(E, KC // 2, 2).transpose(2, 0, 1).reshape(P, KC // 2),
        "f1": np.concatenate([pairs(f(n)) for n in ("b1", "g1", "be1", "m1", "v1")], 1),
        "f2": np.concatenate([pairs(f(n)) for n in ("b2", "g2", "be2", "m2", "v2")], 1),
    }
    rows = {"bq": t("bq"), "bout": t("bout"), "bv": a("bv"), "ao_b": a("bo"), "br": f("br")}
    side = lambda pack, d: np.concatenate([d[n] for n, _ in pack], 1)
    return {
        "x": w["x"], "ident": k["ident"], "band": k["band"], "iota": k["iota"], "pair": np.tile(k["pair"], (3, 1)),
        "emb3": np.concatenate([t("emb_byte").T, t("Win")[0:E], t("Wq")], 1), "winm": t("Win")[2 * E:],
        "w128": side(PACK128, w128), "w64": tall(side(PACK64, w64)), "cols": side(COLS, cols),
        "rows": np.concatenate([rows[n] for n, _ in ROWS])[None, :], "bo8": np.tile(f("bo"), (3, 1)),
        "w2": f("W2").reshape(NPAIR, 2, E, E).transpose(1, 2, 0, 3), "table": t("hash_tables").reshape(NW * MOD, E),
    }


def kernel(**inputs):
    import concourse.bacc as bacc
    from concourse.bass_utils import run_bass_kernel_spmd

    nc = bacc.Bacc("TRN2", target_bir_lowering=False, num_devices=1)
    arrays = {k: np.ascontiguousarray(v) for k, v in layout(inputs).items()}
    tensors = {k: nc.dram_tensor("in_" + k, v.shape, mybir.dt.from_np(v.dtype), kind="ExternalInput").ap()
               for k, v in arrays.items()}
    tensors["out"] = nc.dram_tensor("result", (B, T, E), F32, kind="ExternalOutput").ap()
    tensors["skew"] = nc.dram_tensor("skewed", (B, NT, NH, P, PW), F32).ap()
    tensors["parts"] = nc.dram_tensor("query_key_parts", (B, 3, 2, NH, HD, T), BF16).ap()
    tower(nc, tensors)
    return run_bass_kernel_spmd(nc, [{"in_" + k: v for k, v in arrays.items()}], core_ids=[0]).results[0]["result"]
```
